# Optimizing a Trainium2 kernel written in Bass

```python
import numpy as np
import jax
import jax.numpy as jnp

def _softmax(x, axis=-1):
    return jax.nn.softmax(x, axis=axis)

def _gelu(x):
    return jax.nn.gelu(x, approximate=True)

def _silu(x):
    return jax.nn.silu(x)

def _sigmoid(x):
    return jax.nn.sigmoid(x)

def _layernorm(x, axis=-1, eps=1e-05):
    m = jnp.mean(x, axis=axis, keepdims=True)
    v = jnp.var(x, axis=axis, keepdims=True)
    return (x - m) / jnp.sqrt(v + eps)

def _scatter_add(tgt, idx, src, axis=0):
    return tgt.at[idx].add(src)

def _segment_sum(src, seg, n):
    return jax.ops.segment_sum(src, seg, n)
kernel_name = 'mk_flamingo_gated_d2_seqx_r4_598e35'

def setup_inputs(seed: int=0):
    np.random.seed(seed)
    _w = jnp.asarray

    def _rec_inputs():
        import jax
        import jax.numpy as jnp
        _rk = jax.random.key(seed)
        x = 6.313e-05 + 0.9998 * jax.random.normal(jax.random.fold_in(_rk, 1), (8, 112, 256), jnp.float32)
        _lenS = 112 - jax.random.randint(jax.random.fold_in(_rk, 7), (8,), 0, max(1, 112 // 4) + 1, jnp.int32)
        _lenS2 = 375 - jax.random.randint(jax.random.fold_in(_rk, 8), (8,), 0, max(1, 375 // 4) + 1, jnp.int32)
        _ctx_1024P = jax.random.normal(jax.random.fold_in(_rk, 11), (8, 16, 256), jnp.float32)
        _ctx_1024c = jax.random.dirichlet(jax.random.fold_in(_rk, 511), 0.3 * jnp.ones((16,), jnp.float32), (8, 375))
        _ctx_1024t = jnp.einsum('bsk,bkd->bsd', _ctx_1024c, _ctx_1024P)
        _ctx_1024t = _ctx_1024t * jax.lax.rsqrt(jnp.mean(jnp.square(_ctx_1024t)) + 1e-12) * 0.953939
        ctx_1024 = -0.000214406 + 1.00034 * (_ctx_1024t + 0.3 * jax.random.normal(jax.random.fold_in(_rk, 611), (8, 375, 256), jnp.float32))
        _g = jax.random.normal(jax.random.fold_in(_rk, 9001), (2, 2), jnp.float32)
        _g = jnp.sign(_g) * jnp.maximum(jnp.abs(_g), 1.0) + (_g == 0) * 1.0
        g_xattn = _g[0]
        g_ffn = _g[1]
        return (x, ctx_1024, g_xattn, g_ffn)
    x, ctx_1024, g_xattn, g_ffn = _rec_inputs()

    def _L0_xattn_setup():
        import jax, jax.numpy as jnp
        import numpy as np
        from jax import lax
        BIG = jnp.float32(1e+30)

        def _pairwise_euclidean(a, b):
            aa = jnp.sum(a * a, axis=-1)[:, None]
            bb = jnp.sum(b * b, axis=-1)[None, :]
            ab = a @ b.T
            return jnp.sqrt(jnp.maximum(aa + bb - 2.0 * ab, 0.0))

        def _dtw_cost(D):
            row0 = jnp.cumsum(D[0])

            def row_step(prev_row, d_row):
                first = d_row[0] + prev_row[0]

                def col_step(left, inp):
                    d_ij, up, diag = inp
                    r = d_ij + jnp.minimum(jnp.minimum(up, left), diag)
                    return (r, r)
                _, rest = lax.scan(col_step, first, (d_row[1:], prev_row[1:], prev_row[:-1]))
                row = jnp.concatenate([first[None], rest])
                return (row, row)
            _, rows = lax.scan(row_step, row0, D[1:])
            return jnp.concatenate([row0[None], rows], axis=0)

        def _backtrack(R, T1, T2):
            L = T1 + T2 - 1

            def step(carry, _):
                i, j, done = carry
                valid = jnp.logical_not(done)
                cd = jnp.where((i > 0) & (j > 0), R[jnp.maximum(i - 1, 0), jnp.maximum(j - 1, 0)], BIG)
                cu = jnp.where(i > 0, R[jnp.maximum(i - 1, 0), j], BIG)
                cl = jnp.where(j > 0, R[i, jnp.maximum(j - 1, 0)], BIG)
                choice = jnp.argmin(jnp.stack([cd, cu, cl]))
                ni = jnp.where(choice <= 1, i - 1, i)
                nj = jnp.where((choice == 0) | (choice == 2), j - 1, j)
                at_origin = (i == 0) & (j == 0)
                ni = jnp.where(at_origin, 0, ni)
                nj = jnp.where(at_origin, 0, nj)
                return ((ni, nj, done | at_origin), (i, j, valid))
            init = (jnp.int32(T1 - 1), jnp.int32(T2 - 1), jnp.bool_(False))
            _, (i_idx, j_idx, valid) = lax.scan(step, init, None, length=L)
            return (i_idx, j_idx, valid)

        def _align_one(small, large):
            T_small, d = small.shape
            T_large = large.shape[0]
            D = _pairwise_euclidean(small, large)
            R = _dtw_cost(D)
            i_idx, j_idx, valid = _backtrack(R, T_small, T_large)
            contrib = small[i_idx] * valid[:, None].astype(small.dtype)
            expanded = jnp.zeros((T_large, d), dtype=small.dtype).at[j_idx].add(contrib)
            return expanded
        key = jax.random.key(seed)
        k1, k2 = jax.random.split(key)
        teacher = jax.random.normal(k1, (16, 100, 256), dtype=jnp.float32)
        student = jax.random.normal(k2, (16, 150, 256), dtype=jnp.float32)
        return {'teacher_features': teacher, 'student_features': student}
    _L0_xattn_all = _L0_xattn_setup()
    _L0_xattn_in = {k: v for k, v in _L0_xattn_all.items() if k in ()}
    del _L0_xattn_all

    def _L0_ffn_setup():
        import jax, jax.numpy as jnp
        import numpy as np
        B, S, D_MODEL, D_HIDDEN = (4, 512, 256, 1024)

        def act_quant(x):
            scale = 127.0 / jnp.clip(jnp.max(jnp.abs(x), axis=-1, keepdims=True), 1e-05)
            return jnp.clip(jnp.round(x * scale), -128, 127) / scale

        def weight_quant(w):
            scale = 1.0 / jnp.clip(jnp.mean(jnp.abs(w)), 1e-05)
            return jnp.clip(jnp.round(w * scale), -1, 1) / scale

        def bit_linear(x, w):
            xq = x + jax.lax.stop_gradient(act_quant(x) - x)
            wq = w + jax.lax.stop_gradient(weight_quant(w) - w)
            return jnp.einsum('bsd,hd->bsh', xq, wq)

        def depthwise_conv1d(x_bcl, w, b):
            y = jax.lax.conv_general_dilated(x_bcl, w, window_strides=(1,), padding=[(1, 1)], dimension_numbers=('NCH', 'OIH', 'NCH'), feature_group_count=x_bcl.shape[1])
            return y + b[None, :, None]
        key = jax.random.key(seed)
        ks = jax.random.split(key, 5)
        lim1 = 1.0 / np.sqrt(D_MODEL)
        lim2 = 1.0 / np.sqrt(D_HIDDEN)
        limc = 1.0 / np.sqrt(3.0)
        return {'x': jax.random.normal(ks[0], (B, S, D_MODEL), dtype=jnp.float32), 'w1': jax.random.uniform(ks[1], (D_HIDDEN, D_MODEL), jnp.float32, -lim1, lim1), 'conv_w': jax.random.uniform(ks[2], (D_HIDDEN, 1, 3), jnp.float32, -limc, limc), 'conv_b': jax.random.uniform(ks[3], (D_HIDDEN,), jnp.float32, -limc, limc), 'w2': jax.random.uniform(ks[4], (D_MODEL, D_HIDDEN), jnp.float32, -lim2, lim2)}
    _L0_ffn_all = _L0_ffn_setup()
    _L0_ffn_in = {k: v for k, v in _L0_ffn_all.items() if k in ('w1', 'conv_w', 'conv_b', 'w2')}
    del _L0_ffn_all

    def _L1_xattn_setup():
        import jax, jax.numpy as jnp
        import numpy as np
        EMBED_DIM = 256
        NUM_HEADS = 16
        HEAD_DIM = EMBED_DIM // NUM_HEADS
        SCALE = HEAD_DIM ** (-0.5)
        key = jax.random.key(seed)
        ks = jax.random.split(key, 12)
        B, S, D = (1, 1024, EMBED_DIM)
        w_std = D ** (-0.5)
        return {'query': jax.random.normal(ks[0], (B, S, D), dtype=jnp.float32), 'key': jax.random.normal(ks[1], (B, S, D), dtype=jnp.float32), 'value': jax.random.normal(ks[2], (B, S, D), dtype=jnp.float32), 'Wq': jax.random.normal(ks[3], (D, D), dtype=jnp.float32) * w_std, 'bq': jax.random.normal(ks[4], (D,), dtype=jnp.float32) * 0.01, 'Wk': jax.random.normal(ks[5], (D, D), dtype=jnp.float32) * w_std, 'bk': jax.random.normal(ks[6], (D,), dtype=jnp.float32) * 0.01, 'Wv': jax.random.normal(ks[7], (D, D), dtype=jnp.float32) * w_std, 'bv': jax.random.normal(ks[8], (D,), dtype=jnp.float32) * 0.01, 'Wo': jax.random.normal(ks[9], (D, D), dtype=jnp.float32) * w_std, 'bo': jax.random.normal(ks[10], (D,), dtype=jnp.float32) * 0.01}
    _L1_xattn_all = _L1_xattn_setup()
    _L1_xattn_in = {k: v for k, v in _L1_xattn_all.items() if k in ('Wq', 'bq', 'Wk', 'bk', 'Wv', 'bv', 'Wo', 'bo')}
    del _L1_xattn_all

    def _L1_ffn_setup():
        import jax, jax.numpy as jnp
        import numpy as np

        def gelu(x):
            return jax.nn.gelu(x, approximate=False)
        key = jax.random.key(seed)
        ks = jax.random.split(key, 6)
        B, S, d_model = (4, 512, 256)
        n_input, n_process, n_output, d_pv = (2048, 1024, 2048, 128)
        s = 0.02
        return {'x': jax.random.normal(ks[0], (B, S, d_model), jnp.float32), 'input_patterns': jax.random.normal(ks[1], (n_input, d_model), jnp.float32) * s, 'process_input_weights': jax.random.normal(ks[2], (n_process, n_input), jnp.float32) * s, 'process_values': jax.random.normal(ks[3], (n_process, d_pv), jnp.float32) * s, 'output_input_weights': jax.random.normal(ks[4], (n_output, d_pv), jnp.float32) * s, 'output_patterns': jax.random.normal(ks[5], (n_output, d_model), jnp.float32) * s}
    _L1_ffn_all = _L1_ffn_setup()
    _L1_ffn_in = {k: v for k, v in _L1_ffn_all.items() if k in ('input_patterns', 'process_input_weights', 'process_values', 'output_input_weights', 'output_patterns')}
    del _L1_ffn_all
    return {'x': x, 'ctx_1024': ctx_1024, 'g_xattn': g_xattn, 'g_ffn': g_ffn, 'L0_ffn_w1': _L0_ffn_in['w1'], 'L0_ffn_conv_w': _L0_ffn_in['conv_w'], 'L0_ffn_conv_b': _L0_ffn_in['conv_b'], 'L0_ffn_w2': _L0_ffn_in['w2'], 'L1_xattn_Wq': _L1_xattn_in['Wq'], 'L1_xattn_bq': _L1_xattn_in['bq'], 'L1_xattn_Wk': _L1_xattn_in['Wk'], 'L1_xattn_bk': _L1_xattn_in['bk'], 'L1_xattn_Wv': _L1_xattn_in['Wv'], 'L1_xattn_bv': _L1_xattn_in['bv'], 'L1_xattn_Wo': _L1_xattn_in['Wo'], 'L1_xattn_bo': _L1_xattn_in['bo'], 'L1_ffn_input_patterns': _L1_ffn_in['input_patterns'], 'L1_ffn_process_input_weights': _L1_ffn_in['process_input_weights'], 'L1_ffn_process_values': _L1_ffn_in['process_values'], 'L1_ffn_output_input_weights': _L1_ffn_in['output_input_weights'], 'L1_ffn_output_patterns': _L1_ffn_in['output_patterns']}

def reference(x, ctx_1024, g_xattn, g_ffn, L0_ffn_w1, L0_ffn_conv_w, L0_ffn_conv_b, L0_ffn_w2, L1_xattn_Wq, L1_xattn_bq, L1_xattn_Wk, L1_xattn_bk, L1_xattn_Wv, L1_xattn_bv, L1_xattn_Wo, L1_xattn_bo, L1_ffn_input_patterns, L1_ffn_process_input_weights, L1_ffn_process_values, L1_ffn_output_input_weights, L1_ffn_output_patterns):
    import jax
    import jax.numpy as jnp

    def _L0_xattn_ref(teacher_features, student_features):
        import jax, jax.numpy as jnp
        import numpy as np
        from jax import lax
        BIG = jnp.float32(1e+30)

        def _pairwise_euclidean(a, b):
            aa = jnp.sum(a * a, axis=-1)[:, None]
            bb = jnp.sum(b * b, axis=-1)[None, :]
            ab = a @ b.T
            return jnp.sqrt(jnp.maximum(aa + bb - 2.0 * ab, 0.0))

        def _dtw_cost(D):
            row0 = jnp.cumsum(D[0])

            def row_step(prev_row, d_row):
                first = d_row[0] + prev_row[0]

                def col_step(left, inp):
                    d_ij, up, diag = inp
                    r = d_ij + jnp.minimum(jnp.minimum(up, left), diag)
                    return (r, r)
                _, rest = lax.scan(col_step, first, (d_row[1:], prev_row[1:], prev_row[:-1]))
                row = jnp.concatenate([first[None], rest])
                return (row, row)
            _, rows = lax.scan(row_step, row0, D[1:])
            return jnp.concatenate([row0[None], rows], axis=0)

        def _backtrack(R, T1, T2):
            L = T1 + T2 - 1

            def step(carry, _):
                i, j, done = carry
                valid = jnp.logical_not(done)
                cd = jnp.where((i > 0) & (j > 0), R[jnp.maximum(i - 1, 0), jnp.maximum(j - 1, 0)], BIG)
                cu = jnp.where(i > 0, R[jnp.maximum(i - 1, 0), j], BIG)
                cl = jnp.where(j > 0, R[i, jnp.maximum(j - 1, 0)], BIG)
                choice = jnp.argmin(jnp.stack([cd, cu, cl]))
                ni = jnp.where(choice <= 1, i - 1, i)
                nj = jnp.where((choice == 0) | (choice == 2), j - 1, j)
                at_origin = (i == 0) & (j == 0)
                ni = jnp.where(at_origin, 0, ni)
                nj = jnp.where(at_origin, 0, nj)
                return ((ni, nj, done | at_origin), (i, j, valid))
            init = (jnp.int32(T1 - 1), jnp.int32(T2 - 1), jnp.bool_(False))
            _, (i_idx, j_idx, valid) = lax.scan(step, init, None, length=L)
            return (i_idx, j_idx, valid)

        def _align_one(small, large):
            T_small, d = small.shape
            T_large = large.shape[0]
            D = _pairwise_euclidean(small, large)
            R = _dtw_cost(D)
            i_idx, j_idx, valid = _backtrack(R, T_small, T_large)
            contrib = small[i_idx] * valid[:, None].astype(small.dtype)
            expanded = jnp.zeros((T_large, d), dtype=small.dtype).at[j_idx].add(contrib)
            return expanded
        return jax.vmap(_align_one)(teacher_features, student_features)

    def _L0_ffn_ref(x, w1, conv_w, conv_b, w2):
        import jax, jax.numpy as jnp
        import numpy as np
        B, S, D_MODEL, D_HIDDEN = (4, 512, 256, 1024)

        def act_quant(x):
            scale = 127.0 / jnp.clip(jnp.max(jnp.abs(x), axis=-1, keepdims=True), 1e-05)
            return jnp.clip(jnp.round(x * scale), -128, 127) / scale

        def weight_quant(w):
            scale = 1.0 / jnp.clip(jnp.mean(jnp.abs(w)), 1e-05)
            return jnp.clip(jnp.round(w * scale), -1, 1) / scale

        def bit_linear(x, w):
            xq = x + jax.lax.stop_gradient(act_quant(x) - x)
            wq = w + jax.lax.stop_gradient(weight_quant(w) - w)
            return jnp.einsum('bsd,hd->bsh', xq, wq)

        def depthwise_conv1d(x_bcl, w, b):
            y = jax.lax.conv_general_dilated(x_bcl, w, window_strides=(1,), padding=[(1, 1)], dimension_numbers=('NCH', 'OIH', 'NCH'), feature_group_count=x_bcl.shape[1])
            return y + b[None, :, None]
        h = bit_linear(x, w1)
        h = depthwise_conv1d(h.transpose(0, 2, 1), conv_w, conv_b)
        h = h.transpose(0, 2, 1)
        h = jax.nn.silu(h)
        return bit_linear(h, w2)

    def _L1_xattn_ref(query, key, value, Wq, bq, Wk, bk, Wv, bv, Wo, bo):
        import jax, jax.numpy as jnp
        import numpy as np
        EMBED_DIM = 256
        NUM_HEADS = 16
        HEAD_DIM = EMBED_DIM // NUM_HEADS
        SCALE = HEAD_DIM ** (-0.5)
        B, Sq, D = query.shape
        Skv = key.shape[1]
        H, Hd = (NUM_HEADS, HEAD_DIM)
        q = (query @ Wq.T + bq).reshape(B, Sq, H, Hd).transpose(0, 2, 1, 3)
        k = (key @ Wk.T + bk).reshape(B, Skv, H, Hd).transpose(0, 2, 1, 3)
        v = (value @ Wv.T + bv).reshape(B, Skv, H, Hd).transpose(0, 2, 1, 3)
        q = q * SCALE
        scores = jnp.einsum('bhqd,bhkd->bhqk', q, k)
        attn = jax.nn.softmax(scores, axis=-1)
        out = jnp.einsum('bhqk,bhkd->bhqd', attn, v)
        out = out.transpose(0, 2, 1, 3).reshape(B, Sq, D)
        return out @ Wo.T + bo

    def _L1_ffn_ref(x, input_patterns, process_input_weights, process_values, output_input_weights, output_patterns):
        import jax, jax.numpy as jnp
        import numpy as np

        def gelu(x):
            return jax.nn.gelu(x, approximate=False)
        B, S, d_model = x.shape
        n_input = input_patterns.shape[0]
        n_process = process_input_weights.shape[0]
        n_output = output_input_weights.shape[0]
        k_input = max(n_input // 8, 64)
        k_process = max(n_process // 8, 32)
        k_output = max(n_output // 8, 64)
        input_acts = gelu(jnp.einsum('bsd,nd->bsn', x, input_patterns))
        input_acts_seq = input_acts.mean(axis=1)
        top_input_acts, top_input_idx = jax.lax.top_k(input_acts_seq, k_input)
        brow = jnp.arange(B)[:, None]
        input_repr = jnp.zeros((B, n_input), x.dtype).at[brow, top_input_idx].set(top_input_acts)
        process_acts = gelu(jnp.einsum('bn,pn->bp', input_repr, process_input_weights))
        top_process_acts, top_process_idx = jax.lax.top_k(process_acts, k_process)
        selected_process_values = process_values[top_process_idx]
        process_weights = jax.nn.softmax(top_process_acts, axis=-1)
        aggregated_value = jnp.einsum('bk,bkd->bd', process_weights, selected_process_values)
        output_acts_seq = gelu(jnp.einsum('bd,od->bo', aggregated_value, output_input_weights))
        top_output_acts, top_output_idx = jax.lax.top_k(output_acts_seq, k_output)
        selected_output_patterns = output_patterns[top_output_idx]
        out_per_seq = jnp.einsum('bk,bkm->bm', top_output_acts, selected_output_patterns)
        output = jnp.broadcast_to(out_per_seq[:, None, :], (B, S, d_model))
        return output
    x = x + jnp.tanh(g_xattn[0]) * _L0_xattn_ref(ctx_1024, _layernorm(x, axis=-1))
    x = x + jnp.tanh(g_ffn[0]) * _L0_ffn_ref(_layernorm(x, axis=-1), L0_ffn_w1, L0_ffn_conv_w, L0_ffn_conv_b, L0_ffn_w2)
    x = x + jnp.tanh(g_xattn[1]) * _L1_xattn_ref(_layernorm(x, axis=-1), ctx_1024, ctx_1024, L1_xattn_Wq, L1_xattn_bq, L1_xattn_Wk, L1_xattn_bk, L1_xattn_Wv, L1_xattn_bv, L1_xattn_Wo, L1_xattn_bo)
    x = x + jnp.tanh(g_ffn[1]) * _L1_ffn_ref(_layernorm(x, axis=-1), L1_ffn_input_patterns, L1_ffn_process_input_weights, L1_ffn_process_values, L1_ffn_output_input_weights, L1_ffn_output_patterns)
    return x

_drawn_inputs = setup_inputs


def setup_inputs(seed=0):
    import zlib

    import numpy as np

    out = dict(_drawn_inputs(seed))
    spreads = {'g_ffn': (-1.0, 0.6)}
    factors = {'L0_ffn_w1': 6.984,
     'L0_ffn_conv_w': 6.831,
     'L0_ffn_conv_b': 6.119,
     'L0_ffn_w2': 4.584,
     'L1_xattn_bq': 64.0,
     'L1_xattn_bk': 64.0,
     'L1_xattn_bv': 49.069,
     'L1_xattn_bo': 38.129,
     'L1_ffn_input_patterns': 8.0,
     'L1_ffn_process_input_weights': 8.0,
     'L1_ffn_process_values': 8.0,
     'L1_ffn_output_input_weights': 8.0,
     'L1_ffn_output_patterns': 8.0,
     'L1_xattn_Wq': 2.793,
     'L1_xattn_Wk': 2.693}
    for name, (base, spread) in spreads.items():
        noise = np.random.default_rng([zlib.crc32(name.encode()), seed]).standard_normal(out[name].shape)
        drawn = base * np.exp(spread * noise) if base else spread * noise
        out[name] = jnp.asarray(drawn.astype(out[name].dtype))
    for name, factor in factors.items():
        out[name] = (out[name] * factor).astype(out[name].dtype)
    return out
```

```python
import numpy as np
import concourse.bass as bass
from concourse import mybir
from contextlib import ExitStack

F32, BF16, I32 = mybir.dt.float32, mybir.dt.bfloat16, mybir.dt.int32
ALU = mybir.AluOpType
ACT = mybir.ActivationFunctionType
AX = mybir.AxisListType

B, S, D, SC = 8, 112, 256, 375
DH = D // 128
KB, RB = 16, 24
CT = 4
T = S + KB - 1
HID, HT = 1024, 8
NH, HD = 16, 16
KC, KCH = 125, 3
VW = NH * (HD + 1) + 15
NI, NP, NO, DPV = 2048, 1024, 2048, 128
NIT, NPT, NOT = NI // 128, NP // 128, NO // 128
BIG = 1.0e30
MAGIC = 12582912.0
TOK = B * S


SIGNALLED_BY_RESULT = ("expand", "ffn_down", "pattern", "process", "output", "spread")


class Group:

    def __init__(self, name, banks, nth, nth_drain, before):
        self.name, self.banks, self.nth, self.nth_drain, self.before = name, banks, nth, nth_drain, before


class PsumPlan:

    def __init__(self, nbanks):
        self.uses = [0] * nbanks
        self.drains = [0] * nbanks
        self.last = [None] * nbanks
        self.groups = {}

    def add(self, name, *banks):
        before = []
        for b in banks:
            if self.last[b] is not None and self.last[b] not in before:
                before.append(self.last[b])
        self.uses[banks[0]] += 1
        if (name if isinstance(name, str) else name[0]) not in SIGNALLED_BY_RESULT:
            self.drains[banks[0]] += 1
        g = Group(name, banks, self.uses[banks[0]], self.drains[banks[0]], before)
        for b in banks:
            self.last[b] = g
        self.groups[name] = g

    def __getitem__(self, name):
        return self.groups[name]


def plan_psum():
    p = PsumPlan(8)
    n = [0]

    def ring(name, banks=tuple(range(8))):
        p.add(name, banks[n[0] % len(banks)])
        n[0] += 1

    for h in range(DH):
        for half in range(2):
            ring(("lnT0", h, half))
    for b in range(B):
        for h in range(DH):
            ring(("ctxT", b, h))
    ring("aaT")
    for b in range(B):
        ring(("dist", b))
    for m in range(KB // 2):
        ring(("skew", m))
    for m in range(RB // 4):
        ring(("dwave", m))
    for w in range(4):
        ring(("attnWT", w))
    ring("wsum")
    for b in range(B):
        for c in range(KCH):
            ring(("V", b, c))
    for w in range(2):
        for h in range(2):
            ring(("ternT", w, h))
    for t in range(4):
        for b in range(B):
            ring(("kT", t, b))
    for m in range(3):
        ring(("pathT", m))
    for b in range(B):
        ring(("path", b))
    for b in range(B):
        ring(("expand", b))
    for h in range(DH):
        ring(("qxT", h))
    for half in range(2):
        ring(("sxbc", half))
    for c in range(HT):
        for half in range(2):
            ring(("ffn_up", c, half))
    for half in range(2):
        ring(("hmaxT", half))
    for half in range(2):
        ring(("s2bc", half))
    for b in range(B):
        ring(("ffn_down", b))
    for h in range(DH):
        for half in range(2):
            ring(("lnT2", h, half))
    for t in range(4):
        for half in range(2):
            ring(("qT", t, half))
    for b in range(-1, B + 1):
        for t in range(4):
            if b + 1 < B:
                for u in range(2):
                    p.add(("smax", b + 1, t, u), 2 * u, 2 * u + 1)
            if 0 <= b < B:
                for g in range(4):
                    p.add(("scoreT", b, t, g), 4 + g % 2)
                    if t == 0 and g == 0:
                        p.add(("pv", b), 6)
            if b >= 1 and t == 0:
                p.add(("pvT", b - 1), 7)
            if b >= 1 and t == 1:
                p.add(("oT", b - 1), 7)
            if b >= 1 and t == 2:
                p.add(("wo", b - 1), 7)
        if b + 1 < B:
            p.add(("negmT", b + 1), 7)
    n[0] = 0
    for h in range(DH):
        for half in range(2):
            ring(("lnT3", h, half))
    for m in range(NIT // 2):
        ring(("patT", m))
    for i in range(NIT):
        for half in range(2):
            ring(("pattern", i, half))
    for m in range(NOT // 4):
        ring(("oiwT", m))
    n[0] = 0
    for p_ in range(NPT):
        for m in range(NIT // 4):
            ring(("piwT", p_, m), (0, 1, 2, 3))
    for k in range(3):
        for r in range(16):
            p.add(("count", k, r), 4 + r % 2)
        p.add(("ties", k), 6)
        if k == 0:
            p.add("process", 7)
        if k == 1:
            p.add("pmaxT", 7)
            p.add("pmaxb", 6)
            p.add("aggr", 7)
            p.add("output", 6)
    p.add("final", 7)
    for b in range(B):
        p.add(("spread", b), b % 4)
    return p



def build_program(nc, x_in, ctx_in, g_xattn, g_ffn, w1_in, conv_w, conv_b, w2_in,
                  wq_in, bq_in, wk_in, bk_in, wv_in, bv_in, wo_in, bo_in,
                  pat_in, piw_in, pval_in, oiw_in, opat_in, out):
    plan = plan_psum()
    ctx = ExitStack()
    with ctx:
        class Region:

            def __init__(self, start):
                self.at = start

            def take(self, name, shape, dt=F32):
                size = int(np.prod(shape[1:])) * (2 if dt == BF16 else 4)
                h = nc.alloc_sbuf_tensor_at(name, list(shape), dt, offset=self.at)
                self.at += (size + 31) // 32 * 32
                return h

        top = (nc.sbuf_base + 63) // 64 * 64
        ra = Region(top)
        ident = ra.take("ident", [128, 128])
        identb = ra.take("identb", [128, 128], BF16)
        ones = ra.take("ones", [128, 128])
        onesb = ra.take("onesb", [128, 128], BF16)
        below = ra.take("below", [128, 128], BF16)
        skewI = ra.take("skewI", [128, T + KB - 1])
        skewB = ra.take("skewB", [128, T + KB - 1], BF16)
        steps = ra.take("steps", [128, 8, 3])
        seg = ra.take("seg", [128, B * NIT])
        seg8 = ra.take("seg8", [128, B * NPT])
        iota_i = ra.take("iota_i", [128, 1], I32)
        iota_t = ra.take("iota_t", [128, T])
        blk_i = ra.take("blk_i", [128, 1], I32)
        blk = ra.take("blk", [128, 1])
        lane_i = ra.take("lane_i", [128, 1], I32)
        lane = ra.take("lane", [128, 1])
        onerow = ra.take("onerow", [128, 1])
        first_up = ra.take("first_up", [128, 1])
        last_big = ra.take("last_big", [128, 1])
        wavepad = ra.take("wavepad", [128, T])
        seed = ra.take("seed", [128, 48], BF16)
        eps = ra.take("eps", [128, 1])
        x = ra.take("x", [S, B, D])
        gates = ra.take("gates", [128, 4])
        tg = ra.take("tg", [128, 4])
        bn6 = ra.take("bn6", [S, B, 6])
        mv = ra.take("mv", [S, B, 2])
        sd = ra.take("sd", [S, B])
        rstd = ra.take("rstd", [S, B])
        bb = ra.take("bb", [S, B])
        aa = ra.take("aa", [128, CT * B])
        aaT = ra.take("aaT", [CT * B, 128])
        bqP = ra.take("bqP", [128, 4])
        bkP = ra.take("bkP", [128, 4])
        bqs = ra.take("bqs", [128, 4])
        bvr = ra.take("bvr", [1, D])
        bor = ra.take("bor", [1, D])
        cw = ra.take("cw", [128, HT, 3])
        cb = ra.take("cb", [128, HT])
        cws = ra.take("cws", [128, HT, 3])
        wabs = ra.take("wabs", [128, 2])
        wmean = ra.take("wmean", [128, 2])
        winv = ra.take("winv", [128, 2])
        am = ra.take("am", [S, B])
        ari = ra.take("ari", [S, B])
        asc = ra.take("asc", [S, B])
        sx = ra.take("sx", [S, B])
        actscr = ra.take("actscr", [128, D])
        rw = Region(ra.at)
        w1T = rw.take("w1T", [128, DH, HID], BF16)
        w2T = rw.take("w2T", [128, HT, D], BF16)
        wqP = rw.take("wqP", [128, DH, 512])
        wkP = rw.take("wkP", [128, DH, 512])
        wvT = rw.take("wvT", [128, DH, D])
        woT = rw.take("woT", [128, DH, D])
        piw = Region(ra.at).take("piw", [128, 2, NI])
        rk = Region(rw.at)
        kT = rk.take("kT", [128, 4, B, SC])
        v1 = rk.take("v1", [KC, KCH, B, VW])
        rn = Region(rw.at)
        wnat = rn.take("wnat", [128, 4, 2, D])
        w1n = rn.take("w1n", [128, 2048])
        w2n = rn.take("w2n", [128, 2048])
        tern = [rn.take(f"tern{i}", [128, 2048], BF16) for i in range(2)]
        ln0 = rn.take("ln0", [S, B, D])
        ln0T = rn.take("ln0T", [128, DH, TOK])
        rl = Region(rw.at)
        piwT = rl.take("piwT", [128, NIT, NP])
        ln3 = rl.take("ln3", [S, B, D])
        c0 = rk.at
        rc = Region(c0)
        ctxP = rc.take("ctxP", [128, CT, B, D])
        rz = Region(rc.at)
        ctxT = rc.take("ctxT", [128, DH, B, KB * RB])
        dist = rc.take("dist", [S, B, KB, RB])
        LG = rz.take("LG", [128, T, 50], BF16)
        UU = rz.take("UU", [128, T, 50], BF16)
        PR = rz.take("PR", [128, T + 1, 50], BF16)
        rd = Region(max(rc.at, rz.at))
        rp = Region(rd.at)
        rmin = Region(rd.at).take("rmin", [128, T, RB])
        dwave = rd.take("dwave", [128, T, RB])
        skewed = Region(rd.at).take("skewed", [T, B, KB, RB])
        R = rd.take("R", [128, T + 1, RB + 1])
        dmin = rd.take("dmin", [128, RB])
        prod = rd.take("prod", [128, 48], BF16)
        pathT = rp.take("pathT", [T, B, KB, 32], BF16)
        path = rp.take("path", [128, B, CT, S])
        rf = Region(c0)
        hs = rf.take("hs", [128, HT, TOK])
        ln1 = rf.take("ln1", [S, B, D])
        qx = rf.take("qx", [S, B, D], BF16)
        qxT = rf.take("qxT", [128, DH, TOK], BF16)
        sxbc = rf.take("sxbc", [128, TOK])
        hb = rf.take("hb", [128, 2, B, S + 2])
        ct0 = rf.take("ct0", [128, 2, TOK])
        hmax = rf.take("hmax", [128, TOK])
        hmax2 = rf.take("hmax2", [128, TOK])
        s2bc = rf.take("s2bc", [128, TOK])
        q2 = rf.take("q2", [128, HT, TOK], BF16)
        rt = Region(c0)
        ln2 = rt.take("ln2", [S, B, D])
        ln2T = rt.take("ln2T", [128, DH, TOK])
        qT = rt.take("qT", [128, 4, TOK])
        negm = rt.take("negm", [S, 2, 512])
        E = rt.take("E", [KC, 4, KCH * S])
        pvs = rt.take("pvs", [128, 4 * S])
        rs = rt.take("rs", [S, NH])
        o = rt.take("o", [S, NH, HD])
        oT = rt.take("oT", [128, DH, S])
        loads = Region(max(rd.at, rf.at) - 4 * (NIT * D + NOT * DPV + NOT * D + NPT * DPV))
        assert rt.at <= loads.at
        r1 = Region(c0)
        ln3T = r1.take("ln3T", [128, DH, TOK])
        patT = r1.take("patT", [128, DH, NI])
        oiwT = r1.take("oiwT", [128, NO])
        gel = r1.take("gel", [128, 2, 448])
        acts = [r1.take(f"acts{k}", [128, B * n]) for k, n in enumerate((NIT, NPT, NOT))]
        key = r1.take("key", [128, B * NOT], I32)
        sgn = r1.take("sgn", [128, B * NOT], I32)
        khi = r1.take("khi", [128, B * NOT])
        klo = r1.take("klo", [128, B * NOT])
        mask = r1.take("mask", [128, 3 * B * NOT])
        cand = r1.take("cand", [128, 3, B])
        cnt = r1.take("cnt", [128, 3, B], BF16)
        ge = r1.take("ge", [128, 3, B])
        nsel = r1.take("nsel", [128, B])
        bound = r1.take("bound", [128, B])
        eq = r1.take("eq", [128, B * NOT], BF16)
        gt = r1.take("gt", [128, B * NOT])
        gsum = r1.take("gsum", [128, B], BF16)
        need = r1.take("need", [128, B])
        tot = r1.take("tot", [128, B * NOT])
        incl = r1.take("incl", [128, B * NOT])
        rank = r1.take("rank", [128, B * NOT])
        sel = r1.take("sel", [128, B * NOT])
        esel = r1.take("esel", [128, B * NPT])
        pmx = r1.take("pmx", [128, B])
        pm8 = r1.take("pm8", [B, 1])
        pmd = r1.take("pmd", [B, B])
        agr = r1.take("agr", [128, B])
        agg = r1.take("agg", [128, B])
        fin = r1.take("fin", [B, D])
        assert r1.at <= loads.at, (r1.at - c0, loads.at - c0)
        patn = loads.take("patn", [128, NIT, D])
        oiwn = loads.take("oiwn", [128, NOT, DPV])
        opat = loads.take("opat", [128, NOT, D])
        pval = loads.take("pval", [128, NPT, DPV])
        assert max(rd.at, rf.at, loads.at) <= nc.sbuf_usable_end, (rd.at, rf.at, nc.sbuf_usable_end)

        psmax = [ctx.enter_context(nc.psum_tensor(f"psmax{i}", [128, 2, 512], F32)) for i in range(2)]
        ps = [psmax[i // 2][:, i % 2, :] for i in range(4)]
        ps += [ctx.enter_context(nc.psum_tensor(f"ps{i}", [128, 512], F32))[:, :] for i in range(4, 8)]

        def sem(name):
            return ctx.enter_context(nc.semaphore(name))

        filled = [sem(f"filled{i}") for i in range(8)]
        drained = [sem(f"drained{i}") for i in range(8)]

        def fill(ins, name):
            ins.then_inc(filled[plan[name].banks[0]], 1)

        def drain(ins, name):
            ins.then_inc(drained[plan[name].banks[0]], 1)

        def wait_filled(eng, name):
            g = plan[name]
            eng.wait_ge(filled[g.banks[0]], g.nth)

        def wait_drained(eng, name):
            kind = name if isinstance(name, str) else name[0]
            if kind == "expand":
                eng.wait_ge(x_ready, name[1] + 1)
            elif kind == "ffn_down":
                eng.wait_ge(x_ready, B + name[1] + 1)
            elif kind == "spread":
                eng.wait_ge(x_ready, 3 * B + name[1] + 1)
            elif kind == "pattern":
                eng.wait_ge(gel_ready, 2 * name[1] + name[2] + 1)
            elif kind == "process":
                eng.wait_ge(acts_ready, 1)
            elif kind == "output":
                eng.wait_ge(acts_ready, 2)
            else:
                g = plan[name]
                eng.wait_ge(drained[g.banks[0]], g.nth_drain)

        def claim(eng, name):
            for g in plan[name].before:
                wait_drained(eng, g.name)

        def bank(name):
            return ps[plan[name].banks[0]]

        def bankb(name):
            return ps[plan[name].banks[0]][:, :].bitcast(BF16)

        names = ("x", "ctx", "attnW", "ffnW", "small", "biasP", "pat", "oiw", "opat", "pval", "piw0", "piw1")
        loaded = {n: sem(f"loaded_{n}") for n in names}
        (consts_ready, onerow_ready, pads_ready, stored, tg_ready, var_ready, sd_ready, ln_ready, bb_ready, aa_ready,
         wabs_ready, winv_ready, tern_ready, ones_v_ready, path_zero, seed_ready, path_done, x_ready, qx_ready, sx_ready, hb_ready,
         ct0_ready, conv_done, silu_done, hmax_ready, s2_ready, q2_ready, hmax_part, negm_ready, qmax_ready, e_ready,
         pv_part, o_ready, cnt_ready, eq_ready, sel_ready, gel_ready, gel_used, acts_ready, pmx_ready, pmd_ready,
         psh_ready, pexp_ready, esel_ready, agg_ready, vec, scl, pol) = [sem(n) for n in (
             "consts_ready onerow_ready pads_ready stored tg_ready var_ready sd_ready ln_ready bb_ready aa_ready "
             "wabs_ready winv_ready tern_ready ones_v_ready path_zero seed_ready path_done x_ready qx_ready sx_ready hb_ready "
             "ct0_ready conv_done silu_done hmax_ready s2_ready q2_ready hmax_part negm_ready qmax_ready e_ready "
             "pv_part o_ready cnt_ready eq_ready sel_ready gel_ready gel_used acts_ready pmx_ready pmd_ready "
             "psh_ready pexp_ready esel_ready agg_ready vec scl pol").split()]

        def counter(eng, s):
            n = [0]

            def did(ins):
                n[0] += 1
                ins.then_inc(s, 1)

            def settle():
                eng.wait_ge(s, n[0])
            return did, settle

        def cells(t, n):
            return t[:, 0:B * n].rearrange("p (b n) -> p b n", b=B)

        def hand(ap, dims):
            return bass.AP(ap.tensor, ap.offset, [list(ap.ap[0])] + dims)

        NCTX = 17
        block = ctx.enter_context(nc.Block())

        @block.sync
        def _(sp):
            sp.dma_start(x[:, :, :], x_in.rearrange("b s d -> s b d")).then_inc(loaded["x"], 16)
            for kt in range(CT):
                for g in range(4):
                    row = RB * (4 * kt + g)
                    n = min(32, SC - row)
                    sp.dma_start(ctxP[32 * g:32 * g + n, kt, :, :],
                                 ctx_in[:, row:row + n, :].rearrange("b r d -> r b d")).then_inc(loaded["ctx"], 16)
                    if n < 32:
                        sp.dma_start(ctxP[32 * g + n:32 * g + 32, kt, :, :],
                                     ctx_in[:, 0:32 - n, :].rearrange("b r d -> r b d")).then_inc(loaded["ctx"], 16)
            for i, w in enumerate((wq_in, wk_in, wv_in, wo_in)):
                sp.dma_start(wnat[:, i, :, :], w.rearrange("(c p) d -> p c d", p=128)).then_inc(loaded["attnW"], 16)
            sp.dma_start(w1n[:, :].rearrange("p (c d) -> p c d", c=HT),
                         w1_in.rearrange("(c p) d -> p c d", p=128)).then_inc(loaded["ffnW"], 16)
            sp.dma_start(w2n[:, :].rearrange("p (c d) -> p c d", c=2),
                         w2_in.rearrange("(c p) d -> p c d", p=128)).then_inc(loaded["ffnW"], 16)
            sp.dma_start(cw[:, :, :], conv_w.rearrange("(c p) o k -> p c (o k)", p=128)).then_inc(loaded["small"], 16)
            sp.dma_start(cb[:, :], conv_b.rearrange("(c p) -> p c", p=128),
                         allow_slow_non_contiguous=True).then_inc(loaded["small"], 16)
            sp.dma_start(bvr[0:1, :], bv_in.rearrange("(o d) -> o d", o=1)).then_inc(loaded["small"], 16)
            sp.dma_start(bor[0:1, :], bo_in.rearrange("(o d) -> o d", o=1)).then_inc(loaded["small"], 16)
            for i, g in enumerate((g_xattn, g_ffn)):
                sp.dma_start(gates[:, 2 * i:2 * i + 2],
                             g.rearrange("(o d) -> o d", o=1).broadcast_to([128, 2])).then_inc(loaded["small"], 16)
            sp.wait_ge(pads_ready, 1)
            for dst, src in ((bqP, bq_in), (bkP, bk_in)):
                for g in range(4):
                    sp.dma_start(dst[32 * g:32 * g + HD, :],
                                 src.rearrange("(t g d) -> g d t", t=4, g=4)[g],
                                 allow_slow_non_contiguous=True).then_inc(loaded["biasP"], 16)
            sp.wait_ge(x_ready, 2 * B)
            sp.dma_start(patn[:, :, :], pat_in.rearrange("(c p) d -> p c d", p=128)).then_inc(loaded["pat"], 16)
            sp.dma_start(oiwn[:, :, :], oiw_in.rearrange("(c p) d -> p c d", p=128)).then_inc(loaded["oiw"], 16)
            sp.dma_start(opat[:, :, :], opat_in.rearrange("(c p) d -> p c d", p=128)).then_inc(loaded["opat"], 16)
            sp.dma_start(pval[:, :, :], pval_in.rearrange("(c p) d -> p c d", p=128)).then_inc(loaded["pval"], 16)
            sp.wait_ge(x_ready, 3 * B)
            for i in range(NPT):
                if i >= 2:
                    wait_filled(sp, ("piwT", i - 2, NIT // 4 - 1))
                sp.dma_start(piw[:, i % 2, :], piw_in[128 * i:128 * (i + 1), :]).then_inc(loaded[f"piw{i % 2}"], 16)
            for b in range(B):
                sp.wait_ge(x_ready, 3 * B + b + 1)
                sp.dma_start(out[b], x[:, b, :]).then_inc(stored, 16)
            sp.wait_ge(stored, 16 * B)

        @block.gpsimd
        def _(pool):
            did, settle = counter(pool, pol)
            for t in (ident, identb, skewI, skewB, bqP, bkP):
                did(pool.memset(t[:, :], 0.0))
            for t in (ones, onesb, below, seg, seg8):
                did(pool.memset(t[:, :], 1.0))
            for r in range(8):
                for m in range(3):
                    did(pool.memset(steps[:, r, m:m + 1], float((m + 1) * 4 ** (7 - r))))
            did(pool.memset(eps[:, :], 1e-5))
            did(pool.iota(iota_i[:, :], [[0, 1]], base=0, channel_multiplier=1))
            did(pool.iota(iota_t[:, :], [[1, T]], base=0, channel_multiplier=0,
                          allow_small_or_imprecise_dtypes=True))
            settle()
            for t in (ident, identb):
                did(pool.affine_select(out=t[:, :], in_=t[:, :], compare_op=ALU.not_equal, fill=1.0, base=0,
                                       pattern=[[-1, 128]], channel_multiplier=1))
            for t in (skewI, skewB):
                did(pool.affine_select(out=t[:, :], in_=t[:, :], compare_op=ALU.not_equal, fill=1.0, base=KB - 1,
                                       pattern=[[-1, T + KB - 1]], channel_multiplier=1))
            did(pool.affine_select(out=below[:, :], in_=below[:, :], compare_op=ALU.is_gt, fill=0.0, base=0,
                                   pattern=[[1, 128]], channel_multiplier=-1))
            did(pool.memset(cells(seg, NIT)[:, :, 0:1], 0.0))
            did(pool.memset(cells(seg8, NPT)[:, :, 0:1], 0.0))
            settle()
            pool.memset(wqP[:, :, :], 0.0).then_inc(consts_ready, 1)
            pool.memset(wkP[:, :, :], 0.0).then_inc(consts_ready, 1)
            pool.wait_ge(onerow_ready, 1)
            pool.tensor_scalar(bkP[:, :], bkP[:, :], onerow[:, 0:1], None, ALU.add).then_inc(pads_ready, 1)
            pool.wait_ge(winv_ready, 1)
            for i, w in enumerate((w1n, w2n)):
                did(pool.tensor_scalar(w[:, :], w[:, :], winv[:, i:i + 1], MAGIC, ALU.mult, ALU.add))
                settle()
                did(pool.tensor_scalar(w[:, :], w[:, :], MAGIC, -1.0, ALU.subtract, ALU.max))
                settle()
                pool.tensor_scalar(tern[i][:, :], w[:, :], 1.0, None, ALU.min).then_inc(tern_ready, 1)
            wait_drained(pool, ("attnWT", 3))
            wait_filled(pool, ("dist", B - 1))
            pool.memset(v1[:, :, :, :], 1.0).then_inc(ones_v_ready, 1)

        @block.vector
        def _(dve):
            did, settle = counter(dve, vec)
            tt, ts, stt = dve.tensor_tensor, dve.tensor_scalar, dve.scalar_tensor_tensor

            def layernorm(n, src, dst):
                for b in range(B):
                    if n:
                        dve.wait_ge(x_ready, (n - 1) * B + b + 1)
                    did(dve.bn_stats(bn6[:, b, :], src[:, b, :]))
                settle()
                for b in range(B):
                    last = dve.bn_aggr(mv[:, b, :], bn6[:, b, :])
                    if b < B - 1:
                        did(last)
                last.then_inc(var_ready, 1)
                dve.wait_ge(sd_ready, n + 1)
                did(dve.reciprocal(rstd[:, :], sd[:, :]))
                settle()
                for b in range(B):
                    ts(dst[:, b, :], src[:, b, :], mv[:, b, 0:1], rstd[:, b:b + 1],
                       ALU.subtract, ALU.mult).then_inc(ln_ready, 1)

            dve.wait_ge(loaded["x"], 16)
            layernorm(0, x, ln0)

            dve.wait_ge(consts_ready, 1)
            did(dve.tensor_single_scalar(blk_i[:, :], iota_i[:, :], 15, ALU.bitwise_and))
            did(dve.tensor_single_scalar(lane_i[:, :], iota_i[:, :], 31, ALU.bitwise_and))
            settle()
            did(dve.tensor_copy(blk[:, :], blk_i[:, :]))
            did(dve.tensor_copy(lane[:, :], lane_i[:, :]))
            settle()
            ts(onerow[:, :], lane[:, :], float(HD), None, ALU.is_equal).then_inc(onerow_ready, 1)
            did(ts(first_up[:, :], blk[:, :], 0.5, BIG, ALU.is_gt, ALU.mult))
            did(ts(last_big[:, :], blk[:, :], float(KB - 1), BIG, ALU.is_equal, ALU.mult))
            did(ts(wavepad[:, :], iota_t[:, :], blk[:, 0:1], BIG, ALU.is_lt, ALU.mult))
            did(dve.memset(seed[:, :], 0.0))
            settle()
            qs = RB - 1 - (SC - 1) % RB
            did(ts(seed[:, 2 * qs:2 * qs + 1], blk[:, :], float(KB - 1), None, ALU.is_equal))

            for b in range(B):
                for h in range(DH):
                    nm = ("ctxT", b, h)
                    wait_filled(dve, nm)
                    drain(dve.tensor_copy(
                        ctxT[:, h, b, :].rearrange("p (k r) -> p k r", r=RB),
                        bank(nm)[:, :].rearrange("p (k r) -> p k r", r=32)[:, :, 0:RB]), nm)
            dve.wait_ge(bb_ready, 1)
            for b in range(B):
                nm = ("dist", b)
                wait_filled(dve, nm)
                drain(ts(dist[:, b, :, :].rearrange("p k r -> p (k r)"), bank(nm)[0:S, 0:KB * RB],
                         bb[:, b:b + 1], 0.0, ALU.add, ALU.max), nm)

            for m in range(RB // 4):
                nm = ("dwave", m)
                wait_filled(dve, nm)
                drain(tt(dwave[:, :, 4 * m:4 * m + 4].rearrange("p t r -> p r t"),
                         bank(nm)[:, 0:4 * T].rearrange("p (r t) -> p r t", r=4),
                         wavepad[:, :].unsqueeze(1).broadcast_to([128, 4, T]), ALU.add), nm)
            wait_drained(dve, ("dwave", RB // 4 - 1))
            did(ts(dwave[:, :, RB - 1], dwave[:, :, RB - 1], last_big[:, 0:1], None, ALU.add))
            did(dve.memset(R[:, 0, :], BIG))
            did(dve.memset(R[:, 1, 0:1], BIG))
            settle()

            above = [p - 1 if p % KB else p + KB - 1 for p in range(32)]
            for t in range(T):
                did(tt(dmin[:, :], R[:, t, 0:RB], R[:, t, 1:RB + 1], ALU.min))
                settle()
                did(dve.tensor_tensor_scan(R[:, t + 1, 1:RB + 1], dmin[:, :], dwave[:, t, :],
                                           first_up[:, 0:1] if t == 0 else R[:, t + 1, 0:1], ALU.min, ALU.add))
                settle()
                if t < T - 1:
                    did(dve.stream_shuffle(R[:, t + 2, 0:1], R[:, t + 1, RB:RB + 1], above))
                    settle()
                if t == 40:
                    wait_filled(dve, "wsum")
                    drain(ts(wmean[:, :], bank("wsum")[:, 0:2], 1.0 / (HID * D), 1e-5, ALU.mult, ALU.max), "wsum")
                    wait_drained(dve, "wsum")
                    dve.reciprocal(winv[:, :], wmean[:, :]).then_inc(winv_ready, 1)

            cd, cl, cu = R[:, 0:T, 0:RB], R[:, 0:T, 1:RB + 1], R[:, 1:T + 1, 0:RB]
            last = 2 * (RB - 1)
            Gr = hand(LG[:, :, last + 2:last + 3], [[50, T], [-2, RB]])
            Lr = hand(LG[:, :, last + 1:last + 2], [[50, T], [-2, RB]])
            Ur = hand(UU[:, :, last + 2:last + 3], [[50, T], [-2, RB]])
            wait_filled(dve, ("kT", 3, B - 1))
            did(tt(rmin[:, :, :], cu, cl, ALU.min))
            did(tt(Ur, cu, cl, ALU.is_le))
            did(dve.memset(hand(UU[:, :, 1:2], [[50, T], [2, RB]]), 1.0))
            settle()
            did(tt(Gr, rmin[:, :, :], cd, ALU.is_ge))
            settle()
            did(tt(Ur, Ur, Gr, ALU.is_gt))
            settle()
            did(tt(Lr, Ur, Gr, ALU.is_equal))
            below_lane = [p + 1 if p % KB < KB - 1 else p - KB + 1 for p in range(32)]
            did(dve.memset(LG[:, T - 1, 0:1], 0.0))
            did(dve.memset(UU[:, T - 1, 0:1], 0.0))
            did(dve.memset(PR[:, T, :], 0.0))
            did(dve.memset(PR[:, T - 1, 1:2], 0.0))
            did(dve.stream_shuffle(LG[:, 0:T - 1, 0], LG[:, 1:T, 2 * RB], below_lane))
            did(dve.stream_shuffle(UU[:, 0:T - 1, 0], UU[:, 1:T, 2 * RB], below_lane))
            settle()
            for t in range(T - 1, -1, -1):
                if t < T - 1:
                    did(tt(prod[:, :].rearrange("p (q e) -> p q e", e=2),
                           hand(PR[:, t + 1, 1:2], [[2, RB], [2, 2]]),
                           LG[:, t + 1, 0:48].rearrange("p (q e) -> p q e", e=2), ALU.mult))
                    settle()
                ins = dve.tensor_tensor_scan(PR[:, t, 2:50], UU[:, t, 0:48], seed[:, :] if t == T - 1 else prod[:, :],
                                             PR[:, t, 1:2], ALU.mult, ALU.add)
                if t:
                    did(ins)
                    settle()
                    did(dve.stream_shuffle(PR[:, t - 1, 1:2], PR[:, t, 49:50], below_lane))
                    settle()
                else:
                    ins.then_inc(path_done, 1)
            dve.memset(pathT[:, :, :, RB:32], 0.0).then_inc(path_zero, 1)
            for m in range(3):
                nm = ("pathT", m)
                wait_filled(dve, nm)
                dst = hand(pathT[:, 0, 0, RB - 1 - 8 * m:RB - 8 * m], [[-1, 8], [32, B * KB]])
                drain(dve.tensor_copy(dst, bankb(nm)[0:T, :].rearrange("p (r l) -> p r l", r=8)), nm)
            dve.wait_ge(tg_ready, 1)
            for b in range(B):
                nm = ("expand", b)
                wait_filled(dve, nm)
                stt(x[:, b, :], bank(nm)[0:S, 0:D], tg[0:S, 0:1], x[:, b, :], ALU.mult, ALU.add).then_inc(x_ready, 1)

            layernorm(1, x, ln1)
            dve.wait_ge(ln_ready, 2 * B)
            did(dve.tensor_reduce(am[:, :], ln1[:, :, :], AX.X, ALU.max, apply_absolute_value=True))
            settle()
            did(ts(am[:, :], am[:, :], 1e-5, None, ALU.max))
            settle()
            did(dve.reciprocal(ari[:, :], am[:, :]))
            settle()
            did(ts(asc[:, :], ari[:, :], 127.0, None, ALU.mult))
            ts(sx[:, :], am[:, :], 1.0 / 127.0, None, ALU.mult).then_inc(sx_ready, 1)
            settle()
            for b in range(B):
                did(ts(ln1[:, b, :], ln1[:, b, :], asc[:, b:b + 1], MAGIC, ALU.mult, ALU.add))
            settle()
            for b in range(B):
                ts(qx[:, b, :], ln1[:, b, :], MAGIC, None, ALU.subtract).then_inc(qx_ready, 1)
            dve.wait_ge(loaded["small"], 96)
            did(ts(cws[:, :, :], cw[:, :, :], wmean[:, 0:1], None, ALU.mult))
            did(dve.memset(hb[:, :, :, 0:1], 0.0))
            did(dve.memset(hb[:, :, :, S + 1:S + 2], 0.0))
            for half in range(2):
                nm = ("sxbc", half)
                wait_filled(dve, nm)
                drain(dve.tensor_copy(sxbc[:, 448 * half:448 * half + 448], bank(nm)[:, 0:448]), nm)
            settle()
            wait_drained(dve, ("sxbc", 1))
            wait_drained(dve, ("sxbc", 0))
            for c in range(HT + 2):
                if c < HT:
                    for half in range(2):
                        nm = ("ffn_up", c, half)
                        wait_filled(dve, nm)
                        if c >= 2:
                            dve.wait_ge(ct0_ready, c - 1)
                            dve.wait_ge(conv_done, c - 1)
                        drain(tt(hb[:, c % 2, 4 * half:4 * half + 4, 1:S + 1],
                                 bank(nm)[:, 0:448].rearrange("p (b s) -> p b s", b=4),
                                 sxbc[:, 448 * half:448 * half + 448].rearrange("p (b s) -> p b s", b=4),
                                 ALU.mult), nm)
                if 1 <= c <= HT:
                    e = c - 1
                    acc = ct0[:, e % 2, :].rearrange("p (b s) -> p b s", b=B)
                    dve.wait_ge(ct0_ready, e + 1)
                    did(stt(acc, hb[:, e % 2, :, 0:S], cws[:, e, 0:1], acc, ALU.mult, ALU.add))
                    settle()
                    stt(acc, hb[:, e % 2, :, 2:S + 2], cws[:, e, 2:3], acc, ALU.mult, ALU.add).then_inc(conv_done, 1)
                if c >= 2 and c % 2:
                    e = c - 3
                    dve.wait_ge(silu_done, e + 2)
                    pair = hs[:, e:e + 2, :].rearrange("p c t -> p t c")
                    if e == 0:
                        ins = dve.tensor_reduce(hmax[:, :], pair, AX.X, ALU.max, apply_absolute_value=True)
                    else:
                        did(dve.tensor_reduce(hmax2[:, :], pair, AX.X, ALU.max, apply_absolute_value=True))
                        settle()
                        dve.wait_ge(hmax_part, e // 2)
                        ins = tt(hmax[:, :], hmax[:, :], hmax2[:, :], ALU.max)
                    ins.then_inc(hmax_part, 1)
            for half in range(2):
                nm = ("hmaxT", half)
                wait_filled(dve, nm)
                drain(dve.tensor_reduce(am[:, 4 * half:4 * half + 4],
                                        bank(nm)[0:S, :].rearrange("p (b c) -> p b c", b=4), AX.X, ALU.max), nm)
            wait_drained(dve, ("hmaxT", 0))
            wait_drained(dve, ("hmaxT", 1))
            did(ts(am[:, :], am[:, :], 1e-5, None, ALU.max))
            settle()
            did(dve.reciprocal(ari[:, :], am[:, :]))
            settle()
            ts(asc[:, :], ari[:, :], 127.0, None, ALU.mult).then_inc(s2_ready, 1)
            did(ts(sx[:, :], am[:, :], 1.0 / 127.0, wmean[0:S, 1:2], ALU.mult, ALU.mult))
            settle()
            did(ts(sx[:, :], sx[:, :], tg[0:S, 2:3], None, ALU.mult))
            for half in range(2):
                nm = ("s2bc", half)
                wait_filled(dve, nm)
                drain(dve.tensor_copy(s2bc[:, 448 * half:448 * half + 448], bank(nm)[:, 0:448]), nm)
            wait_drained(dve, ("s2bc", 0))
            wait_drained(dve, ("s2bc", 1))
            for c in range(HT):
                did(tt(hs[:, c, :], hs[:, c, :], s2bc[:, :], ALU.mult))
                if c:
                    ts(q2[:, c - 1, :], hs[:, c - 1, :], MAGIC, MAGIC, ALU.add, ALU.subtract).then_inc(q2_ready, 1)
                settle()
            ts(q2[:, HT - 1, :], hs[:, HT - 1, :], MAGIC, MAGIC, ALU.add, ALU.subtract).then_inc(q2_ready, 1)
            for b in range(B):
                nm = ("ffn_down", b)
                wait_filled(dve, nm)
                stt(x[:, b, :], bank(nm)[0:S, 0:D], sx[:, b:b + 1], x[:, b, :], ALU.mult, ALU.add).then_inc(x_ready, 1)

            layernorm(2, x, ln2)
            did(dve.memset(negm[:, :, :], 0.0))
            settle()
            for t in range(4):
                for half in range(2):
                    wait_drained(dve, ("qT", t, half))
            for b in range(-1, B + 1):
                for t in range(4):
                    if b + 1 < B:
                        if b + 1 >= 2 and t == 0:
                            wait_filled(dve, ("negmT", b - 1))
                        for u in range(2):
                            nm = ("smax", b + 1, t, u)
                            wait_filled(dve, nm)
                            n0 = plan[nm].banks[0]
                            dst = negm[:, (b + 1) % 2, 128 * t + 64 * u + HD:128 * t + 64 * u + HD + 33:32]
                            drain(dve.tensor_reduce(dst, psmax[n0 // 2][0:S, :, 0:SC], AX.X, ALU.max,
                                                    negate=True), nm)
                    if b >= 1 and t == 0:
                        nm = ("pvT", b - 1)
                        wait_filled(dve, nm)
                        pvt = bank(nm)[0:S, :].rearrange("p (h e) -> p h e", e=32)
                        did(dve.reciprocal(rs[:, :], pvt[:, :, HD]))
                        settle()
                        drain(tt(o[:, :, :], pvt[:, :, 0:HD], rs[:, :].unsqueeze(2).broadcast_to([S, NH, HD]),
                                 ALU.mult), nm)
                    if b >= 1 and t == 2:
                        nm = ("wo", b - 1)
                        wait_filled(dve, nm)
                        drain(tt(ln2[:, 0, :], bank(nm)[0:S, 0:D], tg[0:S, 1:2].broadcast_to([S, D]), ALU.mult), nm)
                        wait_drained(dve, nm)
                        tt(x[:, b - 1, :], x[:, b - 1, :], ln2[:, 0, :], ALU.add).then_inc(x_ready, 1)
                if b + 1 < B:
                    nm = ("negmT", b + 1)
                    wait_filled(dve, nm)
                    qb = qT[:, :, S * (b + 1):S * (b + 2)]
                    drain(tt(qb, qb, bank(nm)[:, 0:4 * S].rearrange("p (t s) -> p t s", t=4), ALU.add), nm)

            layernorm(3, x, ln3)
            a0 = cells(acts[0], NIT)
            for i in range(NIT):
                for half in range(2):
                    dve.wait_ge(gel_ready, 2 * i + half + 1)
                    dve.tensor_reduce(a0[:, 4 * half:4 * half + 4, i],
                                      gel[:, half, :].rearrange("p (b s) -> p b s", b=4),
                                      AX.X, ALU.add).then_inc(gel_used, 1)
            dve.wait_ge(gel_used, 2 * NIT)
            did(ts(acts[0][:, :], acts[0][:, :], 1.0 / S, 0.0, ALU.mult, ALU.add))
            settle()

            def largest(k, n, keep, segs):
                w = B * n
                a = acts[k]
                bits = a[:, 0:w].bitcast(I32)
                did(ts(sgn[:, 0:w], bits, 31, 0x7FFFFFFF, ALU.arith_shift_right, ALU.bitwise_and))
                settle()
                did(tt(key[:, 0:w], sgn[:, 0:w], bits, ALU.bitwise_xor))
                settle()
                did(dve.tensor_single_scalar(sgn[:, 0:w], key[:, 0:w], 16, ALU.arith_shift_right))
                settle()
                did(dve.tensor_copy(khi[:, 0:w], sgn[:, 0:w]))
                did(dve.tensor_single_scalar(key[:, 0:w], key[:, 0:w], 0xFFFF, ALU.bitwise_and))
                settle()
                did(dve.tensor_copy(klo[:, 0:w], key[:, 0:w]))
                did(dve.memset(bound[:, :], -32768.0))
                settle()
                for r in range(16):
                    if r == 8:
                        did(tt(cells(khi, n), cells(khi, n), bound[:, :].unsqueeze(2).broadcast_to([128, B, n]),
                               ALU.subtract))
                        settle()
                        did(stt(khi[:, 0:w], khi[:, 0:w], 65536.0, klo[:, 0:w], ALU.mult, ALU.add))
                        did(dve.memset(bound[:, :], 0.0))
                        settle()
                    did(tt(cand[:, :, :], bound[:, :].unsqueeze(1).broadcast_to([128, 3, B]),
                           steps[:, r % 8, :].unsqueeze(2).broadcast_to([128, 3, B]), ALU.add))
                    settle()
                    m4 = mask[:, 0:3 * w].rearrange("p (m b n) -> p m b n", m=3, b=B)
                    did(tt(m4, cells(khi, n).unsqueeze(1).broadcast_to([128, 3, B, n]),
                           cand[:, :, :].unsqueeze(3).broadcast_to([128, 3, B, n]), ALU.is_ge))
                    settle()
                    with nc.allow_low_precision(reason="counts up to 16 are exact"):
                        dve.tensor_reduce(cnt[:, :, :], m4, AX.X, ALU.add).then_inc(cnt_ready, 1)
                    nm = ("count", k, r)
                    wait_filled(dve, nm)
                    drain(ts(ge[:, :, :].rearrange("p m b -> p (m b)"), bank(nm)[:, 0:3 * B], keep - 0.5, None,
                             ALU.is_gt), nm)
                    wait_drained(dve, nm)
                    did(dve.tensor_reduce(nsel[:, :], ge[:, :, :].rearrange("p m b -> p b m"), AX.X, ALU.add))
                    settle()
                    did(stt(bound[:, :], nsel[:, :], float(4 ** (7 - r % 8)), bound[:, :], ALU.mult, ALU.add))
                    settle()
                bb_ = bound[:, :].unsqueeze(2).broadcast_to([128, B, n])
                did(tt(cells(gt, n), cells(khi, n), bb_, ALU.is_gt))
                did(tt(cells(eq, n), cells(khi, n), bb_, ALU.is_equal))
                settle()
                with nc.allow_low_precision(reason="counts up to 16 are exact"):
                    dve.tensor_reduce(gsum[:, :], cells(gt, n), AX.X, ALU.add).then_inc(eq_ready, 1)
                nm = ("ties", k)
                wait_filled(dve, nm)
                did(dve.tensor_copy(tot[:, 0:w], bank(nm)[:, 128:128 + w]))
                did(ts(need[:, :], bank(nm)[:, 256:256 + B], -1.0, float(keep), ALU.mult, ALU.add))
                settle()
                did(dve.tensor_tensor_scan(incl[:, 0:w], segs[:, 0:w], tot[:, 0:w], 0.0, ALU.mult, ALU.add))
                settle()
                did(tt(incl[:, 0:w], incl[:, 0:w], tot[:, 0:w], ALU.subtract))
                settle()
                drain(tt(rank[:, 0:w], incl[:, 0:w], bank(nm)[:, 0:w], ALU.add), nm)
                wait_drained(dve, nm)
                did(tt(cells(rank, n), cells(rank, n), need[:, :].unsqueeze(2).broadcast_to([128, B, n]), ALU.is_lt))
                settle()
                did(tt(rank[:, 0:w], rank[:, 0:w], eq[:, 0:w], ALU.mult))
                settle()
                did(tt(sel[:, 0:w], rank[:, 0:w], gt[:, 0:w], ALU.add))
                settle()

            largest(0, NIT, NI // 8, seg)
            tt(acts[0][:, :], acts[0][:, :], sel[:, 0:B * NIT], ALU.mult).then_inc(sel_ready, 1)
            dve.wait_ge(acts_ready, 1)
            did(dve.tensor_reduce(pmx[:, :], cells(acts[1], NPT), AX.X, ALU.max))
            largest(1, NPT, NP // 8, seg8)
            dve.nop().then_inc(pmx_ready, 1)
            wait_filled(dve, "pmaxT")
            drain(dve.tensor_reduce(pm8[:, :], bank("pmaxT")[0:B, 0:128], AX.X, ALU.max), "pmaxT")
            wait_drained(dve, "pmaxT")
            ts(pmd[:, :], ident[0:B, 0:B], pm8[:, 0:1], None, ALU.mult).then_inc(pmd_ready, 1)
            wait_filled(dve, "pmaxb")
            did(dve.tensor_copy(pmx[:, :], bank("pmaxb")[:, 0:B]))
            settle()
            drain(tt(cells(esel, NPT), cells(acts[1], NPT), pmx[:, :].unsqueeze(2).broadcast_to([128, B, NPT]),
                     ALU.subtract), "pmaxb")
            dve.wait_ge(pexp_ready, 1)
            tt(esel[:, :], esel[:, :], sel[:, 0:B * NPT], ALU.mult).then_inc(esel_ready, 1)
            wait_filled(dve, "aggr")
            did(dve.reciprocal(agr[:, :], bank("aggr")[:, B:2 * B]))
            settle()
            drain(tt(agg[:, :], bank("aggr")[:, 0:B], agr[:, :], ALU.mult), "aggr")
            dve.wait_ge(acts_ready, 2)
            largest(2, NOT, NO // 8, seg)
            tt(acts[2][:, :], acts[2][:, :], sel[:, 0:B * NOT], ALU.mult).then_inc(sel_ready, 1)
            wait_filled(dve, "final")
            drain(dve.tensor_copy(fin[:, :], bank("final")[0:B, 0:D]), "final")
            for b in range(B):
                nm = ("spread", b)
                wait_filled(dve, nm)
                stt(x[:, b, :], bank(nm)[0:S, 0:D], tg[0:S, 3:4], x[:, b, :], ALU.mult, ALU.add).then_inc(x_ready, 1)

        @block.scalar
        def _(act):
            did, settle = counter(act, scl)
            fn = act.activation

            def root(n):
                act.wait_ge(var_ready, n + 1)
                fn(sd[:, :], mv[:, :, 1], ACT.Sqrt, bias=eps[0:S, 0:1]).then_inc(sd_ready, 1)

            act.wait_ge(consts_ready, 1)
            root(0)
            for b in range(B):
                act.wait_ge(ln_ready, b + 1)
                settle()
                ins = fn(actscr[0:S, 0:D], ln0[:, b, :], ACT.Square, accum_out=bb[:, b:b + 1])
                if b == B - 1:
                    ins.then_inc(bb_ready, 1)
                else:
                    did(ins)
            for h in range(DH):
                for half in range(2):
                    nm = ("lnT0", h, half)
                    wait_filled(act, nm)
                    drain(fn(ln0T[:, h, 448 * half:448 * half + 448], bank(nm)[:, 0:448], ACT.Copy, scale=-2.0), nm)
            act.wait_ge(loaded["ctx"], 16 * NCTX)
            for kt in range(CT):
                for b in range(B):
                    i = B * kt + b
                    settle()
                    if i == 0:
                        act.wait_ge(bb_ready, 1)
                    ins = fn(actscr[:, 0:D], ctxP[:, kt, b, :], ACT.Square, accum_out=aa[:, i:i + 1])
                    if i == CT * B - 1:
                        ins.then_inc(aa_ready, 1)
                    else:
                        did(ins)
            wait_filled(act, "aaT")
            drain(fn(aaT[:, :], bank("aaT")[0:CT * B, 0:128], ACT.Copy), "aaT")
            for m in range(KB // 2):
                nm = ("skew", m)
                wait_filled(act, nm)
                drain(fn(skewed[:, :, 2 * m:2 * m + 2, :].rearrange("p b k r -> p k b r"),
                         bank(nm)[0:T, 0:2 * B * RB].rearrange("p (k b r) -> p k b r", k=2, b=B), ACT.Sqrt), nm)
            for i, dst in enumerate((wqP, wkP, wvT, woT)):
                nm = ("attnWT", i)
                wait_filled(act, nm)
                if i < 2:
                    act.wait_ge(consts_ready, 2)
                    drain(fn(dst[:, :, :].rearrange("p h (g e) -> p h g e", e=32)[:, :, :, 0:HD],
                             bank(nm)[:, :].rearrange("p (h g e) -> p h g e", h=DH, e=HD), ACT.Copy), nm)
                else:
                    drain(fn(dst[:, :, :].rearrange("p h d -> p (h d)"), bank(nm)[:, :], ACT.Copy), nm)
            act.wait_ge(loaded["ffnW"], 32)
            did(fn(tern[0][:, :], w1n[:, :], ACT.Abs, accum_out=wabs[:, 0:1]))
            fn(tern[1][:, :], w2n[:, :], ACT.Abs, accum_out=wabs[:, 1:2]).then_inc(wabs_ready, 1)
            act.wait_ge(loaded["small"], 96)
            fn(tg[:, :], gates[:, :], ACT.Tanh).then_inc(tg_ready, 1)
            act.wait_ge(ones_v_ready, 1)
            for b in range(B):
                for c in range(KCH):
                    nm = ("V", b, c)
                    wait_filled(act, nm)
                    drain(fn(v1[:, c, b, 0:NH * (HD + 1)].rearrange("p (h e) -> p h e", e=HD + 1)[:, :, 0:HD],
                             bank(nm)[0:KC, 0:D].rearrange("p (h e) -> p h e", e=HD), ACT.Copy), nm)
            for w in range(2):
                for h in range(2):
                    nm = ("ternT", w, h)
                    wait_filled(act, nm)
                    if w == 0:
                        drain(fn(w1T[:, h, :], bankb(nm), ACT.Copy), nm)
                    else:
                        drain(fn(w2T[:, 4 * h:4 * h + 4, :].rearrange("p c d -> p (c d)"), bankb(nm), ACT.Copy), nm)
            act.wait_ge(loaded["biasP"], 128)
            for t in range(4):
                for b in range(B):
                    nm = ("kT", t, b)
                    wait_filled(act, nm)
                    drain(fn(kT[:, t, b, :], bank(nm)[:, 0:SC], ACT.Identity, bias=bkP[:, t:t + 1]), nm)
            fn(bqs[:, :], bqP[:, :], ACT.Copy, scale=HD ** -0.5).then_inc(scl, 1)
            for b in range(B):
                nm = ("path", b)
                wait_filled(act, nm)
                drain(fn(path[:, b, :, :].rearrange("p c s -> p (c s)"), bank(nm)[:, 0:4 * S], ACT.Copy), nm)
            root(1)
            for h in range(DH):
                nm = ("qxT", h)
                wait_filled(act, nm)
                drain(fn(qxT[:, h, :], bankb(nm)[:, 0:TOK], ACT.Copy), nm)
            for c in range(HT + 1):
                if c < HT:
                    wait_drained(act, ("ffn_up", c, 1))
                    wait_drained(act, ("ffn_up", c, 0))
                    if c >= 2:
                        act.wait_ge(silu_done, c - 1)
                    fn(ct0[:, c % 2, :].rearrange("p (b s) -> p b s", b=B), hb[:, c % 2, :, 1:S + 1], ACT.Identity,
                       bias=cb[:, c:c + 1], scale=cws[:, c, 1:2]).then_inc(ct0_ready, 1)
                if c >= 1:
                    act.wait_ge(conv_done, c)
                    fn(hs[:, c - 1, :], ct0[:, (c - 1) % 2, :], ACT.Silu).then_inc(silu_done, 1)
            root(2)
            for h in range(DH):
                for half in range(2):
                    nm = ("lnT2", h, half)
                    wait_filled(act, nm)
                    drain(fn(ln2T[:, h, 448 * half:448 * half + 448], bank(nm)[:, 0:448], ACT.Copy), nm)
            for t in range(4):
                for half in range(2):
                    nm = ("qT", t, half)
                    wait_filled(act, nm)
                    drain(fn(qT[:, t, 448 * half:448 * half + 448], bank(nm)[:, 0:448], ACT.Identity,
                             bias=bqs[:, t:t + 1], scale=HD ** -0.5), nm)
            for b in range(B + 1):
                for t in range(4):
                    if b < B:
                        for g in range(4):
                            n = NH * b + 4 * t + g
                            nm = ("scoreT", b, t, g)
                            wait_filled(act, nm)
                            if n >= 4:
                                pb, ph = divmod(n - 4, NH)
                                if ph == NH - 1:
                                    wait_filled(act, ("pv", pb))
                                else:
                                    act.wait_ge(pv_part, (NH - 1) * pb + ph + 1)
                            ins = fn(E[:, n % 4, :], bank(nm)[0:KC, 0:KCH * S], ACT.Exp)
                            drain(ins, nm)
                    if b >= 1 and t == 1:
                        nm = ("oT", b - 1)
                        wait_filled(act, nm)
                        drain(fn(oT[:, :, :].rearrange("p h s -> p (h s)"), bank(nm)[:, 0:DH * S], ACT.Copy), nm)
                if b < B:
                    nm = ("pv", b)
                    wait_filled(act, nm)
                    drain(fn(pvs[:, :], bank(nm)[:, 0:4 * S], ACT.Copy), nm)
            root(3)
            for h in range(DH):
                for half in range(2):
                    nm = ("lnT3", h, half)
                    wait_filled(act, nm)
                    drain(fn(ln3T[:, h, 448 * half:448 * half + 448], bank(nm)[:, 0:448], ACT.Copy), nm)
            for m in range(NIT // 2):
                nm = ("patT", m)
                wait_filled(act, nm)
                drain(fn(patT[:, :, 256 * m:256 * m + 256], bank(nm)[:, :].rearrange("p (h n) -> p h n", h=DH),
                         ACT.Copy), nm)
            for i in range(NIT):
                for half in range(2):
                    nm = ("pattern", i, half)
                    wait_filled(act, nm)
                    if i >= 1:
                        act.wait_ge(gel_used, 2 * (i - 1) + half + 1)
                    fn(gel[:, half, :], bank(nm)[:, 0:448], ACT.Gelu).then_inc(gel_ready, 1)
            for m in range(NOT // 4):
                nm = ("oiwT", m)
                wait_filled(act, nm)
                drain(fn(oiwT[:, 512 * m:512 * m + 512], bank(nm)[:, :], ACT.Copy), nm)
            for i in range(NPT):
                for m in range(NIT // 4):
                    nm = ("piwT", i, m)
                    wait_filled(act, nm)
                    drain(fn(piwT[:, 4 * m:4 * m + 4, 128 * i:128 * i + 128],
                             bank(nm)[:, :].rearrange("p (c n) -> p c n", c=4), ACT.Copy), nm)
            wait_filled(act, "process")
            fn(cells(acts[1], NPT), bank("process")[:, 0:B * NPT].rearrange("p (n b) -> p b n", b=B),
               ACT.Gelu).then_inc(acts_ready, 1)
            wait_drained(act, "pmaxb")
            fn(esel[:, :], esel[:, :], ACT.Exp).then_inc(pexp_ready, 1)
            wait_filled(act, "output")
            fn(cells(acts[2], NOT), bank("output")[:, 0:B * NOT].rearrange("p (n b) -> p b n", b=B),
               ACT.Gelu).then_inc(acts_ready, 1)

        @block.tensor
        def _(pe):
            mm, tr = pe.matmul, pe.transpose

            def ln_transposes(n, name, src, dt_ident):
                for h in range(DH):
                    for half in range(2):
                        nm = (name, h, half)
                        claim(pe, nm)
                        for i in range(4):
                            b = 4 * half + i
                            pe.wait_ge(ln_ready, n * B + b + 1)
                            ins = tr(bank(nm)[:, S * i:S * i + S], src[:, b, 128 * h:128 * h + 128],
                                     ident[0:S, 0:S])
                        fill(ins, nm)

            pe.wait_ge(consts_ready, 1)
            ln_transposes(0, "lnT0", ln0, ident)
            pe.wait_ge(loaded["ctx"], 16 * NCTX)
            for b in range(B):
                for h in range(DH):
                    nm = ("ctxT", b, h)
                    claim(pe, nm)
                    for kt in range(CT):
                        ins = tr(bank(nm)[:, 128 * kt:128 * kt + 128], ctxP[:, kt, b, 128 * h:128 * h + 128],
                                 ident[:, :])
                    fill(ins, nm)
            claim(pe, "aaT")
            pe.wait_ge(aa_ready, 1)
            fill(tr(bank("aaT")[0:CT * B, 0:128], aa[:, :], ident[:, :]), "aaT")
            for h in range(DH):
                for half in range(2):
                    wait_drained(pe, ("lnT0", h, half))
            wait_drained(pe, "aaT")
            for b in range(B):
                nm = ("dist", b)
                claim(pe, nm)
                for h in range(DH):
                    wait_drained(pe, ("ctxT", b, h))
                    mm(bank(nm)[0:S, 0:KB * RB], ln0T[:, h, S * b:S * b + S], ctxT[:, h, b, :],
                       start=(h == 0), stop=False)
                for kt in range(CT):
                    i = B * kt + b
                    ins = mm(bank(nm)[0:S, 96 * kt:96 * kt + 96], ident[0:CT * B, i:i + 1].broadcast_to([CT * B, S]),
                             aaT[:, :].rearrange("p (g r) -> p g r", g=4)[:, :, 0:RB], start=False,
                             stop=(kt == CT - 1))
                fill(ins, nm)
            for b in range(B):
                wait_drained(pe, ("dist", b))
            for m in range(KB // 2):
                nm = ("skew", m)
                claim(pe, nm)
                for e in range(2):
                    k = 2 * m + e
                    ins = mm(bank(nm)[0:T, B * RB * e:B * RB * (e + 1)], skewI[0:S, KB - 1 - k:KB - 1 - k + T],
                             dist[:, :, k, :], start=True, stop=True)
                fill(ins, nm)
            for m in range(KB // 2):
                wait_drained(pe, ("skew", m))
            for m in range(RB // 4):
                nm = ("dwave", m)
                claim(pe, nm)
                for i in range(4):
                    ins = tr(bank(nm)[:, T * i:T * i + T],
                             skewed[:, :, :, 4 * m + i].rearrange("p b k -> p (b k)"), ident[0:T, 0:T])
                fill(ins, nm)
            pe.wait_ge(loaded["attnW"], 64)
            for i in range(4):
                nm = ("attnWT", i)
                claim(pe, nm)
                for h in range(DH):
                    for c in range(2):
                        ins = tr(bank(nm)[:, D * h + 128 * c:D * h + 128 * c + 128],
                                 wnat[:, i, c, 128 * h:128 * h + 128], ident[:, :])
                fill(ins, nm)
            claim(pe, "wsum")
            pe.wait_ge(wabs_ready, 1)
            fill(mm(bank("wsum")[:, 0:2], ones[:, :], wabs[:, :], start=True, stop=True), "wsum")
            pe.wait_ge(loaded["small"], 96)
            wait_drained(pe, ("attnWT", 2))
            for b in range(B):
                for c in range(KCH):
                    nm = ("V", b, c)
                    claim(pe, nm)
                    for h in range(DH):
                        mm(bank(nm)[0:KC, 0:D], ctxT[:, h, b, KC * c:KC * c + KC], wvT[:, h, :],
                           start=(h == 0), stop=False)
                    fill(mm(bank(nm)[0:KC, 0:D], ones[0:1, 0:KC], bvr[0:1, :], start=False, stop=True), nm)
            for w in range(2):
                pe.wait_ge(tern_ready, w + 1)
                for h in range(2):
                    nm = ("ternT", w, h)
                    claim(pe, nm)
                    for i in range(8):
                        if w == 0:
                            src = tern[0][:, D * i + 128 * h:D * i + 128 * h + 128]
                        else:
                            src = tern[1][:, HID * (i % 2) + 128 * (4 * h + i // 2):][:, 0:128]
                        ins = tr(bankb(nm)[:, 128 * i:128 * i + 128], src, identb[:, :])
                    fill(ins, nm)
            for t in range(4):
                for b in range(B):
                    nm = ("kT", t, b)
                    claim(pe, nm)
                    for h in range(DH):
                        ins = mm(bank(nm)[:, 0:SC], wkP[:, h, 128 * t:128 * t + 128], ctxT[:, h, b, 0:SC],
                                 start=(h == 0), stop=(h == DH - 1))
                    fill(ins, nm)
            pe.wait_ge(path_done, 1)
            for m in range(3):
                nm = ("pathT", m)
                claim(pe, nm)
                for i in range(8):
                    ins = tr(bankb(nm)[0:T, 128 * i:128 * i + 128], PR[:, 0:T, 2 * (8 * m + i) + 3], identb[:, :])
                fill(ins, nm)
            for m in range(3):
                wait_drained(pe, ("pathT", m))
            pe.wait_ge(path_zero, 1)
            for b in range(B):
                nm = ("path", b)
                claim(pe, nm)
                for kt in range(CT):
                    for g in range(4):
                        k = 4 * kt + g
                        ins = mm(bank(nm)[32 * g:32 * g + 32, S * kt:S * kt + S], pathT[:, b, k, :],
                                 skewB[0:T, KB - 1 + k:KB - 1 + k + S], start=True, stop=True)
                fill(ins, nm)
            for b in range(B):
                nm = ("expand", b)
                claim(pe, nm)
                wait_drained(pe, ("path", b))
                for kt in range(CT):
                    ins = mm(bank(nm)[0:S, 0:D], path[:, b, kt, :], ctxP[:, kt, b, :], start=(kt == 0),
                             stop=(kt == CT - 1))
                fill(ins, nm)
            pe.wait_ge(qx_ready, B)
            for h in range(DH):
                nm = ("qxT", h)
                claim(pe, nm)
                for b in range(B):
                    ins = tr(bankb(nm)[:, S * b:S * b + S], qx[:, b, 128 * h:128 * h + 128], identb[0:S, 0:S])
                fill(ins, nm)
            pe.wait_ge(sx_ready, 1)

            def token_rows(name, cols):
                for half in range(2):
                    nm = (name, half)
                    claim(pe, nm)
                    for i in range(4):
                        b = 4 * half + i
                        ins = mm(bank(nm)[:, S * i:S * i + S], cols[:, b:b + 1].broadcast_to([S, 128]),
                                 ident[0:S, 0:S], start=True, stop=True)
                    fill(ins, nm)

            token_rows("sxbc", sx)
            for h in range(DH):
                wait_drained(pe, ("qxT", h))
            for c in range(HT):
                for half in range(2):
                    nm = ("ffn_up", c, half)
                    claim(pe, nm)
                    for h in range(DH):
                        ins = mm(bank(nm)[:, 0:448], w1T[:, h, 128 * c:128 * c + 128],
                                 qxT[:, h, 448 * half:448 * half + 448], start=(h == 0), stop=(h == DH - 1))
                    fill(ins, nm)
            pe.wait_ge(hmax_part, HT // 2)
            for half in range(2):
                nm = ("hmaxT", half)
                claim(pe, nm)
                for i in range(4):
                    b = 4 * half + i
                    ins = tr(bank(nm)[0:S, 128 * i:128 * i + 128], hmax[:, S * b:S * b + S], ident[:, :])
                fill(ins, nm)
            pe.wait_ge(s2_ready, 1)
            token_rows("s2bc", asc)
            for b in range(B):
                nm = ("ffn_down", b)
                claim(pe, nm)
                for c in range(HT):
                    if b == 0:
                        pe.wait_ge(q2_ready, c + 1)
                    ins = mm(bank(nm)[0:S, 0:D], q2[:, c, S * b:S * b + S], w2T[:, c, :], start=(c == 0),
                             stop=(c == HT - 1))
                fill(ins, nm)
            ln_transposes(2, "lnT2", ln2, ident)
            for h in range(DH):
                for half in range(2):
                    wait_drained(pe, ("lnT2", h, half))
            for t in range(4):
                for half in range(2):
                    nm = ("qT", t, half)
                    claim(pe, nm)
                    for h in range(DH):
                        ins = mm(bank(nm)[:, 0:448], wqP[:, h, 128 * t:128 * t + 128],
                                 ln2T[:, h, 448 * half:448 * half + 448], start=(h == 0), stop=(h == DH - 1))
                    fill(ins, nm)
            for t in range(4):
                for half in range(2):
                    wait_drained(pe, ("qT", t, half))

            def value_product(b, n):
                t, g = n // 4, n % 4
                wait_drained(pe, ("scoreT", b, t, g))
                if n == 0:
                    claim(pe, ("pv", b))
                m = NH * b + n
                for c in range(KCH):
                    ins = mm(bank(("pv", b))[32 * g:32 * g + 32, S * t:S * t + S],
                             v1[:, c, b, (HD + 1) * n:(HD + 1) * n + 32], E[:, m % 4, S * c:S * c + S],
                             start=(c == 0), stop=(c == KCH - 1))
                if n == NH - 1:
                    fill(ins, ("pv", b))
                else:
                    ins.then_inc(pv_part, 1)

            for b in range(-1, B + 1):
                for t in range(4):
                    if b + 1 < B:
                        for u in range(2):
                            nm = ("smax", b + 1, t, u)
                            claim(pe, nm)
                            for e in range(2):
                                g = 2 * u + e
                                ins = mm(psmax[u][0:S, e, 0:SC], qT[32 * g:32 * g + 32, t, S * (b + 1):S * (b + 2)],
                                         kT[32 * g:32 * g + 32, t, b + 1, :], start=True, stop=True)
                            fill(ins, nm)
                    if b >= 1 and t == 0:
                        nm = ("pvT", b - 1)
                        claim(pe, nm)
                        wait_drained(pe, ("pv", b - 1))
                        for i in range(4):
                            ins = tr(bank(nm)[0:S, 128 * i:128 * i + 128], pvs[:, S * i:S * i + S], ident[:, :])
                        fill(ins, nm)
                    if b >= 1 and t == 1:
                        nm = ("oT", b - 1)
                        claim(pe, nm)
                        of = o[:, :, :].rearrange("p h e -> p (h e)")
                        for h in range(DH):
                            ins = tr(bank(nm)[:, S * h:S * h + S], of[:, 128 * h:128 * h + 128], ident[0:S, 0:S])
                        fill(ins, nm)
                    if b >= 1 and t == 2:
                        nm = ("wo", b - 1)
                        claim(pe, nm)
                        for h in range(DH):
                            mm(bank(nm)[0:S, 0:D], oT[:, h, :], woT[:, h, :], start=(h == 0), stop=False)
                        fill(mm(bank(nm)[0:S, 0:D], ones[0:1, 0:S], bor[0:1, :], start=False, stop=True), nm)
                    if 0 <= b < B:
                        for g in range(4):
                            nm = ("scoreT", b, t, g)
                            claim(pe, nm)
                            if t == 0 and g == 0:
                                wait_drained(pe, ("negmT", b))
                            for c in range(KCH):
                                ins = mm(bank(nm)[0:KC, S * c:S * c + S],
                                         kT[32 * g:32 * g + 32, t, b, KC * c:KC * c + KC],
                                         qT[32 * g:32 * g + 32, t, S * b:S * b + S], start=True, stop=True)
                            fill(ins, nm)
                            if 4 * t + g >= 1:
                                value_product(b, 4 * t + g - 1)
                if 0 <= b < B:
                    value_product(b, NH - 1)
                if b + 1 < B:
                    nm = ("negmT", b + 1)
                    claim(pe, nm)
                    for t in range(4):
                        for u in range(2):
                            wait_drained(pe, ("smax", b + 1, t, u))
                        ins = tr(bank(nm)[:, S * t:S * t + S], negm[:, (b + 1) % 2, 128 * t:128 * t + 128],
                                 ident[0:S, 0:S])
                    fill(ins, nm)
            ln_transposes(3, "lnT3", ln3, ident)
            pe.wait_ge(loaded["pat"], 16)
            for m in range(NIT // 2):
                nm = ("patT", m)
                claim(pe, nm)
                for h in range(DH):
                    for i in range(2):
                        ins = tr(bank(nm)[:, 256 * h + 128 * i:256 * h + 128 * i + 128],
                                 patn[:, 2 * m + i, 128 * h:128 * h + 128], ident[:, :])
                fill(ins, nm)
            for h in range(DH):
                for half in range(2):
                    wait_drained(pe, ("lnT3", h, half))
            for i in range(NIT):
                wait_drained(pe, ("patT", i // 2))
                for half in range(2):
                    nm = ("pattern", i, half)
                    claim(pe, nm)
                    for h in range(DH):
                        ins = mm(bank(nm)[:, 0:448], patT[:, h, 128 * i:128 * i + 128],
                                 ln3T[:, h, 448 * half:448 * half + 448], start=(h == 0), stop=(h == DH - 1))
                    fill(ins, nm)
            pe.wait_ge(loaded["oiw"], 16)
            for m in range(NOT // 4):
                nm = ("oiwT", m)
                claim(pe, nm)
                for i in range(4):
                    ins = tr(bank(nm)[:, 128 * i:128 * i + 128], oiwn[:, 4 * m + i, :], ident[:, :])
                fill(ins, nm)

            def count(k, r):
                nm = ("count", k, r)
                claim(pe, nm)
                pe.wait_ge(cnt_ready, 16 * k + r + 1)
                fill(mm(bank(nm)[:, 0:3 * B], onesb[:, :], cnt[:, :, :].rearrange("p m b -> p (m b)"),
                        start=True, stop=True), nm)

            def ties(k, n):
                nm = ("ties", k)
                claim(pe, nm)
                pe.wait_ge(eq_ready, k + 1)
                w = B * n
                mm(bank(nm)[:, 0:w], below[:, :], eq[:, 0:w], start=True, stop=True)
                mm(bank(nm)[:, 128:128 + w], onesb[:, :], eq[:, 0:w], start=True, stop=True)
                fill(mm(bank(nm)[:, 256:256 + B], onesb[:, :], gsum[:, :], start=True, stop=True), nm)

            for i in range(NPT):
                pe.wait_ge(loaded[f"piw{i % 2}"], 16 * (i // 2 + 1))
                for m in range(NIT // 4):
                    nm = ("piwT", i, m)
                    claim(pe, nm)
                    for e in range(4):
                        c = 4 * m + e
                        ins = tr(bank(nm)[:, 128 * e:128 * e + 128], piw[:, i % 2, 128 * c:128 * c + 128],
                                 ident[:, :])
                    fill(ins, nm)
                for r in (2 * i, 2 * i + 1):
                    count(0, r)
            ties(0, NIT)
            claim(pe, "process")
            pe.wait_ge(sel_ready, 1)
            for i in range(NPT):
                for m in range(NIT // 4):
                    wait_drained(pe, ("piwT", i, m))
                for c in range(NIT):
                    ins = mm(bank("process")[:, B * i:B * i + B], piwT[:, c, 128 * i:128 * i + 128],
                             cells(acts[0], NIT)[:, :, c], start=(c == 0), stop=(c == NIT - 1))
            fill(ins, "process")
            for r in range(16):
                count(1, r)
            ties(1, NPT)
            claim(pe, "pmaxT")
            pe.wait_ge(pmx_ready, 1)
            fill(tr(bank("pmaxT")[0:B, 0:128], pmx[:, :], ident[:, :]), "pmaxT")
            claim(pe, "pmaxb")
            pe.wait_ge(pmd_ready, 1)
            fill(mm(bank("pmaxb")[:, 0:B], ones[0:B, :], pmd[:, :], start=True, stop=True), "pmaxb")
            claim(pe, "aggr")
            pe.wait_ge(esel_ready, 1)
            pe.wait_ge(loaded["pval"], 16)
            for i in range(NPT):
                mm(bank("aggr")[:, 0:B], pval[:, i, :], cells(esel, NPT)[:, :, i], start=(i == 0),
                   stop=(i == NPT - 1))
            for i in range(NPT):
                ins = mm(bank("aggr")[:, B:2 * B], ones[:, :], cells(esel, NPT)[:, :, i], start=(i == 0),
                         stop=(i == NPT - 1))
            fill(ins, "aggr")
            claim(pe, "output")
            wait_drained(pe, "aggr")
            for m in range(NOT // 4):
                wait_drained(pe, ("oiwT", m))
            for i in range(NOT):
                ins = mm(bank("output")[:, B * i:B * i + B], oiwT[:, 128 * i:128 * i + 128], agg[:, :], start=True,
                         stop=True)
            fill(ins, "output")
            for r in range(16):
                count(2, r)
            ties(2, NOT)
            claim(pe, "final")
            pe.wait_ge(sel_ready, 2)
            pe.wait_ge(loaded["opat"], 16)
            for i in range(NOT):
                ins = mm(bank("final")[0:B, 0:D], cells(acts[2], NOT)[:, :, i], opat[:, i, :], start=(i == 0),
                         stop=(i == NOT - 1))
            fill(ins, "final")
            wait_drained(pe, "final")
            for b in range(B):
                nm = ("spread", b)
                claim(pe, nm)
                fill(mm(bank(nm)[0:S, 0:D], ident[0:B, b:b + 1].broadcast_to([B, S]), fin[:, :], start=True,
                        stop=True), nm)


INPUTS = ["x", "ctx_1024", "g_xattn", "g_ffn", "L0_ffn_w1", "L0_ffn_conv_w", "L0_ffn_conv_b", "L0_ffn_w2",
          "L1_xattn_Wq", "L1_xattn_bq", "L1_xattn_Wk", "L1_xattn_bk", "L1_xattn_Wv", "L1_xattn_bv",
          "L1_xattn_Wo", "L1_xattn_bo", "L1_ffn_input_patterns", "L1_ffn_process_input_weights",
          "L1_ffn_process_values", "L1_ffn_output_input_weights", "L1_ffn_output_patterns"]


def kernel(**inputs):
    import concourse.bacc as bacc
    from concourse.bass_utils import run_bass_kernel_spmd

    nc = bacc.Bacc("TRN2", target_bir_lowering=False, num_devices=1)
    arrays, args = {}, []
    for name in INPUTS:
        a = np.ascontiguousarray(inputs[name])
        arrays[f"in_{name}"] = a
        args.append(nc.dram_tensor(f"in_{name}", a.shape, mybir.dt.from_np(a.dtype), kind="ExternalInput").ap())
    args.append(nc.dram_tensor("out", (B, S, D), F32, kind="ExternalOutput").ap())
    build_program(nc, *args)
    return run_bass_kernel_spmd(nc, [arrays], core_ids=[0]).results[0]["out"]
```

```python
import numpy as np
import concourse.bass as bass
from concourse import mybir
from contextlib import ExitStack

F32, BF16, I32 = mybir.dt.float32, mybir.dt.bfloat16, mybir.dt.int32
ALU = mybir.AluOpType
ACT = mybir.ActivationFunctionType
AX = mybir.AxisListType

B, S, D, SC = 8, 112, 256, 375
DH = D // 128
KB, RB = 16, 24
CT = 4
T = S + KB - 1
HID, HT = 1024, 8
NH, HD = 16, 16
KC, KCH = 125, 3
VW = NH * (HD + 1) + 15
NI, NP, NO, DPV = 2048, 1024, 2048, 128
NIT, NPT, NOT = NI // 128, NP // 128, NO // 128
BIG = 1.0e30
MAGIC = 12582912.0
TOK = B * S


SIGNALLED_BY_RESULT = ("expand", "ffn_down", "pattern", "output", "spread")


class Group:

    def __init__(self, name, banks, nth, nth_drain, before):
        self.name, self.banks, self.nth, self.nth_drain, self.before = name, banks, nth, nth_drain, before


class PsumPlan:

    def __init__(self, nbanks):
        self.uses = [0] * nbanks
        self.drains = [0] * nbanks
        self.last = [None] * nbanks
        self.groups = {}

    def add(self, name, *banks):
        before = []
        for b in banks:
            if self.last[b] is not None and self.last[b] not in before:
                before.append(self.last[b])
        self.uses[banks[0]] += 1
        if (name if isinstance(name, str) else name[0]) not in SIGNALLED_BY_RESULT:
            self.drains[banks[0]] += 1
        g = Group(name, banks, self.uses[banks[0]], self.drains[banks[0]], before)
        for b in banks:
            self.last[b] = g
        self.groups[name] = g

    def __getitem__(self, name):
        return self.groups[name]


def plan_psum():
    p = PsumPlan(8)
    n = [0]

    def ring(name, banks=tuple(range(8))):
        p.add(name, banks[n[0] % len(banks)])
        n[0] += 1

    for h in range(DH):
        for half in range(2):
            ring(("lnT0", h, half))
    for b in range(B):
        for h in range(DH):
            ring(("ctxT", b, h))
    ring("aaT")
    for b in range(B):
        ring(("dist", b))
    for m in range(KB // 2):
        ring(("skew", m))
    for m in range(RB // 4):
        ring(("dwave", m))
    for w in range(4):
        ring(("attnWT", w))
    ring("wsum")
    for b in range(B):
        for c in range(KCH):
            ring(("V", b, c))
    for w in range(2):
        for h in range(2):
            ring(("ternT", w, h))
    for t in range(4):
        for b in range(B):
            ring(("kT", t, b))
    for m in range(3):
        ring(("pathT", m))
    for b in range(B):
        ring(("path", b))
    for b in range(B):
        ring(("expand", b))
    for h in range(DH):
        ring(("qxT", h))
    for half in range(2):
        ring(("sxbc", half))
    for c in range(HT):
        for half in range(2):
            ring(("ffn_up", c, half))
    for half in range(2):
        ring(("hmaxT", half))
    for half in range(2):
        ring(("s2bc", half))
    for b in range(B):
        ring(("ffn_down", b))
    for h in range(DH):
        for half in range(2):
            ring(("lnT2", h, half))
    for t in range(4):
        for half in range(2):
            ring(("qT", t, half))
    for b in range(-1, B + 1):
        for t in range(4):
            if b + 1 < B:
                for u in range(2):
                    p.add(("smax", b + 1, t, u), 2 * u, 2 * u + 1)
            if 0 <= b < B:
                for c in range(KCH):
                    p.add(("scoreT", b, t, c), 4 + (KCH * t + c) % 2)
            if 0 <= b < B and t == 1:
                p.add(("pv", b), 6)
            if b >= 1 and t >= 1:
                p.add((("pvT", "oT", "wo")[t - 1], b - 1), 7)
        if b + 1 < B:
            p.add(("negmT", b + 1), 7)
    n[0] = 0
    for h in range(DH):
        for half in range(2):
            ring(("lnT3", h, half))
    for m in range(NIT // 2):
        ring(("patT", m))
    for i in range(NIT):
        for half in range(2):
            ring(("pattern", i, half))
    for m in range(NOT // 4):
        ring(("oiwT", m))
    n[0] = 0
    for p_ in range(NPT):
        for m in range(NIT // 4):
            ring(("piwT", p_, m), (0, 1, 2, 3))
    for k in range(3):
        p.add(("actT", k), 7)
        for r in range(16):
            p.add(("count", k, r), 4 + r % 2)
        p.add(("ties", k), 6)
        p.add(("selT", k), 7)
        if k == 0:
            p.add(("process", 0), 0)
            p.add(("process", 1), 1)
            p.add(("processT", 0), 2)
            p.add(("processT", 1), 3)
            p.add("pmaxT", 0)
            p.add("pmaxb", 1)
        elif k == 1:
            p.add("aggr", 2)
            p.add("output", 3)
    p.add("final", 0)
    for b in range(B):
        p.add(("spread", b), b % 4)
    return p



def build_program(nc, x_in, ctx_in, g_xattn, g_ffn, w1_in, conv_w, conv_b, w2_in,
                  wq_in, bq_in, wk_in, bk_in, wv_in, bv_in, wo_in, bo_in,
                  pat_in, piw_in, pval_in, oiw_in, opat_in, out):
    plan = plan_psum()
    ctx = ExitStack()
    with ctx:
        class Region:

            def __init__(self, start):
                self.at = start

            def take(self, name, shape, dt=F32):
                size = int(np.prod(shape[1:])) * (2 if dt == BF16 else 4)
                h = nc.alloc_sbuf_tensor_at(name, list(shape), dt, offset=self.at)
                self.at += (size + 31) // 32 * 32
                return h

        top = (nc.sbuf_base + 63) // 64 * 64
        ra = Region(top)
        ident = ra.take("ident", [128, 128])
        identb = ra.take("identb", [128, 128], BF16)
        ones = ra.take("ones", [128, 128])
        same = [ra.take(f"same{n}", [B * n, B * n], BF16) for n in (NIT, NPT)]
        under = [ra.take(f"under{n}", [B * n, B * n], BF16) for n in (NIT, NPT)]
        gmask = ra.take("gmask", [128, 4])
        skewI = ra.take("skewI", [128, T + KB - 1])
        skewB = ra.take("skewB", [128, T + KB - 1], BF16)
        steps = ra.take("steps", [128, 8, 3])
        iota_i = ra.take("iota_i", [128, 1], I32)
        iota_t = ra.take("iota_t", [128, T])
        blk_i = ra.take("blk_i", [128, 1], I32)
        blk = ra.take("blk", [128, 1])
        lane_i = ra.take("lane_i", [128, 1], I32)
        lane = ra.take("lane", [128, 1])
        onerow = ra.take("onerow", [128, 1])
        first_up = ra.take("first_up", [128, 1])
        last_big = ra.take("last_big", [128, 1])
        wavepad = ra.take("wavepad", [128, T])
        seed = ra.take("seed", [128, 48], BF16)
        eps = ra.take("eps", [128, 1])
        x = ra.take("x", [S, B, D])
        gates = ra.take("gates", [128, 4])
        tg = ra.take("tg", [128, 4])
        bn6 = ra.take("bn6", [S, B, 6])
        mv = ra.take("mv", [S, B, 2])
        sd = ra.take("sd", [S, B])
        rstd = ra.take("rstd", [S, B])
        bb = ra.take("bb", [S, B])
        aa = ra.take("aa", [128, CT * B])
        aaT = ra.take("aaT", [CT * B, 128])
        bqP = ra.take("bqP", [128, 4])
        bkP = ra.take("bkP", [128, 4])
        bqs = ra.take("bqs", [128, 4])
        bvr = ra.take("bvr", [1, D])
        bor = ra.take("bor", [1, D])
        cw = ra.take("cw", [128, HT, 3])
        cb = ra.take("cb", [128, HT])
        cws = ra.take("cws", [128, HT, 3])
        wabs = ra.take("wabs", [128, 2])
        wmean = ra.take("wmean", [128, 2])
        winv = ra.take("winv", [128, 2])
        am = ra.take("am", [S, B])
        ari = ra.take("ari", [S, B])
        asc = ra.take("asc", [S, B])
        sx = ra.take("sx", [S, B])
        actscr = ra.take("actscr", [128, D])
        rw = Region(ra.at)
        w1T = rw.take("w1T", [128, DH, HID], BF16)
        w2T = rw.take("w2T", [128, HT, D], BF16)
        wqP = rw.take("wqP", [128, DH, 512])
        wkP = rw.take("wkP", [128, DH, 512])
        wvT = rw.take("wvT", [128, DH, D])
        woT = rw.take("woT", [128, DH, D])
        piw = Region(ra.at).take("piw", [128, 2, NI])
        rk = Region(rw.at)
        kT = rk.take("kT", [128, 4, B, SC])
        v1 = rk.take("v1", [KC, KCH, B, VW])
        rn = Region(rw.at)
        wnat = rn.take("wnat", [128, 4, 2, D])
        w1n = rn.take("w1n", [128, 2048])
        w2n = rn.take("w2n", [128, 2048])
        tern = [rn.take(f"tern{i}", [128, 2048], BF16) for i in range(2)]
        ln0 = rn.take("ln0", [S, B, D])
        ln0T = rn.take("ln0T", [128, DH, TOK])
        rl = Region(rw.at)
        piwT = rl.take("piwT", [128, NIT, NP])
        ln3 = rl.take("ln3", [S, B, D])
        c0 = rk.at
        rc = Region(c0)
        ctxP = rc.take("ctxP", [128, CT, B, D])
        rz = Region(c0)
        LG = rz.take("LG", [128, T, 50], BF16)
        UU = rz.take("UU", [128, T, 50], BF16)
        PR = rz.take("PR", [128, T + 1, 50], BF16)
        rx = Region(max(rc.at, rz.at))
        ctxT = Region(rx.at).take("ctxT", [128, DH, B, KB * RB])
        ctx2 = rx.take("ctx2", [128, CT, B, D])
        rd = Region(rx.at)
        dist = Region(rd.at).take("dist", [S, B, KB, RB])
        rp = Region(rd.at)
        dwave = rd.take("dwave", [128, T, RB])
        skewed = Region(max(rd.at, rx.at + 4 * B * KB * RB)).take("skewed", [T, B, KB, RB])
        rd.at = max(rd.at, rx.at + 4 * B * KB * RB)
        R = rd.take("R", [128, T + 1, RB + 1])
        dmin = rd.take("dmin", [128, RB])
        rmin = rd.take("rmin", [128, 3 * RB])
        prod = rd.take("prod", [128, 48], BF16)
        pathT = rp.take("pathT", [T, B, KB, 32], BF16)
        path = rp.take("path", [128, B, CT, S])
        rf = Region(c0)
        hs = rf.take("hs", [128, HT, TOK])
        ln1 = rf.take("ln1", [S, B, D])
        qx = rf.take("qx", [S, B, D], BF16)
        qxT = rf.take("qxT", [128, DH, TOK], BF16)
        sxbc = rf.take("sxbc", [128, TOK])
        hb = rf.take("hb", [128, 2, B, S + 2])
        ct0 = rf.take("ct0", [128, 2, TOK])
        hmax = rf.take("hmax", [128, TOK])
        hmax2 = rf.take("hmax2", [128, TOK])
        s2bc = rf.take("s2bc", [128, TOK])
        q2 = rf.take("q2", [128, HT, TOK], BF16)
        rt = Region(c0)
        re_ = Region(rt.at)
        ln2 = rt.take("ln2", [S, B, D])
        ln2T = rt.take("ln2T", [128, DH, TOK])
        E = re_.take("E", [KC, 6, 4 * S])
        negm = re_.take("negm", [S, 2, 512])
        rt.at = max(rt.at, re_.at)
        qT = rt.take("qT", [128, 4, TOK])
        qm = rt.take("qm", [128, 2, 4, 4, S])
        pvs = rt.take("pvs", [128, 4 * S])
        rs = rt.take("rs", [S, NH])
        o = rt.take("o", [S, NH, HD])
        oT = rt.take("oT", [128, DH, S])
        gated = rt.take("gated", [S, D])
        loads = Region(max(rd.at, rf.at) - 4 * (NIT * D + NOT * DPV + NOT * D + NPT * DPV))
        assert rt.at <= loads.at
        r1 = Region(c0)
        ln3T = r1.take("ln3T", [128, DH, TOK])
        patT = r1.take("patT", [128, DH, NI])
        oiwT = r1.take("oiwT", [128, NO])
        gel = r1.take("gel", [128, 2, 448])
        acts = [r1.take(f"acts{k}", [128, B * n]) for k, n in enumerate((NIT, NPT, NOT))]
        aT = r1.take("aT", [128, 128])
        key = r1.take("key", [128, 128], I32)
        sgn = r1.take("sgn", [128, 128], I32)
        khi = r1.take("khi", [128, 128])
        klo = r1.take("klo", [128, 128])
        kval = r1.take("kval", [128, 128])
        picked = kval
        reach = r1.take("reach", [128, 3, 128], BF16)
        cand = r1.take("cand", [128, 3])
        nextb = r1.take("nextb", [128, 3])
        cnt = r1.take("cnt", [128, 4], BF16)
        ge = r1.take("ge", [128, 4])
        nsel = r1.take("nsel", [128, 1])
        bound = r1.take("bound", [128, 1])
        eq = r1.take("eq", [128, 128])
        gt = r1.take("gt", [128, 128])
        tie = r1.take("tie", [128, 2], BF16)
        need = r1.take("need", [128, 1])
        incl = r1.take("incl", [128, 128])
        sel = r1.take("sel", [128, 128])
        repr32 = r1.take("repr32", [128, NIT, 32])
        pact = r1.take("pact", [128, NP])
        praw = r1.take("praw", [128, B * NPT])
        outr = r1.take("outr", [128, B * NOT])
        esel = r1.take("esel", [128, B * NPT])
        pmx = r1.take("pmx", [128, B])
        pm8 = r1.take("pm8", [B, 1])
        pmd = r1.take("pmd", [B, B])
        agr = r1.take("agr", [128, B])
        agg = r1.take("agg", [128, B])
        fin = r1.take("fin", [B, D])
        assert r1.at <= loads.at, (r1.at - c0, loads.at - c0)
        patn = loads.take("patn", [128, NIT, D])
        oiwn = loads.take("oiwn", [128, NOT, DPV])
        opat = loads.take("opat", [128, NOT, D])
        pval = loads.take("pval", [128, NPT, DPV])
        assert max(rd.at, rf.at, loads.at) <= nc.sbuf_usable_end, (rd.at, rf.at, nc.sbuf_usable_end)

        psmax = [ctx.enter_context(nc.psum_tensor(f"psmax{i}", [128, 2, 512], F32)) for i in range(2)]
        ps = [psmax[i // 2][:, i % 2, :] for i in range(4)]
        ps += [ctx.enter_context(nc.psum_tensor(f"ps{i}", [128, 512], F32))[:, :] for i in range(4, 8)]

        def sem(name):
            return ctx.enter_context(nc.semaphore(name))

        filled = [sem(f"filled{i}") for i in range(8)]
        drained = [sem(f"drained{i}") for i in range(8)]

        def fill(ins, name):
            ins.then_inc(filled[plan[name].banks[0]], 1)

        def drain(ins, name):
            ins.then_inc(drained[plan[name].banks[0]], 1)

        def wait_filled(eng, name):
            g = plan[name]
            eng.wait_ge(filled[g.banks[0]], g.nth)

        def wait_drained(eng, name):
            kind = name if isinstance(name, str) else name[0]
            if kind == "expand":
                eng.wait_ge(x_ready, name[1] + 1)
            elif kind == "ffn_down":
                eng.wait_ge(x_ready, B + name[1] + 1)
            elif kind == "spread":
                eng.wait_ge(x_ready, 3 * B + name[1] + 1)
            elif kind == "pattern":
                eng.wait_ge(gel_ready, 2 * name[1] + name[2] + 1)
            elif kind == "output":
                eng.wait_ge(acts_ready, 3)
            else:
                g = plan[name]
                eng.wait_ge(drained[g.banks[0]], g.nth_drain)

        def claim(eng, name):
            for g in plan[name].before:
                wait_drained(eng, g.name)

        def bank(name):
            return ps[plan[name].banks[0]]

        def bankb(name):
            return ps[plan[name].banks[0]][:, :].bitcast(BF16)

        names = ("x", "ctx0", "ctx1", "ctx2", "ctx3", "again", "attnW", "ffnW", "small", "biasP", "pat", "oiw", "opat", "pval", "piw0", "piw1")
        loaded = {n: sem(f"loaded_{n}") for n in names}
        (consts_ready, onerow_ready, pads_ready, stored, tg_ready, var_ready, sd_ready, ln_ready, bb_ready, aa_ready,
         wabs_ready, winv_ready, tern_ready, ones_v_ready, path_zero, seed_ready, path_done, x_ready, qx_ready, sx_ready, hb_ready,
         ct0_ready, conv_done, silu_done, hmax_ready, s2_ready, q2_ready, hmax_part, negm_ready, qm_ready, praw_ready,
         pv_part, o_ready, cnt_ready, tie_ready, sel_ready, gel_ready, gel_used, acts_ready, pmx_ready, pmd_ready,
         psh_ready, pexp_ready, esel_ready, agg_ready, vec, scl, pol) = [sem(n) for n in (
             "consts_ready onerow_ready pads_ready stored tg_ready var_ready sd_ready ln_ready bb_ready aa_ready "
             "wabs_ready winv_ready tern_ready ones_v_ready path_zero seed_ready path_done x_ready qx_ready sx_ready hb_ready "
             "ct0_ready conv_done silu_done hmax_ready s2_ready q2_ready hmax_part negm_ready qm_ready praw_ready "
             "pv_part o_ready cnt_ready tie_ready sel_ready gel_ready gel_used acts_ready pmx_ready pmd_ready "
             "psh_ready pexp_ready esel_ready agg_ready vec scl pol").split()]

        def counter(eng, s):
            n = [0]

            def did(ins):
                n[0] += 1
                ins.then_inc(s, 1)
                return n[0]

            def settle(upto=None):
                eng.wait_ge(s, n[0] if upto is None else upto)
            return did, settle

        def wait_values(eng, step):
            if step % 4 == 3:
                wait_filled(eng, ("pv", step // 4))
            else:
                eng.wait_ge(pv_part, 3 * (step // 4) + step % 4 + 1)

        def cells(t, n):
            return t[:, 0:B * n].rearrange("p (b n) -> p b n", b=B)

        def hand(ap, dims):
            return bass.AP(ap.tensor, ap.offset, [list(ap.ap[0])] + dims)

        NCTX = (4, 4, 4, 5)
        block = ctx.enter_context(nc.Block())

        @block.sync
        def _(sp):
            sp.dma_start(x[:, :, :], x_in.rearrange("b s d -> s b d")).then_inc(loaded["x"], 16)
            def load_context(dst, sems):
                for kt in range(CT):
                    for g in range(4):
                        row = RB * (4 * kt + g)
                        n = min(32, SC - row)
                        sp.dma_start(dst[32 * g:32 * g + n, kt, :, :],
                                     ctx_in[:, row:row + n, :].rearrange("b r d -> r b d")).then_inc(sems[kt], 16)
                        if n < 32:
                            sp.dma_start(dst[32 * g + n:32 * g + 32, kt, :, :],
                                         ctx_in[:, 0:32 - n, :].rearrange("b r d -> r b d")).then_inc(sems[kt], 16)

            load_context(ctxP, [loaded[f"ctx{kt}"] for kt in range(CT)])
            for i, w in enumerate((wq_in, wk_in, wv_in, wo_in)):
                sp.dma_start(wnat[:, i, :, :], w.rearrange("(c p) d -> p c d", p=128)).then_inc(loaded["attnW"], 16)
            sp.dma_start(w1n[:, :].rearrange("p (c d) -> p c d", c=HT),
                         w1_in.rearrange("(c p) d -> p c d", p=128)).then_inc(loaded["ffnW"], 16)
            sp.dma_start(w2n[:, :].rearrange("p (c d) -> p c d", c=2),
                         w2_in.rearrange("(c p) d -> p c d", p=128)).then_inc(loaded["ffnW"], 16)
            sp.dma_start(cw[:, :, :], conv_w.rearrange("(c p) o k -> p c (o k)", p=128)).then_inc(loaded["small"], 16)
            sp.dma_start(cb[:, :], conv_b.rearrange("(c p) -> p c", p=128),
                         allow_slow_non_contiguous=True).then_inc(loaded["small"], 16)
            sp.dma_start(bvr[0:1, :], bv_in.rearrange("(o d) -> o d", o=1)).then_inc(loaded["small"], 16)
            sp.dma_start(bor[0:1, :], bo_in.rearrange("(o d) -> o d", o=1)).then_inc(loaded["small"], 16)
            for i, g in enumerate((g_xattn, g_ffn)):
                sp.dma_start(gates[:, 2 * i:2 * i + 2],
                             g.rearrange("(o d) -> o d", o=1).broadcast_to([128, 2])).then_inc(loaded["small"], 16)
            sp.wait_ge(pads_ready, 1)
            for dst, src in ((bqP, bq_in), (bkP, bk_in)):
                for g in range(4):
                    sp.dma_start(dst[32 * g:32 * g + HD, :],
                                 src.rearrange("(t g d) -> g d t", t=4, g=4)[g],
                                 allow_slow_non_contiguous=True).then_inc(loaded["biasP"], 16)
            wait_filled(sp, ("kT", 3, B - 1))
            load_context(ctx2, [loaded["again"]] * CT)
            sp.wait_ge(x_ready, 2 * B)
            sp.dma_start(patn[:, :, :], pat_in.rearrange("(c p) d -> p c d", p=128)).then_inc(loaded["pat"], 16)
            sp.dma_start(oiwn[:, :, :], oiw_in.rearrange("(c p) d -> p c d", p=128)).then_inc(loaded["oiw"], 16)
            sp.dma_start(opat[:, :, :], opat_in.rearrange("(c p) d -> p c d", p=128)).then_inc(loaded["opat"], 16)
            sp.dma_start(pval[:, :, :], pval_in.rearrange("(c p) d -> p c d", p=128)).then_inc(loaded["pval"], 16)
            sp.wait_ge(x_ready, 3 * B)
            for i in range(NPT):
                if i >= 2:
                    wait_filled(sp, ("piwT", i - 2, NIT // 4 - 1))
                sp.dma_start(piw[:, i % 2, :], piw_in[128 * i:128 * (i + 1), :]).then_inc(loaded[f"piw{i % 2}"], 16)
            for b in range(B):
                sp.wait_ge(x_ready, 3 * B + b + 1)
                sp.dma_start(out[b], x[:, b, :]).then_inc(stored, 16)
            sp.wait_ge(stored, 16 * B)

        @block.gpsimd
        def _(pool):
            did, settle = counter(pool, pol)
            for t in (ident, identb, skewI, skewB, bqP, bkP):
                did(pool.memset(t[:, :], 0.0))
            for t in (ones, same[0], same[1], gmask):
                did(pool.memset(t[:, :], 1.0))
            for r in range(8):
                for m in range(3):
                    did(pool.memset(steps[:, r, m:m + 1], float((m + 1) * 4 ** (7 - r))))
            did(pool.memset(eps[:, :], 1e-5))
            did(pool.iota(iota_i[:, :], [[0, 1]], base=0, channel_multiplier=1))
            did(pool.iota(iota_t[:, :], [[1, T]], base=0, channel_multiplier=0,
                          allow_small_or_imprecise_dtypes=True))
            settle()
            for t in (ident, identb):
                did(pool.affine_select(out=t[:, :], in_=t[:, :], compare_op=ALU.not_equal, fill=1.0, base=0,
                                       pattern=[[-1, 128]], channel_multiplier=1))
            for t in (skewI, skewB):
                did(pool.affine_select(out=t[:, :], in_=t[:, :], compare_op=ALU.not_equal, fill=1.0, base=KB - 1,
                                       pattern=[[-1, T + KB - 1]], channel_multiplier=1))
            for t, n in list(zip(same, (NIT, NPT))) + [(gmask, 32)]:
                j = 1 if t is gmask else n
                v = t[:, :].rearrange("p (g j) -> p g j", j=j)
                g = v.shape[1]
                did(pool.affine_select(out=v, in_=v, compare_op=ALU.is_ge, fill=0.0, base=0,
                                       pattern=[[-n, g], [0, j]], channel_multiplier=1))
                settle()
                did(pool.affine_select(out=v, in_=v, compare_op=ALU.is_ge, fill=0.0, base=n - 1,
                                       pattern=[[n, g], [0, j]], channel_multiplier=-1))
            settle()
            for a, u in zip(same, under):
                did(pool.affine_select(out=u[:, :], in_=a[:, :], compare_op=ALU.is_gt, fill=0.0, base=0,
                                       pattern=[[1, a.shape[1]]], channel_multiplier=-1))
            settle()
            pool.memset(wqP[:, :, :], 0.0).then_inc(consts_ready, 1)
            pool.memset(wkP[:, :, :], 0.0).then_inc(consts_ready, 1)
            pool.wait_ge(onerow_ready, 1)
            pool.tensor_scalar(bkP[:, :], bkP[:, :], onerow[:, 0:1], None, ALU.add).then_inc(pads_ready, 1)
            pool.wait_ge(winv_ready, 1)
            for i, w in enumerate((w1n, w2n)):
                did(pool.tensor_scalar(w[:, :], w[:, :], winv[:, i:i + 1], MAGIC, ALU.mult, ALU.add))
                settle()
                did(pool.tensor_scalar(w[:, :], w[:, :], -MAGIC, 1.0, ALU.add, ALU.mult))
                settle()
                pool.tensor_scalar(tern[i][:, :], w[:, :], 1.0, -1.0, ALU.min, ALU.max).then_inc(tern_ready, 1)
            wait_drained(pool, ("attnWT", 3))
            wait_filled(pool, ("dist", B - 1))
            pool.memset(v1[:, :, :, :], 1.0).then_inc(ones_v_ready, 1)
            for t in range(4):
                for half in range(2):
                    wait_drained(pool, ("qT", t, half))
            for b in range(B):
                if b >= 2:
                    wait_filled(pool, ("scoreT", b - 2, 3, KCH - 1))
                for g in range(4):
                    pool.tensor_scalar(qm[:, b % 2, :, g, :], qT[:, :, S * b:S * b + S], gmask[:, g:g + 1], 1.0,
                                       ALU.mult, ALU.mult).then_inc(qm_ready, 1)

        @block.vector
        def _(dve):
            did, settle = counter(dve, vec)
            tt, ts, stt = dve.tensor_tensor, dve.tensor_scalar, dve.scalar_tensor_tensor

            def layernorm(n, src, dst):
                for b in range(B):
                    if n:
                        dve.wait_ge(x_ready, (n - 1) * B + b + 1)
                    did(dve.bn_stats(bn6[:, b, :], src[:, b, :]))
                settle()
                for b in range(B):
                    last = dve.bn_aggr(mv[:, b, :], bn6[:, b, :])
                    if b < B - 1:
                        did(last)
                last.then_inc(var_ready, 1)
                dve.wait_ge(sd_ready, n + 1)
                did(dve.reciprocal(rstd[:, :], sd[:, :]))
                settle()
                for b in range(B):
                    ts(dst[:, b, :], src[:, b, :], mv[:, b, 0:1], rstd[:, b:b + 1],
                       ALU.subtract, ALU.mult).then_inc(ln_ready, 1)

            dve.wait_ge(loaded["x"], 16)
            layernorm(0, x, ln0)

            dve.wait_ge(consts_ready, 1)
            did(dve.tensor_single_scalar(blk_i[:, :], iota_i[:, :], 15, ALU.bitwise_and))
            did(dve.tensor_single_scalar(lane_i[:, :], iota_i[:, :], 31, ALU.bitwise_and))
            settle()
            did(dve.tensor_copy(blk[:, :], blk_i[:, :]))
            did(dve.tensor_copy(lane[:, :], lane_i[:, :]))
            settle()
            ts(onerow[:, :], lane[:, :], float(HD), None, ALU.is_equal).then_inc(onerow_ready, 1)
            did(ts(first_up[:, :], blk[:, :], 0.5, BIG, ALU.is_gt, ALU.mult))
            did(ts(last_big[:, :], blk[:, :], float(KB - 1), BIG, ALU.is_equal, ALU.mult))
            did(ts(wavepad[:, :], iota_t[:, :], blk[:, 0:1], BIG, ALU.is_lt, ALU.mult))
            did(dve.memset(seed[:, :], 0.0))
            settle()
            qs = RB - 1 - (SC - 1) % RB
            did(ts(seed[:, 2 * qs:2 * qs + 1], blk[:, :], float(KB - 1), None, ALU.is_equal))

            for b in range(B):
                for h in range(DH):
                    nm = ("ctxT", b, h)
                    wait_filled(dve, nm)
                    drain(dve.tensor_copy(
                        ctxT[:, h, b, :].rearrange("p (k r) -> p k r", r=RB),
                        bank(nm)[:, :].rearrange("p (k r) -> p k r", r=32)[:, :, 0:RB]), nm)
            dve.wait_ge(bb_ready, 1)
            for b in range(B):
                nm = ("dist", b)
                wait_filled(dve, nm)
                drain(ts(dist[:, b, :, :].rearrange("p k r -> p (k r)"), bank(nm)[0:S, 0:KB * RB],
                         bb[:, b:b + 1], 0.0, ALU.add, ALU.max), nm)

            for m in range(RB // 4):
                nm = ("dwave", m)
                wait_filled(dve, nm)
                drain(tt(dwave[:, :, 4 * m:4 * m + 4].rearrange("p t r -> p r t"),
                         bank(nm)[:, 0:4 * T].rearrange("p (r t) -> p r t", r=4),
                         wavepad[:, :].unsqueeze(1).broadcast_to([128, 4, T]), ALU.add), nm)
            wait_drained(dve, ("dwave", RB // 4 - 1))
            did(ts(dwave[:, :, RB - 1], dwave[:, :, RB - 1], last_big[:, 0:1], None, ALU.add))
            did(dve.memset(R[:, 0, :], BIG))
            did(dve.memset(R[:, 1, 0:1], BIG))
            for b in range(B):
                wait_filled(dve, ("ctxT", b, DH - 1))
            wait_filled(dve, "aaT")
            did(dve.memset(hand(UU[:, :, 1:2], [[50, T], [2, RB]]), 1.0))
            settle()

            above = [p - 1 if p % KB else p + KB - 1 for p in range(32)]

            def choices():
                last = 2 * (RB - 1)
                for t0 in range(0, T, 3):
                    n = min(3, T - t0)
                    cd, cl, cu = R[:, t0:t0 + n, 0:RB], R[:, t0:t0 + n, 1:RB + 1], R[:, t0 + 1:t0 + n + 1, 0:RB]
                    G = hand(LG[:, t0, last + 2:last + 3], [[50, n], [-2, RB]])
                    L = hand(LG[:, t0, last + 1:last + 2], [[50, n], [-2, RB]])
                    U = hand(UU[:, t0, last + 2:last + 3], [[50, n], [-2, RB]])
                    m = rmin[:, 0:n * RB].rearrange("p (t r) -> p t r", r=RB)
                    yield t0 + n, lambda m=m, cu=cu, cl=cl: tt(m, cu, cl, ALU.min)
                    yield t0 + n, lambda U=U, cu=cu, cl=cl: tt(U, cu, cl, ALU.is_le)
                    yield t0 + n, lambda G=G, m=m, cd=cd: tt(G, m, cd, ALU.is_ge)
                    yield t0 + n, lambda U=U, G=G: tt(U, U, G, ALU.is_gt)
                    yield t0 + n, lambda L=L, U=U, G=G: tt(L, U, G, ALU.is_equal)

            todo = list(choices())
            at = [0, None]

            def choose(complete):
                if at[0] < len(todo) and todo[at[0]][0] <= complete:
                    if at[1] is not None:
                        settle(at[1])
                    at[1] = did(todo[at[0]][1]())
                    at[0] += 1

            for t in range(T):
                inner = did(tt(dmin[:, :], R[:, t, 0:RB], R[:, t, 1:RB + 1], ALU.min))
                if t:
                    inner = did(dve.stream_shuffle(R[:, t + 1, 0:1], R[:, t, RB:RB + 1], above))
                choose(t - 1)
                settle(inner)
                scan = did(dve.tensor_tensor_scan(R[:, t + 1, 1:RB + 1], dmin[:, :], dwave[:, t, :],
                                                  first_up[:, 0:1] if t == 0 else R[:, t + 1, 0:1],
                                                  ALU.min, ALU.add))
                choose(t - 1)
                settle(scan)
                if t == 40:
                    wait_filled(dve, "wsum")
                    drain(ts(wmean[:, :], bank("wsum")[:, 0:2], 1.0 / (HID * D), 1e-5, ALU.mult, ALU.max), "wsum")
                    wait_drained(dve, "wsum")
                    dve.reciprocal(winv[:, :], wmean[:, :]).then_inc(winv_ready, 1)
            while at[0] < len(todo):
                choose(T)
            below_lane = [p + 1 if p % KB < KB - 1 else p - KB + 1 for p in range(32)]
            settle()
            did(dve.memset(LG[:, T - 1, 0:1], 0.0))
            did(dve.memset(UU[:, T - 1, 0:1], 0.0))
            did(dve.memset(PR[:, T, :], 0.0))
            did(dve.memset(PR[:, T - 1, 1:2], 0.0))
            did(dve.stream_shuffle(LG[:, 0:T - 1, 0], LG[:, 1:T, 2 * RB], below_lane))
            did(dve.stream_shuffle(UU[:, 0:T - 1, 0], UU[:, 1:T, 2 * RB], below_lane))
            settle()
            for t in range(T - 1, -1, -1):
                if t < T - 1:
                    inner = did(tt(prod[:, :].rearrange("p (q e) -> p q e", e=2),
                                   hand(PR[:, t + 1, 1:2], [[2, RB], [2, 2]]),
                                   LG[:, t + 1, 0:48].rearrange("p (q e) -> p q e", e=2), ALU.mult))
                    inner = did(dve.stream_shuffle(PR[:, t, 1:2], PR[:, t + 1, 49:50], below_lane))
                    settle(inner)
                scan = dve.tensor_tensor_scan(PR[:, t, 2:50], UU[:, t, 0:48], seed[:, :] if t == T - 1 else prod[:, :],
                                              PR[:, t, 1:2], ALU.mult, ALU.add)
                if t:
                    did(scan)
                    settle()
                else:
                    scan.then_inc(path_done, 1)
            dve.memset(pathT[:, :, :, RB:32], 0.0).then_inc(path_zero, 1)
            for m in range(3):
                nm = ("pathT", m)
                wait_filled(dve, nm)
                dst = hand(pathT[:, 0, 0, RB - 1 - 8 * m:RB - 8 * m], [[-1, 8], [32, B * KB]])
                drain(dve.tensor_copy(dst, bankb(nm)[0:T, :].rearrange("p (r l) -> p r l", r=8)), nm)
            dve.wait_ge(tg_ready, 1)
            for b in range(B):
                nm = ("expand", b)
                wait_filled(dve, nm)
                stt(x[:, b, :], bank(nm)[0:S, 0:D], tg[0:S, 0:1], x[:, b, :], ALU.mult, ALU.add).then_inc(x_ready, 1)

            layernorm(1, x, ln1)
            dve.wait_ge(ln_ready, 2 * B)
            did(dve.tensor_reduce(am[:, :], ln1[:, :, :], AX.X, ALU.max, apply_absolute_value=True))
            settle()
            did(ts(am[:, :], am[:, :], 1e-5, None, ALU.max))
            settle()
            did(dve.reciprocal(ari[:, :], am[:, :]))
            settle()
            did(ts(asc[:, :], ari[:, :], 127.0, None, ALU.mult))
            ts(sx[:, :], am[:, :], 1.0 / 127.0, None, ALU.mult).then_inc(sx_ready, 1)
            settle()
            for b in range(B):
                did(ts(ln1[:, b, :], ln1[:, b, :], asc[:, b:b + 1], MAGIC, ALU.mult, ALU.add))
            settle()
            for b in range(B):
                ts(qx[:, b, :], ln1[:, b, :], MAGIC, None, ALU.subtract).then_inc(qx_ready, 1)
            dve.wait_ge(loaded["small"], 96)
            did(ts(cws[:, :, :], cw[:, :, :], wmean[:, 0:1], None, ALU.mult))
            did(dve.memset(hb[:, :, :, 0:1], 0.0))
            did(dve.memset(hb[:, :, :, S + 1:S + 2], 0.0))
            for half in range(2):
                nm = ("sxbc", half)
                wait_filled(dve, nm)
                drain(dve.tensor_copy(sxbc[:, 448 * half:448 * half + 448], bank(nm)[:, 0:448]), nm)
            settle()
            wait_drained(dve, ("sxbc", 1))
            wait_drained(dve, ("sxbc", 0))
            for c in range(HT + 2):
                if c < HT:
                    for half in range(2):
                        nm = ("ffn_up", c, half)
                        wait_filled(dve, nm)
                        if c >= 2:
                            dve.wait_ge(ct0_ready, c - 1)
                            dve.wait_ge(conv_done, c - 1)
                        drain(tt(hb[:, c % 2, 4 * half:4 * half + 4, 1:S + 1],
                                 bank(nm)[:, 0:448].rearrange("p (b s) -> p b s", b=4),
                                 sxbc[:, 448 * half:448 * half + 448].rearrange("p (b s) -> p b s", b=4),
                                 ALU.mult), nm)
                if 1 <= c <= HT:
                    e = c - 1
                    acc = ct0[:, e % 2, :].rearrange("p (b s) -> p b s", b=B)
                    dve.wait_ge(ct0_ready, e + 1)
                    did(stt(acc, hb[:, e % 2, :, 0:S], cws[:, e, 0:1], acc, ALU.mult, ALU.add))
                    settle()
                    stt(acc, hb[:, e % 2, :, 2:S + 2], cws[:, e, 2:3], acc, ALU.mult, ALU.add).then_inc(conv_done, 1)
                if c >= 2 and c % 2:
                    e = c - 3
                    dve.wait_ge(silu_done, e + 2)
                    pair = hs[:, e:e + 2, :].rearrange("p c t -> p t c")
                    if e == 0:
                        ins = dve.tensor_reduce(hmax[:, :], pair, AX.X, ALU.max, apply_absolute_value=True)
                    else:
                        did(dve.tensor_reduce(hmax2[:, :], pair, AX.X, ALU.max, apply_absolute_value=True))
                        settle()
                        dve.wait_ge(hmax_part, e // 2)
                        ins = tt(hmax[:, :], hmax[:, :], hmax2[:, :], ALU.max)
                    ins.then_inc(hmax_part, 1)
            for half in range(2):
                nm = ("hmaxT", half)
                wait_filled(dve, nm)
                drain(dve.tensor_reduce(am[:, 4 * half:4 * half + 4],
                                        bank(nm)[0:S, :].rearrange("p (b c) -> p b c", b=4), AX.X, ALU.max), nm)
            wait_drained(dve, ("hmaxT", 0))
            wait_drained(dve, ("hmaxT", 1))
            did(ts(am[:, :], am[:, :], 1e-5, None, ALU.max))
            settle()
            did(dve.reciprocal(ari[:, :], am[:, :]))
            settle()
            ts(asc[:, :], ari[:, :], 127.0, None, ALU.mult).then_inc(s2_ready, 1)
            did(ts(sx[:, :], am[:, :], 1.0 / 127.0, wmean[0:S, 1:2], ALU.mult, ALU.mult))
            settle()
            did(ts(sx[:, :], sx[:, :], tg[0:S, 2:3], None, ALU.mult))
            for half in range(2):
                nm = ("s2bc", half)
                wait_filled(dve, nm)
                drain(dve.tensor_copy(s2bc[:, 448 * half:448 * half + 448], bank(nm)[:, 0:448]), nm)
            wait_drained(dve, ("s2bc", 0))
            wait_drained(dve, ("s2bc", 1))
            for c in range(HT):
                did(tt(hs[:, c, :], hs[:, c, :], s2bc[:, :], ALU.mult))
                if c:
                    ts(q2[:, c - 1, :], hs[:, c - 1, :], MAGIC, MAGIC, ALU.add, ALU.subtract).then_inc(q2_ready, 1)
                settle()
            ts(q2[:, HT - 1, :], hs[:, HT - 1, :], MAGIC, MAGIC, ALU.add, ALU.subtract).then_inc(q2_ready, 1)
            for b in range(B):
                nm = ("ffn_down", b)
                wait_filled(dve, nm)
                stt(x[:, b, :], bank(nm)[0:S, 0:D], sx[:, b:b + 1], x[:, b, :], ALU.mult, ALU.add).then_inc(x_ready, 1)

            layernorm(2, x, ln2)
            for t in range(4):
                for half in range(2):
                    wait_filled(dve, ("qT", t, half))
            did(dve.memset(negm[:, :, :], 0.0))
            settle()
            for b in range(-1, B + 1):
                for t in range(4):
                    if b + 1 < B:
                        if b + 1 >= 2 and t == 0:
                            wait_filled(dve, ("negmT", b - 1))
                        for u in range(2):
                            nm = ("smax", b + 1, t, u)
                            wait_filled(dve, nm)
                            c0_ = 128 * t + 64 * u + HD
                            drain(dve.tensor_reduce(negm[:, (b + 1) % 2, c0_:c0_ + 33:32],
                                                    psmax[u][0:S, :, 0:SC], AX.X, ALU.max, negate=True), nm)
                    if b >= 1 and t == 1:
                        nm = ("pvT", b - 1)
                        wait_filled(dve, nm)
                        pvt = bank(nm)[0:S, :].rearrange("p (h e) -> p h e", e=32)
                        did(dve.reciprocal(rs[:, :], pvt[:, :, HD]))
                        settle()
                        drain(tt(o[:, :, :], pvt[:, :, 0:HD], rs[:, :].unsqueeze(2).broadcast_to([S, NH, HD]),
                                 ALU.mult), nm)
                    if b >= 1 and t == 3:
                        nm = ("wo", b - 1)
                        wait_filled(dve, nm)
                        drain(stt(x[:, b - 1, :], bank(nm)[0:S, 0:D], tg[0:S, 1:2], x[:, b - 1, :],
                                  ALU.mult, ALU.add), nm)
                        wait_drained(dve, nm)
                        dve.nop().then_inc(x_ready, 1)
                if b + 1 < B:
                    nm = ("negmT", b + 1)
                    wait_filled(dve, nm)
                    for g in range(4):
                        q = qm[:, (b + 1) % 2, :, g, :]
                        ins = stt(q, bank(nm)[:, 0:4 * S].rearrange("p (t s) -> p t s", t=4), gmask[:, g:g + 1], q,
                                  ALU.mult, ALU.add)
                        if g == 3:
                            drain(ins, nm)
                        else:
                            did(ins)

            layernorm(3, x, ln3)
            a0 = cells(acts[0], NIT)
            for i in range(NIT):
                for half in range(2):
                    dve.wait_ge(gel_ready, 2 * i + half + 1)
                    dve.tensor_reduce(a0[:, 4 * half:4 * half + 4, i],
                                      gel[:, half, :].rearrange("p (b s) -> p b s", b=4),
                                      AX.X, ALU.add).then_inc(gel_used, 1)
            dve.wait_ge(gel_used, 2 * NIT)
            ts(acts[0][:, :], acts[0][:, :], 1.0 / S, 0.0, ALU.mult, ALU.add).then_inc(acts_ready, 1)

            def largest(k, lanes, keep):
                nm = ("actT", k)
                wait_filled(dve, nm)
                drain(dve.tensor_copy(aT[0:lanes, :], bank(nm)[0:lanes, 0:128]), nm)
                wait_drained(dve, nm)
                bits = aT[0:lanes, :].bitcast(I32)
                v = {"key": key, "sgn": sgn, "low": eq, "khi": khi, "klo": klo, "kval": kval, "cand": cand,
                     "nextb": nextb, "nsel": nsel, "bound": bound, "eq": eq, "gt": gt, "need": need,
                     "incl": incl, "sel": sel}
                v = {n: t[0:lanes, :] for n, t in v.items()}
                v["low"] = v["low"].bitcast(I32)
                did(ts(v["sgn"], bits, 31, 0x7FFFFFFF, ALU.arith_shift_right, ALU.bitwise_and))
                settle()
                did(tt(v["key"], v["sgn"], bits, ALU.bitwise_xor))
                settle()
                did(dve.tensor_single_scalar(v["sgn"], v["key"], 16, ALU.arith_shift_right))
                did(dve.tensor_single_scalar(v["low"], v["key"], 0xFFFF, ALU.bitwise_and))
                settle()
                did(dve.tensor_copy(v["khi"], v["sgn"]))
                did(dve.tensor_copy(v["klo"], v["low"]))
                did(dve.memset(v["bound"], -32768.0))
                did(ts(v["cand"], steps[0:lanes, 0, :], -32768.0, None, ALU.add))
                settle()
                val = v["khi"]
                for r in range(16):
                    if r == 8:
                        did(ts(v["kval"], v["khi"], v["bound"], 65536.0, ALU.subtract, ALU.mult))
                        settle()
                        val = v["kval"]
                        did(tt(val, val, v["klo"], ALU.add))
                        did(dve.memset(v["bound"], 0.0))
                        did(dve.tensor_copy(v["cand"], steps[0:lanes, 0, :]))
                        settle()
                    with nc.allow_low_precision(reason="counts up to 128 are exact"):
                        for m in range(3):
                            ins = ts(reach[0:lanes, m, :], val, cand[0:lanes, m:m + 1], None, ALU.is_ge, ALU.add,
                                     accum_out=cnt[0:lanes, m:m + 1])
                            if m < 2:
                                did(ins)
                    ins.then_inc(cnt_ready, 1)
                    last = r % 8 == 7
                    if not last:
                        settle()
                        did(ts(v["nextb"], steps[0:lanes, r % 8 + 1, :], v["bound"], None, ALU.add))
                    nm = ("count", k, r)
                    wait_filled(dve, nm)
                    drain(ts(ge[0:lanes, 0:3], bank(nm)[0:lanes, 0:3], keep - 0.5, None, ALU.is_gt, ALU.add,
                             accum_out=v["nsel"]), nm)
                    settle()
                    wait_drained(dve, nm)
                    step = float(4 ** (7 - r % 8))
                    if not last:
                        c = did(stt(v["cand"], v["nsel"].broadcast_to([lanes, 3]), step, v["nextb"], ALU.mult, ALU.add))
                    did(stt(v["bound"], v["nsel"], step, v["bound"], ALU.mult, ALU.add))
                    settle(None if last else c)
                settle()
                with nc.allow_low_precision(reason="counts up to 128 are exact"):
                    did(ts(v["gt"], val, v["bound"], None, ALU.is_gt, ALU.add, accum_out=tie[0:lanes, 0:1]))
                    ts(v["eq"], val, v["bound"], None, ALU.is_equal, ALU.add,
                       accum_out=tie[0:lanes, 1:2]).then_inc(tie_ready, 1)
                dve.wait_ge(tie_ready, k + 1)
                did(dve.tensor_tensor_scan(v["incl"], ones[0:lanes, :], v["eq"], 0.0, ALU.mult, ALU.add))
                nm = ("ties", k)
                wait_filled(dve, nm)
                drain(ts(v["need"], bank(nm)[0:lanes, 0:1], -1.0, keep + 0.5, ALU.mult, ALU.add), nm)
                settle()
                wait_drained(dve, nm)
                did(stt(v["incl"], v["incl"], v["need"], v["eq"], ALU.is_lt, ALU.mult))
                settle()
                if k == 1:
                    tt(v["sel"], v["incl"], v["gt"], ALU.add).then_inc(sel_ready, 1)
                else:
                    did(tt(v["sel"], v["incl"], v["gt"], ALU.add))
                    settle()
                    tt(picked[0:lanes, :], v["sel"], aT[0:lanes, :], ALU.mult).then_inc(sel_ready, 1)

            did(dve.memset(repr32[:, :, :], 0.0))
            largest(0, B * NIT, NI // 8)
            nm = ("selT", 0)
            wait_filled(dve, nm)
            drain(dve.tensor_copy(repr32[:, :, 0:B], bank(nm)[:, 0:B * NIT].rearrange("p (b n) -> p n b", b=B)), nm)
            for h in range(2):
                nm = ("processT", h)
                wait_filled(dve, nm)
                ins = dve.tensor_reduce(cells(praw, NPT)[:, :, 4 * h:4 * h + 4].rearrange("p b n -> p n b"),
                                        bank(nm)[:, :].rearrange("p (n g e) -> p n e g", n=4, g=4)[:, :, 0:B, :],
                                        AX.X, ALU.add)
                drain(ins, nm)
            dve.wait_ge(acts_ready, 2)
            dve.tensor_reduce(pmx[:, :], cells(acts[1], NPT), AX.X, ALU.max).then_inc(pmx_ready, 1)
            wait_filled(dve, "pmaxT")
            drain(dve.tensor_reduce(pm8[:, :], bank("pmaxT")[0:B, 0:128], AX.X, ALU.max), "pmaxT")
            wait_drained(dve, "pmaxT")
            ts(pmd[:, :], ident[0:B, 0:B], pm8[:, 0:1], None, ALU.mult).then_inc(pmd_ready, 1)
            wait_filled(dve, "pmaxb")
            drain(tt(cells(esel, NPT), cells(acts[1], NPT),
                     bank("pmaxb")[:, 0:B].unsqueeze(2).broadcast_to([128, B, NPT]), ALU.subtract), "pmaxb")
            largest(1, B * NPT, NP // 8)
            nm = ("selT", 1)
            wait_filled(dve, nm)
            dve.wait_ge(pexp_ready, 1)
            drain(tt(esel[:, :], esel[:, :], bank(nm)[:, 0:B * NPT], ALU.mult), nm)
            wait_filled(dve, "aggr")
            did(dve.reciprocal(agr[:, :], bank("aggr")[:, B:2 * B]))
            settle()
            drain(tt(agg[:, :], bank("aggr")[:, 0:B], agr[:, :], ALU.mult), "aggr")
            largest(2, B * NOT, NO // 8)
            nm = ("selT", 2)
            wait_filled(dve, nm)
            drain(dve.tensor_copy(outr[:, :], bank(nm)[:, 0:B * NOT]), nm)
            wait_filled(dve, "final")
            drain(dve.tensor_copy(fin[:, :], bank("final")[0:B, 0:D]), "final")
            for b in range(B):
                nm = ("spread", b)
                wait_filled(dve, nm)
                stt(x[:, b, :], bank(nm)[0:S, 0:D], tg[0:S, 3:4], x[:, b, :], ALU.mult, ALU.add).then_inc(x_ready, 1)

        @block.scalar
        def _(act):
            did, settle = counter(act, scl)
            fn = act.activation

            def root(n):
                act.wait_ge(var_ready, n + 1)
                fn(sd[:, :], mv[:, :, 1], ACT.Sqrt, bias=eps[0:S, 0:1]).then_inc(sd_ready, 1)

            act.wait_ge(consts_ready, 1)
            root(0)
            for b in range(B):
                act.wait_ge(ln_ready, b + 1)
                settle()
                ins = fn(actscr[0:S, 0:D], ln0[:, b, :], ACT.Square, accum_out=bb[:, b:b + 1])
                if b == B - 1:
                    ins.then_inc(bb_ready, 1)
                else:
                    did(ins)
            for h in range(DH):
                for half in range(2):
                    nm = ("lnT0", h, half)
                    wait_filled(act, nm)
                    drain(fn(ln0T[:, h, 448 * half:448 * half + 448], bank(nm)[:, 0:448], ACT.Copy, scale=-2.0), nm)
            for kt in range(CT):
                act.wait_ge(loaded[f"ctx{kt}"], 16 * NCTX[kt])
                for b in range(B):
                    i = B * kt + b
                    settle()
                    if i == 0:
                        act.wait_ge(bb_ready, 1)
                    ins = fn(actscr[:, 0:D], ctxP[:, kt, b, :], ACT.Square, accum_out=aa[:, i:i + 1])
                    if i == CT * B - 1:
                        ins.then_inc(aa_ready, 1)
                    else:
                        did(ins)
            wait_filled(act, "aaT")
            drain(fn(aaT[:, :], bank("aaT")[0:CT * B, 0:128], ACT.Copy), "aaT")
            for m in range(KB // 2):
                nm = ("skew", m)
                wait_filled(act, nm)
                drain(fn(skewed[:, :, 2 * m:2 * m + 2, :].rearrange("p b k r -> p k b r"),
                         bank(nm)[0:T, 0:2 * B * RB].rearrange("p (k b r) -> p k b r", k=2, b=B), ACT.Sqrt), nm)
            for i, dst in enumerate((wqP, wkP, wvT, woT)):
                nm = ("attnWT", i)
                wait_filled(act, nm)
                if i < 2:
                    act.wait_ge(consts_ready, 2)
                    drain(fn(dst[:, :, :].rearrange("p h (g e) -> p h g e", e=32)[:, :, :, 0:HD],
                             bank(nm)[:, :].rearrange("p (h g e) -> p h g e", h=DH, e=HD), ACT.Copy), nm)
                else:
                    drain(fn(dst[:, :, :].rearrange("p h d -> p (h d)"), bank(nm)[:, :], ACT.Copy), nm)
            act.wait_ge(loaded["ffnW"], 32)
            did(fn(tern[0][:, :], w1n[:, :], ACT.Abs, accum_out=wabs[:, 0:1]))
            fn(tern[1][:, :], w2n[:, :], ACT.Abs, accum_out=wabs[:, 1:2]).then_inc(wabs_ready, 1)
            act.wait_ge(loaded["small"], 96)
            fn(tg[:, :], gates[:, :], ACT.Tanh).then_inc(tg_ready, 1)
            act.wait_ge(ones_v_ready, 1)
            for b in range(B):
                for c in range(KCH):
                    nm = ("V", b, c)
                    wait_filled(act, nm)
                    drain(fn(v1[:, c, b, 0:NH * (HD + 1)].rearrange("p (h e) -> p h e", e=HD + 1)[:, :, 0:HD],
                             bank(nm)[0:KC, 0:D].rearrange("p (h e) -> p h e", e=HD), ACT.Copy), nm)
            for w in range(2):
                for h in range(2):
                    nm = ("ternT", w, h)
                    wait_filled(act, nm)
                    if w == 0:
                        drain(fn(w1T[:, h, :], bankb(nm), ACT.Copy), nm)
                    else:
                        drain(fn(w2T[:, 4 * h:4 * h + 4, :].rearrange("p c d -> p (c d)"), bankb(nm), ACT.Copy), nm)
            act.wait_ge(loaded["biasP"], 128)
            for t in range(4):
                for b in range(B):
                    nm = ("kT", t, b)
                    wait_filled(act, nm)
                    drain(fn(kT[:, t, b, :], bank(nm)[:, 0:SC], ACT.Identity, bias=bkP[:, t:t + 1]), nm)
            fn(bqs[:, :], bqP[:, :], ACT.Copy, scale=HD ** -0.5).then_inc(scl, 1)
            for b in range(B):
                nm = ("path", b)
                wait_filled(act, nm)
                drain(fn(path[:, b, :, :].rearrange("p c s -> p (c s)"), bank(nm)[:, 0:4 * S], ACT.Copy), nm)
            root(1)
            for h in range(DH):
                nm = ("qxT", h)
                wait_filled(act, nm)
                drain(fn(qxT[:, h, :], bankb(nm)[:, 0:TOK], ACT.Copy), nm)
            for c in range(HT + 1):
                if c < HT:
                    wait_drained(act, ("ffn_up", c, 1))
                    wait_drained(act, ("ffn_up", c, 0))
                    if c >= 2:
                        act.wait_ge(silu_done, c - 1)
                    fn(ct0[:, c % 2, :].rearrange("p (b s) -> p b s", b=B), hb[:, c % 2, :, 1:S + 1], ACT.Identity,
                       bias=cb[:, c:c + 1], scale=cws[:, c, 1:2]).then_inc(ct0_ready, 1)
                if c >= 1:
                    act.wait_ge(conv_done, c)
                    fn(hs[:, c - 1, :], ct0[:, (c - 1) % 2, :], ACT.Silu).then_inc(silu_done, 1)
            root(2)
            for h in range(DH):
                for half in range(2):
                    nm = ("lnT2", h, half)
                    wait_filled(act, nm)
                    drain(fn(ln2T[:, h, 448 * half:448 * half + 448], bank(nm)[:, 0:448], ACT.Copy), nm)
            for t in range(4):
                for half in range(2):
                    nm = ("qT", t, half)
                    wait_filled(act, nm)
                    drain(fn(qT[:, t, 448 * half:448 * half + 448], bank(nm)[:, 0:448], ACT.Identity,
                             bias=bqs[:, t:t + 1], scale=HD ** -0.5), nm)
            for b in range(B + 1):
                for t in range(4):
                    if b < B:
                        step = 4 * b + t
                        if step >= 2:
                            wait_values(act, step - 2)
                        for c in range(KCH):
                            nm = ("scoreT", b, t, c)
                            wait_filled(act, nm)
                            drain(fn(E[:, (KCH * step + c) % 6, :], bank(nm)[0:KC, 0:4 * S], ACT.Exp), nm)
                    if b >= 1 and t == 0:
                        nm = ("pv", b - 1)
                        wait_filled(act, nm)
                        drain(fn(pvs[:, :], bank(nm)[:, 0:4 * S], ACT.Copy), nm)
                    if b >= 1 and t == 2:
                        nm = ("oT", b - 1)
                        wait_filled(act, nm)
                        drain(fn(oT[:, :, :].rearrange("p h s -> p (h s)"), bank(nm)[:, 0:DH * S], ACT.Copy), nm)
            root(3)
            for h in range(DH):
                for half in range(2):
                    nm = ("lnT3", h, half)
                    wait_filled(act, nm)
                    drain(fn(ln3T[:, h, 448 * half:448 * half + 448], bank(nm)[:, 0:448], ACT.Copy), nm)
            for m in range(NIT // 2):
                nm = ("patT", m)
                wait_filled(act, nm)
                drain(fn(patT[:, :, 256 * m:256 * m + 256], bank(nm)[:, :].rearrange("p (h n) -> p h n", h=DH),
                         ACT.Copy), nm)
            for i in range(NIT):
                for half in range(2):
                    nm = ("pattern", i, half)
                    wait_filled(act, nm)
                    if i >= 1:
                        act.wait_ge(gel_used, 2 * (i - 1) + half + 1)
                    fn(gel[:, half, :], bank(nm)[:, 0:448], ACT.Gelu).then_inc(gel_ready, 1)
            for m in range(NOT // 4):
                nm = ("oiwT", m)
                wait_filled(act, nm)
                drain(fn(oiwT[:, 512 * m:512 * m + 512], bank(nm)[:, :], ACT.Copy), nm)
            for i in range(NPT):
                for m in range(NIT // 4):
                    nm = ("piwT", i, m)
                    wait_filled(act, nm)
                    drain(fn(piwT[:, 4 * m:4 * m + 4, 128 * i:128 * i + 128],
                             bank(nm)[:, :].rearrange("p (c n) -> p c n", c=4), ACT.Copy), nm)
            for h in range(2):
                nm = ("process", h)
                wait_filled(act, nm)
                drain(fn(pact[:, 512 * h:512 * h + 512], bank(nm)[:, :], ACT.Copy), nm)
            for h in range(2):
                wait_drained(act, ("processT", h))
            fn(acts[1][:, :], praw[:, :], ACT.Gelu).then_inc(acts_ready, 1)
            wait_drained(act, "pmaxb")
            fn(esel[:, :], esel[:, :], ACT.Exp).then_inc(pexp_ready, 1)
            wait_filled(act, "output")
            fn(cells(acts[2], NOT), bank("output")[:, 0:B * NOT].rearrange("p (n b) -> p b n", b=B),
               ACT.Gelu).then_inc(acts_ready, 1)

        @block.tensor
        def _(pe):
            mm, tr = pe.matmul, pe.transpose

            def ln_transposes(n, name, src, dt_ident):
                for h in range(DH):
                    for half in range(2):
                        nm = (name, h, half)
                        claim(pe, nm)
                        for i in range(4):
                            b = 4 * half + i
                            pe.wait_ge(ln_ready, n * B + b + 1)
                            ins = tr(bank(nm)[:, S * i:S * i + S], src[:, b, 128 * h:128 * h + 128],
                                     ident[0:S, 0:S])
                        fill(ins, nm)

            pe.wait_ge(consts_ready, 1)
            ln_transposes(0, "lnT0", ln0, ident)
            for kt in range(CT):
                pe.wait_ge(loaded[f"ctx{kt}"], 16 * NCTX[kt])
            for b in range(B):
                for h in range(DH):
                    nm = ("ctxT", b, h)
                    claim(pe, nm)
                    for kt in range(CT):
                        ins = tr(bank(nm)[:, 128 * kt:128 * kt + 128], ctxP[:, kt, b, 128 * h:128 * h + 128],
                                 ident[:, :])
                    fill(ins, nm)
            claim(pe, "aaT")
            pe.wait_ge(aa_ready, 1)
            fill(tr(bank("aaT")[0:CT * B, 0:128], aa[:, :], ident[:, :]), "aaT")
            for h in range(DH):
                for half in range(2):
                    wait_drained(pe, ("lnT0", h, half))
            wait_drained(pe, "aaT")
            for b in range(B):
                nm = ("dist", b)
                claim(pe, nm)
                for h in range(DH):
                    wait_drained(pe, ("ctxT", b, h))
                    mm(bank(nm)[0:S, 0:KB * RB], ln0T[:, h, S * b:S * b + S], ctxT[:, h, b, :],
                       start=(h == 0), stop=False)
                for kt in range(CT):
                    i = B * kt + b
                    ins = mm(bank(nm)[0:S, 96 * kt:96 * kt + 96], ident[0:CT * B, i:i + 1].broadcast_to([CT * B, S]),
                             aaT[:, :].rearrange("p (g r) -> p g r", g=4)[:, :, 0:RB], start=False,
                             stop=(kt == CT - 1))
                fill(ins, nm)
            for b in range(B):
                wait_drained(pe, ("dist", b))
            for m in range(KB // 2):
                nm = ("skew", m)
                claim(pe, nm)
                for e in range(2):
                    k = 2 * m + e
                    ins = mm(bank(nm)[0:T, B * RB * e:B * RB * (e + 1)], skewI[0:S, KB - 1 - k:KB - 1 - k + T],
                             dist[:, :, k, :], start=True, stop=True)
                fill(ins, nm)
            for m in range(KB // 2):
                wait_drained(pe, ("skew", m))
            for m in range(RB // 4):
                nm = ("dwave", m)
                claim(pe, nm)
                for i in range(4):
                    ins = tr(bank(nm)[:, T * i:T * i + T],
                             skewed[:, :, :, 4 * m + i].rearrange("p b k -> p (b k)"), ident[0:T, 0:T])
                fill(ins, nm)
            pe.wait_ge(loaded["attnW"], 64)
            for i in range(4):
                nm = ("attnWT", i)
                claim(pe, nm)
                for h in range(DH):
                    for c in range(2):
                        ins = tr(bank(nm)[:, D * h + 128 * c:D * h + 128 * c + 128],
                                 wnat[:, i, c, 128 * h:128 * h + 128], ident[:, :])
                fill(ins, nm)
            claim(pe, "wsum")
            pe.wait_ge(wabs_ready, 1)
            fill(mm(bank("wsum")[:, 0:2], ones[:, :], wabs[:, :], start=True, stop=True), "wsum")
            pe.wait_ge(loaded["small"], 96)
            wait_drained(pe, ("attnWT", 2))
            for b in range(B):
                for c in range(KCH):
                    nm = ("V", b, c)
                    claim(pe, nm)
                    for h in range(DH):
                        mm(bank(nm)[0:KC, 0:D], ctxT[:, h, b, KC * c:KC * c + KC], wvT[:, h, :],
                           start=(h == 0), stop=False)
                    fill(mm(bank(nm)[0:KC, 0:D], ones[0:1, 0:KC], bvr[0:1, :], start=False, stop=True), nm)
            for w in range(2):
                pe.wait_ge(tern_ready, w + 1)
                for h in range(2):
                    nm = ("ternT", w, h)
                    claim(pe, nm)
                    for i in range(8):
                        if w == 0:
                            src = tern[0][:, D * i + 128 * h:D * i + 128 * h + 128]
                        else:
                            src = tern[1][:, HID * (i % 2) + 128 * (4 * h + i // 2):][:, 0:128]
                        ins = tr(bankb(nm)[:, 128 * i:128 * i + 128], src, identb[:, :])
                    fill(ins, nm)
            for t in range(4):
                for b in range(B):
                    nm = ("kT", t, b)
                    claim(pe, nm)
                    for h in range(DH):
                        ins = mm(bank(nm)[:, 0:SC], wkP[:, h, 128 * t:128 * t + 128], ctxT[:, h, b, 0:SC],
                                 start=(h == 0), stop=(h == DH - 1))
                    fill(ins, nm)
            pe.wait_ge(path_done, 1)
            for m in range(3):
                nm = ("pathT", m)
                claim(pe, nm)
                for i in range(8):
                    ins = tr(bankb(nm)[0:T, 128 * i:128 * i + 128], PR[:, 0:T, 2 * (8 * m + i) + 3], identb[:, :])
                fill(ins, nm)
            for m in range(3):
                wait_drained(pe, ("pathT", m))
            pe.wait_ge(path_zero, 1)
            for b in range(B):
                nm = ("path", b)
                claim(pe, nm)
                for kt in range(CT):
                    for g in range(4):
                        k = 4 * kt + g
                        ins = mm(bank(nm)[32 * g:32 * g + 32, S * kt:S * kt + S], pathT[:, b, k, :],
                                 skewB[0:T, KB - 1 + k:KB - 1 + k + S], start=True, stop=True)
                fill(ins, nm)
            pe.wait_ge(loaded["again"], 16 * sum(NCTX))
            for b in range(B):
                nm = ("expand", b)
                claim(pe, nm)
                wait_drained(pe, ("path", b))
                for kt in range(CT):
                    ins = mm(bank(nm)[0:S, 0:D], path[:, b, kt, :], ctx2[:, kt, b, :], start=(kt == 0),
                             stop=(kt == CT - 1))
                fill(ins, nm)
            pe.wait_ge(qx_ready, B)
            for h in range(DH):
                nm = ("qxT", h)
                claim(pe, nm)
                for b in range(B):
                    ins = tr(bankb(nm)[:, S * b:S * b + S], qx[:, b, 128 * h:128 * h + 128], identb[0:S, 0:S])
                fill(ins, nm)
            pe.wait_ge(sx_ready, 1)

            def token_rows(name, cols):
                for half in range(2):
                    nm = (name, half)
                    claim(pe, nm)
                    for i in range(4):
                        b = 4 * half + i
                        ins = mm(bank(nm)[:, S * i:S * i + S], cols[:, b:b + 1].broadcast_to([S, 128]),
                                 ident[0:S, 0:S], start=True, stop=True)
                    fill(ins, nm)

            token_rows("sxbc", sx)
            for h in range(DH):
                wait_drained(pe, ("qxT", h))
            for c in range(HT):
                for half in range(2):
                    nm = ("ffn_up", c, half)
                    claim(pe, nm)
                    for h in range(DH):
                        ins = mm(bank(nm)[:, 0:448], w1T[:, h, 128 * c:128 * c + 128],
                                 qxT[:, h, 448 * half:448 * half + 448], start=(h == 0), stop=(h == DH - 1))
                    fill(ins, nm)
            pe.wait_ge(hmax_part, HT // 2)
            for half in range(2):
                nm = ("hmaxT", half)
                claim(pe, nm)
                for i in range(4):
                    b = 4 * half + i
                    ins = tr(bank(nm)[0:S, 128 * i:128 * i + 128], hmax[:, S * b:S * b + S], ident[:, :])
                fill(ins, nm)
            pe.wait_ge(s2_ready, 1)
            token_rows("s2bc", asc)
            for b in range(B):
                nm = ("ffn_down", b)
                claim(pe, nm)
                for c in range(HT):
                    if b == 0:
                        pe.wait_ge(q2_ready, c + 1)
                    ins = mm(bank(nm)[0:S, 0:D], q2[:, c, S * b:S * b + S], w2T[:, c, :], start=(c == 0),
                             stop=(c == HT - 1))
                fill(ins, nm)
            ln_transposes(2, "lnT2", ln2, ident)
            for h in range(DH):
                for half in range(2):
                    wait_drained(pe, ("lnT2", h, half))
            for t in range(4):
                for half in range(2):
                    nm = ("qT", t, half)
                    claim(pe, nm)
                    for h in range(DH):
                        ins = mm(bank(nm)[:, 0:448], wqP[:, h, 128 * t:128 * t + 128],
                                 ln2T[:, h, 448 * half:448 * half + 448], start=(h == 0), stop=(h == DH - 1))
                    fill(ins, nm)
            for t in range(4):
                for half in range(2):
                    wait_drained(pe, ("qT", t, half))

            def value_products(b, t):
                for c in range(KCH):
                    wait_drained(pe, ("scoreT", b, t, c))
                    for g in range(4):
                        n = 4 * t + g
                        ins = mm(bank(("pv", b))[32 * g:32 * g + 32, S * t:S * t + S],
                                 v1[:, c, b, (HD + 1) * n:(HD + 1) * n + 32],
                                 E[:, (KCH * (4 * b + t) + c) % 6, S * g:S * g + S],
                                 start=(c == 0), stop=(c == KCH - 1))
                if t == 3:
                    fill(ins, ("pv", b))
                else:
                    ins.then_inc(pv_part, 1)

            for b in range(-1, B + 1):
                for t in range(4):
                    if b + 1 < B:
                        if t == 0:
                            pe.wait_ge(qm_ready, 4 * (b + 2))
                        for u in range(2):
                            nm = ("smax", b + 1, t, u)
                            claim(pe, nm)
                            for e in range(2):
                                ins = mm(psmax[u][0:S, e, 0:SC], qm[:, (b + 1) % 2, t, 2 * u + e, :],
                                         kT[:, t, b + 1, :], start=True, stop=True)
                            fill(ins, nm)
                    if 0 <= b < B:
                        for c in range(KCH):
                            nm = ("scoreT", b, t, c)
                            claim(pe, nm)
                            if t == 0 and c == 0:
                                wait_drained(pe, ("negmT", b))
                            fill(mm(bank(nm)[0:KC, 0:4 * S], kT[:, t, b, KC * c:KC * c + KC],
                                    qm[:, b % 2, t, :, :].rearrange("p g s -> p (g s)"), start=True, stop=True), nm)
                    if 0 <= b < B and t >= 1:
                        if t == 1:
                            claim(pe, ("pv", b))
                        value_products(b, t - 1)
                    if b >= 1 and t == 0:
                        value_products(b - 1, 3)
                    if b >= 1 and t == 1:
                        nm = ("pvT", b - 1)
                        claim(pe, nm)
                        wait_drained(pe, ("pv", b - 1))
                        for i in range(4):
                            ins = tr(bank(nm)[0:S, 128 * i:128 * i + 128], pvs[:, S * i:S * i + S], ident[:, :])
                        fill(ins, nm)
                    if b >= 1 and t == 2:
                        nm = ("oT", b - 1)
                        claim(pe, nm)
                        of = o[:, :, :].rearrange("p h e -> p (h e)")
                        for h in range(DH):
                            ins = tr(bank(nm)[:, S * h:S * h + S], of[:, 128 * h:128 * h + 128], ident[0:S, 0:S])
                        fill(ins, nm)
                    if b >= 1 and t == 3:
                        nm = ("wo", b - 1)
                        claim(pe, nm)
                        for h in range(DH):
                            mm(bank(nm)[0:S, 0:D], oT[:, h, :], woT[:, h, :], start=(h == 0), stop=False)
                        fill(mm(bank(nm)[0:S, 0:D], ones[0:1, 0:S], bor[0:1, :], start=False, stop=True), nm)
                if b + 1 < B:
                    nm = ("negmT", b + 1)
                    claim(pe, nm)
                    for t in range(4):
                        for u in range(2):
                            wait_drained(pe, ("smax", b + 1, t, u))
                        ins = tr(bank(nm)[:, S * t:S * t + S], negm[:, (b + 1) % 2, 128 * t:128 * t + 128],
                                 ident[0:S, 0:S])
                    fill(ins, nm)
            ln_transposes(3, "lnT3", ln3, ident)
            pe.wait_ge(loaded["pat"], 16)
            for m in range(NIT // 2):
                nm = ("patT", m)
                claim(pe, nm)
                for h in range(DH):
                    for i in range(2):
                        ins = tr(bank(nm)[:, 256 * h + 128 * i:256 * h + 128 * i + 128],
                                 patn[:, 2 * m + i, 128 * h:128 * h + 128], ident[:, :])
                fill(ins, nm)
            for h in range(DH):
                for half in range(2):
                    wait_drained(pe, ("lnT3", h, half))
            for i in range(NIT):
                wait_drained(pe, ("patT", i // 2))
                for half in range(2):
                    nm = ("pattern", i, half)
                    claim(pe, nm)
                    for h in range(DH):
                        ins = mm(bank(nm)[:, 0:448], patT[:, h, 128 * i:128 * i + 128],
                                 ln3T[:, h, 448 * half:448 * half + 448], start=(h == 0), stop=(h == DH - 1))
                    fill(ins, nm)
            pe.wait_ge(loaded["oiw"], 16)
            for m in range(NOT // 4):
                nm = ("oiwT", m)
                claim(pe, nm)
                for i in range(4):
                    ins = tr(bank(nm)[:, 128 * i:128 * i + 128], oiwn[:, 4 * m + i, :], ident[:, :])
                fill(ins, nm)

            def lanes_of(k):
                return B * (NIT, NPT, NOT)[k]

            def act_transpose(k):
                nm = ("actT", k)
                claim(pe, nm)
                pe.wait_ge(acts_ready, k + 1)
                fill(tr(bank(nm)[0:lanes_of(k), 0:128], acts[k][:, :], ident[:, :]), nm)

            def count(k, r):
                nm = ("count", k, r)
                n = lanes_of(k)
                claim(pe, nm)
                pe.wait_ge(cnt_ready, 16 * k + r + 1)
                fill(mm(bank(nm)[0:n, 0:3], same[k % 2][:, :], cnt[0:n, 0:3], start=True, stop=True), nm)

            def ties(k):
                nm = ("ties", k)
                n = lanes_of(k)
                claim(pe, nm)
                pe.wait_ge(tie_ready, k + 1)
                mm(bank(nm)[0:n, 0:1], same[k % 2][:, :], tie[0:n, 0:1], start=True, stop=False)
                fill(mm(bank(nm)[0:n, 0:1], under[k % 2][:, :], tie[0:n, 1:2], start=False, stop=True), nm)

            def sel_transpose(k):
                nm = ("selT", k)
                n = lanes_of(k)
                claim(pe, nm)
                pe.wait_ge(sel_ready, k + 1)
                src = sel if k == 1 else picked
                fill(tr(bank(nm)[:, 0:n], src[0:n, :], ident[0:n, 0:n]), nm)

            act_transpose(0)
            for i in range(NPT):
                pe.wait_ge(loaded[f"piw{i % 2}"], 16 * (i // 2 + 1))
                for m in range(NIT // 4):
                    nm = ("piwT", i, m)
                    claim(pe, nm)
                    for e in range(4):
                        c = 4 * m + e
                        ins = tr(bank(nm)[:, 128 * e:128 * e + 128], piw[:, i % 2, 128 * c:128 * c + 128],
                                 ident[:, :])
                    fill(ins, nm)
                for r in (2 * i, 2 * i + 1):
                    count(0, r)
            ties(0)
            sel_transpose(0)
            wait_drained(pe, ("selT", 0))
            for i in range(NPT):
                for m in range(NIT // 4):
                    wait_drained(pe, ("piwT", i, m))
            for h in range(2):
                nm = ("process", h)
                claim(pe, nm)
                for c in range(NIT):
                    g = c % 4
                    ins = mm(bank(nm)[32 * g:32 * g + 32, :], repr32[:, c, :], piwT[:, c, 512 * h:512 * h + 512],
                             start=(c < 4), stop=(c >= NIT - 4))
                fill(ins, nm)
            for h in range(2):
                nm = ("processT", h)
                claim(pe, nm)
                wait_drained(pe, ("process", h))
                for i in range(4):
                    ins = tr(bank(nm)[:, 128 * i:128 * i + 128], pact[:, 512 * h + 128 * i:512 * h + 128 * i + 128],
                             ident[:, :])
                fill(ins, nm)
            claim(pe, "pmaxT")
            pe.wait_ge(pmx_ready, 1)
            fill(tr(bank("pmaxT")[0:B, 0:128], pmx[:, :], ident[:, :]), "pmaxT")
            claim(pe, "pmaxb")
            pe.wait_ge(pmd_ready, 1)
            fill(mm(bank("pmaxb")[:, 0:B], ones[0:B, :], pmd[:, :], start=True, stop=True), "pmaxb")
            act_transpose(1)
            for r in range(16):
                count(1, r)
            ties(1)
            sel_transpose(1)
            claim(pe, "aggr")
            wait_drained(pe, ("selT", 1))
            pe.wait_ge(loaded["pval"], 16)
            for i in range(NPT):
                mm(bank("aggr")[:, 0:B], pval[:, i, :], cells(esel, NPT)[:, :, i], start=(i == 0),
                   stop=(i == NPT - 1))
            for i in range(NPT):
                ins = mm(bank("aggr")[:, B:2 * B], ones[:, :], cells(esel, NPT)[:, :, i], start=(i == 0),
                         stop=(i == NPT - 1))
            fill(ins, "aggr")
            claim(pe, "output")
            wait_drained(pe, "aggr")
            for m in range(NOT // 4):
                wait_drained(pe, ("oiwT", m))
            for i in range(NOT):
                ins = mm(bank("output")[:, B * i:B * i + B], oiwT[:, 128 * i:128 * i + 128], agg[:, :], start=True,
                         stop=True)
            fill(ins, "output")
            act_transpose(2)
            for r in range(16):
                count(2, r)
            ties(2)
            sel_transpose(2)
            wait_drained(pe, ("selT", 2))
            claim(pe, "final")
            pe.wait_ge(loaded["opat"], 16)
            for i in range(NOT):
                ins = mm(bank("final")[0:B, 0:D], cells(outr, NOT)[:, :, i], opat[:, i, :], start=(i == 0),
                         stop=(i == NOT - 1))
            fill(ins, "final")
            wait_drained(pe, "final")
            for b in range(B):
                nm = ("spread", b)
                claim(pe, nm)
                fill(mm(bank(nm)[0:S, 0:D], ident[0:B, b:b + 1].broadcast_to([B, S]), fin[:, :], start=True,
                        stop=True), nm)


INPUTS = ["x", "ctx_1024", "g_xattn", "g_ffn", "L0_ffn_w1", "L0_ffn_conv_w", "L0_ffn_conv_b", "L0_ffn_w2",
          "L1_xattn_Wq", "L1_xattn_bq", "L1_xattn_Wk", "L1_xattn_bk", "L1_xattn_Wv", "L1_xattn_bv",
          "L1_xattn_Wo", "L1_xattn_bo", "L1_ffn_input_patterns", "L1_ffn_process_input_weights",
          "L1_ffn_process_values", "L1_ffn_output_input_weights", "L1_ffn_output_patterns"]


def kernel(**inputs):
    import concourse.bacc as bacc
    from concourse.bass_utils import run_bass_kernel_spmd

    nc = bacc.Bacc("TRN2", target_bir_lowering=False, num_devices=1)
    arrays, args = {}, []
    for name in INPUTS:
        a = np.ascontiguousarray(inputs[name])
        arrays[f"in_{name}"] = a
        args.append(nc.dram_tensor(f"in_{name}", a.shape, mybir.dt.from_np(a.dtype), kind="ExternalInput").ap())
    args.append(nc.dram_tensor("out", (B, S, D), F32, kind="ExternalOutput").ap())
    build_program(nc, *args)
    return run_bass_kernel_spmd(nc, [arrays], core_ids=[0]).results[0]["out"]
```

```python
import numpy as np
import concourse.bass as bass
from concourse import mybir
from contextlib import ExitStack

F32, BF16, I32 = mybir.dt.float32, mybir.dt.bfloat16, mybir.dt.int32
ALU = mybir.AluOpType
ACT = mybir.ActivationFunctionType
AX = mybir.AxisListType

B, S, D, SC = 8, 112, 256, 375
DH = D // 128
KB, RB = 16, 24
CT = 4
T = S + KB - 1
HID, HT = 1024, 8
NH, HD = 16, 16
KC, KCH = 125, 3
K_PARTS = (0, 1, 0, 1, 0, 2)
Q_PARTS = (0, 0, 1, 1, 2, 0)
SR = HD * len(K_PARTS)
LAG = 5
PT = 3
STEPS = (tuple(4 ** (7 - r) for r in range(8)),) + ((2 ** 13, 2 ** 10, 2 ** 7, 2 ** 4, 2, 1),) * 2
NCAND, VC = (3, 7, 7), (3, 4, 4)
ROUNDS = tuple(len(s) for s in STEPS)
ROUNDS_BEFORE = (0, 2 * ROUNDS[0], 2 * (ROUNDS[0] + ROUNDS[1]))
HB = B // 2
FREE = 4 * B - LAG
VW = NH * (HD + 1) + 15
NI, NP, NO, DPV = 2048, 1024, 2048, 128
NIT, NPT, NOT = NI // 128, NP // 128, NO // 128
BIG = 1.0e30
MAGIC = 12582912.0
TOK = B * S


SIGNALLED_BY_RESULT = ("expand", "ffn_down", "wo", "pattern", "output", "spread")


class Group:

    def __init__(self, name, banks, nth, nth_drain, before):
        self.name, self.banks, self.nth, self.nth_drain, self.before = name, banks, nth, nth_drain, before


class PsumPlan:

    def __init__(self, nbanks):
        self.uses = [0] * nbanks
        self.drains = [0] * nbanks
        self.last = [None] * nbanks
        self.groups = {}

    def add(self, name, *banks):
        before = []
        for b in banks:
            if self.last[b] is not None and self.last[b] not in before:
                before.append(self.last[b])
        self.uses[banks[0]] += 1
        if (name if isinstance(name, str) else name[0]) not in SIGNALLED_BY_RESULT:
            self.drains[banks[0]] += 1
        g = Group(name, banks, self.uses[banks[0]], self.drains[banks[0]], before)
        for b in banks:
            self.last[b] = g
        self.groups[name] = g

    def __getitem__(self, name):
        return self.groups[name]


def plan_psum():
    p = PsumPlan(8)
    n = [0]

    def ring(name, banks=tuple(range(8))):
        p.add(name, banks[n[0] % len(banks)])
        n[0] += 1

    for half in range(2):
        for h in range(DH):
            ring(("lnT0", h, half))
    for b in range(B):
        for h in range(DH):
            ring(("ctxT", b, h))
    ring("aaT")
    for b in range(B):
        ring(("dist", b))
    for m in range(KB // 2):
        ring(("skew", m))
    for m in range(RB // 4):
        ring(("dwave", m))
    for w in range(4):
        ring(("attnWT", w))
    ring("wsum")
    ring("bo")
    for b in range(B):
        for c in range(KCH):
            ring(("V", b, c))
    for w in range(2):
        for h in range(2):
            ring(("ternT", w, h))
    for t in range(2):
        for b in range(B):
            ring(("kT", t, b))
    for m in range(3):
        ring(("pathT", m))
    for b in range(B):
        ring(("path", b))
    for b in range(B):
        ring(("expand", b))
    for h in range(DH):
        ring(("qxT", h))
    for half in range(2):
        ring(("sxbc", half))
    for c in range(HT):
        for half in range(2):
            ring(("ffn_up", c, half))
    for half in range(2):
        ring(("hmaxT", half))
    for half in range(2):
        ring(("s2bc", half))
    for b in range(B):
        ring(("ffn_down", b))
    for half in range(2):
        for h in range(DH):
            ring(("lnT2", h, half))
    for half in range(2):
        for t in range(2):
            ring(("qT", t, half))
    for f in range(-LAG - 1, 4 * B + 4):
        if 0 <= f + LAG + 1 < 4 * B:
            p.add(("qstack", f + LAG + 1), 3)
        if 0 <= f + LAG < 4 * B:
            for i in range(4):
                p.add(("smax", f + LAG, i), (4 * (f + LAG) + i) % 3)
        if 0 <= f < 4 * B:
            for c in range(KCH):
                p.add(("scoreT", f, c), 4 + (KCH * f + c) % 2)
            if f % 4 == 1:
                p.add(("pv", f // 4), 6)
        if f in (FREE - 3, FREE - 2):
            p.add(("lnT3", f - FREE + 3, 0), 3)
        if FREE + 1 <= f < FREE + 5:
            for m in range(2):
                p.add(("patT", 2 * (f - FREE - 1) + m), m)
        if f >= 4 * B:
            for i in range(2):
                p.add(("pattern", 2 * (f - 4 * B) + i), i)
        if f >= 4 and f % 4 >= 1:
            p.add((("pvT", "oT", "wo")[f % 4 - 1], f // 4 - 1), 7)
        if 0 <= f + 1 < 4 * B:
            p.add(("negT", f + 1), 7)
    for i in range(8, 2 * NIT):
        p.add(("pattern", i), i % 2)
    for h in range(DH):
        p.add(("lnT3", h, 1), 2 + h)
    for m in range(NOT // 4):
        p.add(("oiwT", m), 4 + m)
    n[0] = 0
    for p_ in range(NPT):
        for m in range(NIT // 4):
            ring(("piwT", p_, m), (0, 1, 2, 3))
    for k in range(3):
        p.add(("actT", k), 7)
        for r in range(2 * ROUNDS[k]):
            p.add(("count", k, r), 4 + r % 2)
        p.add(("ties", k), 6)
        p.add(("selT", k), 7)
        if k == 0:
            p.add(("process", 0), 0)
            p.add(("process", 1), 1)
            p.add(("processT", 0), 2)
            p.add(("processT", 1), 3)
            p.add("pmaxT", 0)
            p.add("pmaxb", 1)
        elif k == 1:
            p.add("aggr", 2)
            p.add("output", 3)
    p.add("final", 0)
    for b in range(B):
        p.add(("spread", b), b % 4)
    return p



def build_program(nc, x_in, ctx_in, g_xattn, g_ffn, w1_in, conv_w, conv_b, w2_in,
                  wq_in, bq_in, wk_in, bk_in, wv_in, bv_in, wo_in, bo_in,
                  pat_in, piw_in, pval_in, oiw_in, opat_in, out, key_parts):
    plan = plan_psum()
    ctx = ExitStack()
    with ctx:
        class Region:

            def __init__(self, start):
                self.at = start

            def take(self, name, shape, dt=F32):
                size = int(np.prod(shape[1:])) * (2 if dt == BF16 else 4)
                h = nc.alloc_sbuf_tensor_at(name, list(shape), dt, offset=self.at)
                self.at += (size + 31) // 32 * 32
                return h

        top = (nc.sbuf_base + 63) // 64 * 64
        ra = Region(top)
        ident = ra.take("ident", [128, 128])
        identb = ra.take("identb", [128, 128], BF16)
        ones = ra.take("ones", [128, 128])
        same = [ra.take(f"same{n}", [B * n, B * n], BF16) for n in (NIT, NPT)]
        under = [ra.take(f"under{n}", [B * n, B * n], BF16) for n in (NIT, NPT)]
        pick = ra.take("pick", [128, 3, 8, SR], BF16)
        skewI = ra.take("skewI", [128, T + KB - 1])
        skewB = ra.take("skewB", [128, T + KB - 1], BF16)
        steps = [ra.take(f"steps{k}", [128, ROUNDS[k], NCAND[k]]) for k in range(2)]
        iota_i = ra.take("iota_i", [128, 1], I32)
        iota_t = ra.take("iota_t", [128, T])
        blk_i = ra.take("blk_i", [128, 1], I32)
        blk = ra.take("blk", [128, 1])
        first_up = ra.take("first_up", [128, 1])
        last_big = ra.take("last_big", [128, 1])
        wavepad = ra.take("wavepad", [128, T])
        seed = ra.take("seed", [128, 48], BF16)
        eps = ra.take("eps", [128, 1])
        no_magic = ra.take("no_magic", [128, 1])
        warm = ra.take("warm", [128, 1])
        x = ra.take("x", [S, B, D])
        gates = ra.take("gates", [128, 4])
        gbo = ra.take("gbo", [S, D])
        tg = ra.take("tg", [128, 4])
        bn6 = ra.take("bn6", [S, B, 6])
        mv = ra.take("mv", [S, B, 2])
        sd = ra.take("sd", [S, B])
        rstd = ra.take("rstd", [S, B])
        bb = ra.take("bb", [S, B])
        aa = ra.take("aa", [128, CT * B])
        aaT = ra.take("aaT", [CT * B, 128])
        bqT = ra.take("bqT", [128, 2])
        bkT = ra.take("bkT", [128, 2])
        bqs = ra.take("bqs", [128, 2])
        bvr = ra.take("bvr", [1, D])
        bor = ra.take("bor", [1, D])
        cw = ra.take("cw", [128, HT, 3])
        cb = ra.take("cb", [128, HT])
        cws = ra.take("cws", [128, HT, 3])
        wabs = ra.take("wabs", [128, 2])
        wmean = ra.take("wmean", [128, 2])
        winv = ra.take("winv", [128, 2])
        am = ra.take("am", [S, B])
        ari = ra.take("ari", [S, B])
        asc = ra.take("asc", [S, B])
        sx = ra.take("sx", [S, B])
        actscr = ra.take("actscr", [128, D])
        rw = Region(ra.at)
        w1T = rw.take("w1T", [128, DH, HID], BF16)
        w2T = rw.take("w2T", [128, HT, D], BF16)
        wqT = rw.take("wqT", [128, DH, D])
        wkT = rw.take("wkT", [128, DH, D])
        wvT = rw.take("wvT", [128, DH, D])
        woT = rw.take("woT", [128, DH, D])
        piw = Region(ra.at).take("piw", [128, 2, NI])
        rk = Region(rw.at)
        ks = rk.take("ks", [128, 3, NH, SC], BF16)
        last_stack = rk.at - 2 * NH * SC
        kx = rk.take("kx", [128, 2, SC])
        kp = rk.take("kp", [128, 2, 3, SC], BF16)
        v1 = rk.take("v1", [KC, KCH, B, VW])
        rn = Region(rw.at)
        wnat = rn.take("wnat", [128, 4, 2, D])
        w1n = rn.take("w1n", [128, 2048])
        w2n = rn.take("w2n", [128, 2048])
        tern = [rn.take(f"tern{i}", [128, 2048], BF16) for i in range(2)]
        ln0 = rn.take("ln0", [S, B, D])
        ln0T = rn.take("ln0T", [128, DH, TOK])
        rl = Region(rw.at)
        piwT = rl.take("piwT", [128, NIT, NP])
        c0 = max(rk.at, rl.at)
        rc = Region(c0)
        ctxP = rc.take("ctxP", [128, CT, B, D])
        rz = Region(c0)
        LG = rz.take("LG", [128, T, 50], BF16)
        UU = rz.take("UU", [128, T, 50], BF16)
        PR = rz.take("PR", [128, T + 1, 50], BF16)
        rx = Region(max(rc.at, rz.at))
        ctxT = Region(rx.at).take("ctxT", [128, DH, B, KB * RB])
        ctx_again = rx.take("ctx_again", [128, CT, B, D])
        rd = Region(rx.at)
        dist = Region(rd.at).take("dist", [S, B, KB, RB])
        rp = Region(rd.at)
        dwave = rd.take("dwave", [128, T, RB])
        skewed = Region(max(rd.at, rx.at + 4 * B * KB * RB)).take("skewed", [T, B, KB, RB])
        rd.at = max(rd.at, rx.at + 4 * B * KB * RB)
        R = rd.take("R", [128, T + 1, RB + 1])
        dmin = rd.take("dmin", [128, RB])
        rmin = rd.take("rmin", [128, 3 * RB])
        prod = rd.take("prod", [128, 48], BF16)
        pathT = rp.take("pathT", [T, B, KB, 32], BF16)
        path = rp.take("path", [128, B, CT, S])
        rf = Region(c0)
        hs = rf.take("hs", [128, HT, TOK])
        ln1 = rf.take("ln1", [S, B, D])
        qx = rf.take("qx", [S, B, D], BF16)
        qxT = rf.take("qxT", [128, DH, TOK], BF16)
        sxbc = rf.take("sxbc", [128, TOK])
        hb = rf.take("hb", [128, 3, B, S + 2])
        ct0 = rf.take("ct0", [128, 3, TOK])
        hmax = rf.take("hmax", [128, TOK])
        hmax2 = rf.take("hmax2", [128, TOK])
        s2bc = rf.take("s2bc", [128, TOK])
        q2 = rf.take("q2", [128, HT, TOK], BF16)
        rt = Region(c0)
        exps = Region(rt.at)
        ln2 = rt.take("ln2", [S, B, D])
        ln2T = rt.take("ln2T", [128, DH, TOK])
        E = exps.take("E", [KC, 6, 4 * S])
        rt.at = max(rt.at, exps.at)
        queries_at = rt.at
        qx32 = rt.take("qx32", [128, 2, TOK])
        after_queries = rt.at
        qp = rt.take("qp", [128, 2, 3, TOK], BF16)
        qs = rt.take("qs", [128, 3, NH, S], BF16)
        negm = rt.take("negm", [S, NH])
        negp = rt.take("negp", [S, 2, NH, 3], BF16)
        pvs = rt.take("pvs", [128, 4 * S])
        rs = rt.take("rs", [S, NH])
        o = rt.take("o", [S, NH, HD])
        oT = rt.take("oT", [128, DH, S])
        loads = Region(max(rd.at, rf.at) - 4 * (NIT * D + NOT * DPV + NOT * D + NPT * DPV))
        assert rt.at <= loads.at
        patT = Region(last_stack).take("patT", [128, DH, NI])
        ln3 = Region(exps.at).take("ln3", [S, HB, D])
        early = Region(queries_at)
        gel = early.take("gel", [128, 2, 448])
        acts0 = early.take("acts0", [128, B * NIT])
        ln3Ta = Region(max(rd.at, rf.at)).take("ln3Ta", [128, DH, HB * S])
        r1 = Region(after_queries)
        ln3T = [ln3Ta, r1.take("ln3Tb", [128, DH, HB * S])]
        oiwT = r1.take("oiwT", [128, NO])
        acts = [acts0] + [r1.take(f"acts{k + 1}", [128, B * n]) for k, n in enumerate((NPT, NOT))]
        aT = r1.take("aT", [128, 128])
        key = r1.take("key", [128, 128], I32)
        sgn = r1.take("sgn", [128, 128], I32)
        khi = r1.take("khi", [128, 128])
        klo = r1.take("klo", [128, 128])
        kval = r1.take("kval", [128, 128])
        picked = kval
        below = r1.take("below", [128, max(NCAND), 128], BF16)
        most = r1.take("most", [128, max(NCAND)])
        cand = r1.take("cand", [128, max(NCAND)])
        nextb = r1.take("nextb", [128, max(NCAND)])
        cnt = r1.take("cnt", [128, 8], BF16)
        reached = r1.take("reached", [128, max(NCAND)])
        nsel = r1.take("nsel", [128, 1])
        bound = r1.take("bound", [128, 1])
        eq = r1.take("eq", [128, 128])
        gt = r1.take("gt", [128, 128])
        tie = r1.take("tie", [128, 2], BF16)
        need = r1.take("need", [128, 1])
        incl = r1.take("incl", [128, 128])
        sel = r1.take("sel", [128, 128])
        repr32 = r1.take("repr32", [128, NIT, 32])
        pact = r1.take("pact", [128, NP])
        praw = r1.take("praw", [128, B * NPT])
        batch_of = r1.take("batch_of", [128, B])
        esel = r1.take("esel", [128, B * NPT])
        pmx = r1.take("pmx", [128, B])
        pm8 = r1.take("pm8", [B, 1])
        pmd = r1.take("pmd", [B, B])
        agr = r1.take("agr", [128, B])
        agg = r1.take("agg", [128, B])
        fin = r1.take("fin", [128, D])
        assert r1.at <= loads.at, (r1.at - c0, loads.at - c0)
        patn = loads.take("patn", [128, NIT, D])
        oiwn = loads.take("oiwn", [128, NOT, DPV])
        opat = loads.take("opat", [128, NOT, D])
        pval = loads.take("pval", [128, NPT, DPV])
        assert max(rd.at, rf.at, loads.at) <= nc.sbuf_usable_end, (rd.at, rf.at, nc.sbuf_usable_end)

        ps = [ctx.enter_context(nc.psum_tensor(f"ps{i}", [128, 512], F32))[:, :] for i in range(8)]

        def sem(name):
            return ctx.enter_context(nc.semaphore(name))

        filled = [sem(f"filled{i}") for i in range(8)]
        drained = [sem(f"drained{i}") for i in range(8)]

        def fill(ins, name):
            ins.then_inc(filled[plan[name].banks[0]], 1)

        def drain(ins, name):
            ins.then_inc(drained[plan[name].banks[0]], 1)

        def wait_filled(eng, name):
            g = plan[name]
            eng.wait_ge(filled[g.banks[0]], g.nth)

        def wait_drained(eng, name):
            kind = name if isinstance(name, str) else name[0]
            if kind == "expand":
                eng.wait_ge(x_ready, name[1] + 1)
            elif kind == "ffn_down":
                eng.wait_ge(x_ready, B + name[1] + 1)
            elif kind == "wo":
                eng.wait_ge(x_ready, 2 * B + name[1] + 1)
            elif kind == "spread":
                eng.wait_ge(x_ready, 3 * B + name[1] + 1)
            elif kind == "pattern":
                eng.wait_ge(gel_ready, name[1] + 1)
            elif kind == "output":
                eng.wait_ge(acts_ready, 3)
            else:
                g = plan[name]
                eng.wait_ge(drained[g.banks[0]], g.nth_drain)

        def claim(eng, name):
            for g in plan[name].before:
                wait_drained(eng, g.name)

        def bank(name):
            return ps[plan[name].banks[0]]

        def bankb(name):
            return ps[plan[name].banks[0]][:, :].bitcast(BF16)

        names = ("x", "ctx0", "ctx1", "ctx2", "ctx3", "again", "attnW", "ffnW", "small", "biasT", "pat", "oiw",
                 "opat", "pval", "piw0", "piw1")
        loaded = {n: sem(f"loaded_{n}") for n in names}
        (consts_ready, stored, tg_ready, var_ready, sd_ready, ln_ready, bb_ready, aa_ready,
         wabs_ready, winv_ready, tern_ready, ones_v_ready, path_zero, path_done, x_ready,
         qx_ready, sx_ready, left_done, scaled, uu_ready, rounded, bias_added, cand_ready,
         signs_ready, ct0_ready, conv_done, silu_done, s2_ready, q2_ready, hmax_part,
         neg_ready, q_split, k_split, k_ones, pv_part, cnt_ready, tie_ready, sel_ready,
         gel_ready, gel_used, acts_ready, pmx_ready, pmd_ready, pexp_ready, vec, scl, pol) = [sem(n) for n in (
             "consts_ready stored tg_ready var_ready sd_ready ln_ready bb_ready aa_ready "
             "wabs_ready winv_ready tern_ready ones_v_ready path_zero path_done x_ready qx_ready "
             "sx_ready left_done scaled uu_ready rounded bias_added cand_ready signs_ready "
             "ct0_ready conv_done silu_done s2_ready q2_ready hmax_part neg_ready q_split "
             "k_split k_ones pv_part cnt_ready tie_ready sel_ready gel_ready gel_used acts_ready "
             "pmx_ready pmd_ready pexp_ready vec scl pol").split()]

        parts_stored = [sem(f"parts_stored{i}") for i in range(2)]
        stack_loaded = [sem(f"stack_loaded{i}") for i in range(3)]

        def counter(eng, s):
            n = [0]

            def did(ins):
                n[0] += 1
                ins.then_inc(s, 1)
                return n[0]

            def settle(upto=None):
                eng.wait_ge(s, n[0] if upto is None else upto)
            return did, settle

        def wait_values(eng, step):
            if step % 4 == 3:
                wait_filled(eng, ("pv", step // 4))
            else:
                eng.wait_ge(pv_part, 3 * (step // 4) + step % 4 + 1)

        def cells(t, n):
            return t[:, 0:B * n].rearrange("p (b n) -> p b n", b=B)

        def hand(ap, dims):
            return bass.AP(ap.tensor, ap.offset, [list(ap.ap[0])] + dims)

        NCTX = (4, 4, 4, 5)
        block = ctx.enter_context(nc.Block())

        @block.sync
        def _(sp):
            sp.dma_start(x[:, :, :], x_in.rearrange("b s d -> s b d")).then_inc(loaded["x"], 16)
            def load_context(dst, sems):
                for kt in range(CT):
                    for g in range(4):
                        row = RB * (4 * kt + g)
                        n = min(32, SC - row)
                        sp.dma_start(dst[32 * g:32 * g + n, kt, :, :],
                                     ctx_in[:, row:row + n, :].rearrange("b r d -> r b d")).then_inc(sems[kt], 16)
                        if n < 32:
                            sp.dma_start(dst[32 * g + n:32 * g + 32, kt, :, :],
                                         ctx_in[:, 0:32 - n, :].rearrange("b r d -> r b d")).then_inc(sems[kt], 16)

            load_context(ctxP, [loaded[f"ctx{kt}"] for kt in range(CT)])
            for i, w in enumerate((wq_in, wk_in, wv_in, wo_in)):
                sp.dma_start(wnat[:, i, :, :], w.rearrange("(c p) d -> p c d", p=128)).then_inc(loaded["attnW"], 16)
            sp.dma_start(w1n[:, :].rearrange("p (c d) -> p c d", c=HT),
                         w1_in.rearrange("(c p) d -> p c d", p=128)).then_inc(loaded["ffnW"], 16)
            sp.dma_start(w2n[:, :].rearrange("p (c d) -> p c d", c=2),
                         w2_in.rearrange("(c p) d -> p c d", p=128)).then_inc(loaded["ffnW"], 16)
            sp.dma_start(cw[:, :, :], conv_w.rearrange("(c p) o k -> p c (o k)", p=128)).then_inc(loaded["small"], 16)
            sp.dma_start(cb[:, :], conv_b.rearrange("(c p) -> p c", p=128),
                         allow_slow_non_contiguous=True).then_inc(loaded["small"], 16)
            sp.dma_start(bvr[0:1, :], bv_in.rearrange("(o d) -> o d", o=1)).then_inc(loaded["small"], 16)
            sp.dma_start(bor[0:1, :], bo_in.rearrange("(o d) -> o d", o=1)).then_inc(loaded["small"], 16)
            for i, g in enumerate((g_xattn, g_ffn)):
                sp.dma_start(gates[:, 2 * i:2 * i + 2],
                             g.rearrange("(o d) -> o d", o=1).broadcast_to([128, 2])).then_inc(loaded["small"], 16)
            for dst, src in ((bqT, bq_in), (bkT, bk_in)):
                sp.dma_start(dst[:, :], src.rearrange("(t p) -> p t", p=128),
                             allow_slow_non_contiguous=True).then_inc(loaded["biasT"], 16)
            for u in range(2 * B):
                t, b = u // B, u % B
                sp.wait_ge(k_split, u + 1)
                sp.dma_start(key_parts[b, :, 128 * t:128 * t + 128, :].rearrange("c p s -> p c s"),
                             kp[:, u % 2, :, :]).then_inc(parts_stored[u % 2], 16)
            wait_filled(sp, ("kT", 1, B - 1))
            load_context(ctx_again, [loaded["again"]] * CT)

            def load_stack(b):
                for j, part in enumerate(K_PARTS):
                    sp.dma_start(ks[HD * j:HD * j + HD, b % 3, :, :],
                                 key_parts[b, part].rearrange("(n d) s -> d n s", d=HD)
                                 ).then_inc(stack_loaded[b % 3], 16)

            for i in range(2):
                sp.wait_ge(parts_stored[i], 16 * B)
            for b in range(3):
                load_stack(b)
            sp.wait_ge(x_ready, 2 * B)
            wait_filled(sp, ("scoreT", 3, KCH - 1))
            load_stack(3)
            sp.dma_start(patn[:, :, :], pat_in.rearrange("(c p) d -> p c d", p=128)).then_inc(loaded["pat"], 16)
            wait_filled(sp, ("scoreT", 7, KCH - 1))
            load_stack(4)
            sp.dma_start(oiwn[:, :, :], oiw_in.rearrange("(c p) d -> p c d", p=128)).then_inc(loaded["oiw"], 16)
            wait_filled(sp, ("scoreT", 11, KCH - 1))
            load_stack(5)
            sp.dma_start(opat[:, :, :], opat_in.rearrange("(c p) d -> p c d", p=128)).then_inc(loaded["opat"], 16)
            sp.dma_start(pval[:, :, :], pval_in.rearrange("(c p) d -> p c d", p=128)).then_inc(loaded["pval"], 16)
            for b in range(6, B):
                wait_filled(sp, ("scoreT", 4 * b - 9, KCH - 1))
                load_stack(b)
            sp.wait_ge(x_ready, 3 * B)
            for i in range(NPT):
                if i >= 2:
                    wait_filled(sp, ("piwT", i - 2, NIT // 4 - 1))
                sp.dma_start(piw[:, i % 2, :], piw_in[128 * i:128 * (i + 1), :]).then_inc(loaded[f"piw{i % 2}"], 16)
            for b in range(B):
                sp.wait_ge(x_ready, 3 * B + b + 1)
                sp.dma_start(out[b], x[:, b, :]).then_inc(stored, 16)
            sp.wait_ge(stored, 16 * B)

        @block.gpsimd
        def _(pool):
            did, settle = counter(pool, pol)
            for t in (ident, identb, skewI, skewB, pick):
                did(pool.memset(t[:, :], 0.0))
            for t in (ones, same[0], same[1]):
                did(pool.memset(t[:, :], 1.0))
            did(pool.memset(eps[:, :], 1e-5))
            did(pool.memset(no_magic[:, :], -MAGIC))
            did(pool.iota(iota_i[:, :], [[0, 1]], base=0, channel_multiplier=1))
            did(pool.iota(iota_t[:, :], [[1, T]], base=0, channel_multiplier=0,
                          allow_small_or_imprecise_dtypes=True))
            settle()
            for t in (ident, identb):
                did(pool.affine_select(out=t[:, :], in_=t[:, :], compare_op=ALU.not_equal, fill=1.0, base=0,
                                       pattern=[[-1, 128]], channel_multiplier=1))
            for t in (skewI, skewB):
                did(pool.affine_select(out=t[:, :], in_=t[:, :], compare_op=ALU.not_equal, fill=1.0, base=KB - 1,
                                       pattern=[[-1, T + KB - 1]], channel_multiplier=1))
            for t, n in zip(same, (NIT, NPT)):
                j = n
                v = t[:, :].rearrange("p (g j) -> p g j", j=j)
                g = v.shape[1]
                did(pool.affine_select(out=v, in_=v, compare_op=ALU.is_ge, fill=0.0, base=0,
                                       pattern=[[-n, g], [0, j]], channel_multiplier=1))
                settle()
                did(pool.affine_select(out=v, in_=v, compare_op=ALU.is_ge, fill=0.0, base=n - 1,
                                       pattern=[[n, g], [0, j]], channel_multiplier=-1))
            settle()
            for a, u in zip(same, under):
                did(pool.affine_select(out=u[:, :], in_=a[:, :], compare_op=ALU.is_gt, fill=0.0, base=0,
                                       pattern=[[1, a.shape[1]]], channel_multiplier=-1))
            settle()
            pool.memset(warm[:, :], 0.0).then_inc(consts_ready, 1)
            for j, part in enumerate(Q_PARTS):
                did(pool.tensor_copy(pick[:, part, :, HD * j:HD * j + HD],
                                     identb[:, :].rearrange("p (e d) -> p e d", d=HD)))
            settle()
            for b in range(B):
                wait_filled(pool, ("ctxT", b, DH - 1))
            wait_filled(pool, "aaT")
            pool.memset(hand(UU[:, :, 1:2], [[50, T], [2, RB]]), 1.0).then_inc(uu_ready, 1)
            pool.wait_ge(uu_ready, 1)
            wait_drained(pool, ("attnWT", 3))
            wait_filled(pool, ("dist", B - 1))
            pool.memset(v1[:, :, :, :], 1.0).then_inc(ones_v_ready, 1)
            pool.wait_ge(winv_ready, 1)
            for i, w in enumerate((w1n, w2n)):
                did(pool.tensor_scalar(w[:, :], w[:, :], winv[:, i:i + 1], MAGIC, ALU.mult, ALU.add))
                settle()
                did(pool.tensor_scalar(w[:, :], w[:, :], -MAGIC, 1.0, ALU.add, ALU.mult))
                settle()
                pool.tensor_scalar(tern[i][:, :], w[:, :], 1.0, -1.0, ALU.min, ALU.max).then_inc(tern_ready, 1)
            pool.wait_ge(tern_ready, 2)
            for k in range(2):
                for r in range(ROUNDS[k]):
                    for m in range(NCAND[k]):
                        did(pool.memset(steps[k][:, r, m:m + 1],
                                        float((m + 1) * STEPS[k][r]) - (0.5 if m >= VC[k] else 0.0)))
            settle()
            for u in range(2 * B):
                wait_drained(pool, ("kT", u // B, u % B))
                x32, part = kx[:, u % 2, :], kp[:, u % 2, :, :]
                did(pool.tensor_tensor(x32, x32, part[:, 0, :], ALU.subtract))
                settle()
                if u >= 2:
                    pool.wait_ge(parts_stored[u % 2], 16 * (u // 2))
                did(pool.tensor_copy(part[:, 1, :], x32))
                settle()
                pool.tensor_tensor(part[:, 2, :], x32, part[:, 1, :], ALU.subtract).then_inc(k_split, 1)
            pool.wait_ge(k_split, 2 * B)
            wait_filled(pool, ("ternT", 1, 1))
            pool.memset(ks[SR:SR + 3, :, :, :], 1.0).then_inc(k_ones, 1)
            pool.wait_ge(k_ones, 1)
            for c in range(HT):
                acc = ct0[:, c % 3, :].rearrange("p (b s) -> p b s", b=B)
                pool.wait_ge(ct0_ready, c + 1)
                left = hs[:, c, :].rearrange("p (b s) -> p b s", b=B)
                did(pool.tensor_scalar(left, hb[:, c % 3, :, 0:S], cws[:, c, 0:1], 0.0, ALU.mult, ALU.add))
                settle()
                pool.tensor_tensor(acc, acc, left, ALU.add).then_inc(left_done, 1)
            wait_drained(pool, ("s2bc", 0))
            wait_drained(pool, ("s2bc", 1))
            for c in range(HT - PT, HT):
                pool.tensor_tensor(hs[:, c, :], hs[:, c, :], s2bc[:, :], ALU.mult).then_inc(scaled, 1)
            wait_drained(pool, "bo")
            pool.wait_ge(scaled, PT)
            pool.wait_ge(ln_ready, 3 * B)
            for b in range(B):
                pool.tensor_tensor(x[:, b, :], x[:, b, :], gbo[:, :], ALU.add).then_inc(bias_added, 1)

        @block.vector
        def _(dve):
            did, settle = counter(dve, vec)
            tt, ts, stt = dve.tensor_tensor, dve.tensor_scalar, dve.scalar_tensor_tensor

            def statistics(n, b):
                if n:
                    dve.wait_ge(x_ready, (n - 1) * B + b + 1)
                did(dve.bn_stats(bn6[:, b, :], x[:, b, :]))

            def layernorm(n, src, dst):
                settle()
                for b in range(B):
                    last = dve.bn_aggr(mv[:, b, :], bn6[:, b, :])
                    if b < B - 1:
                        did(last)
                last.then_inc(var_ready, 1)
                dve.wait_ge(sd_ready, n + 1)
                did(dve.reciprocal(rstd[:, :], sd[:, :]))
                settle()
                for b in range(B):
                    ts(dst[:, b, :], src[:, b, :], mv[:, b, 0:1], rstd[:, b:b + 1],
                       ALU.subtract, ALU.mult).then_inc(ln_ready, 1)

            dve.wait_ge(loaded["x"], 16)
            for b in range(B):
                statistics(0, b)
            layernorm(0, x, ln0)

            dve.wait_ge(consts_ready, 1)
            did(dve.tensor_single_scalar(blk_i[:, :], iota_i[:, :], 15, ALU.bitwise_and))
            settle()
            did(dve.tensor_copy(blk[:, :], blk_i[:, :]))
            settle()
            did(ts(first_up[:, :], blk[:, :], 0.5, BIG, ALU.is_gt, ALU.mult))
            did(ts(last_big[:, :], blk[:, :], float(KB - 1), BIG, ALU.is_equal, ALU.mult))
            did(ts(wavepad[:, :], iota_t[:, :], blk[:, 0:1], BIG, ALU.is_lt, ALU.mult))
            did(dve.memset(seed[:, :], 0.0))
            settle()
            q0 = RB - 1 - (SC - 1) % RB
            did(ts(seed[:, 2 * q0:2 * q0 + 1], blk[:, :], float(KB - 1), None, ALU.is_equal))

            for b in range(B):
                for h in range(DH):
                    nm = ("ctxT", b, h)
                    wait_filled(dve, nm)
                    drain(dve.tensor_copy(
                        ctxT[:, h, b, :].rearrange("p (k r) -> p k r", r=RB),
                        bank(nm)[:, :].rearrange("p (k r) -> p k r", r=32)[:, :, 0:RB]), nm)
            dve.wait_ge(bb_ready, 1)
            for b in range(B):
                nm = ("dist", b)
                wait_filled(dve, nm)
                drain(ts(dist[:, b, :, :].rearrange("p k r -> p (k r)"), bank(nm)[0:S, 0:KB * RB],
                         bb[:, b:b + 1], 0.0, ALU.add, ALU.max), nm)

            for m in range(RB // 4):
                nm = ("dwave", m)
                wait_filled(dve, nm)
                drain(tt(dwave[:, :, 4 * m:4 * m + 4].rearrange("p t r -> p r t"),
                         bank(nm)[:, 0:4 * T].rearrange("p (r t) -> p r t", r=4),
                         wavepad[:, :].unsqueeze(1).broadcast_to([128, 4, T]), ALU.add), nm)
            wait_drained(dve, ("dwave", RB // 4 - 1))
            did(ts(dwave[:, :, RB - 1], dwave[:, :, RB - 1], last_big[:, 0:1], None, ALU.add))
            did(dve.memset(R[:, 0, :], BIG))
            did(dve.memset(R[:, 1, 0:1], BIG))
            for b in range(B):
                wait_filled(dve, ("ctxT", b, DH - 1))
            wait_filled(dve, "aaT")
            dve.wait_ge(uu_ready, 1)
            settle()

            above = [p - 1 if p % KB else p + KB - 1 for p in range(32)]

            def choices():
                last = 2 * (RB - 1)
                for t0 in range(0, T, 3):
                    n = min(3, T - t0)
                    cd, cl, cu = R[:, t0:t0 + n, 0:RB], R[:, t0:t0 + n, 1:RB + 1], R[:, t0 + 1:t0 + n + 1, 0:RB]
                    G = hand(LG[:, t0, last + 2:last + 3], [[50, n], [-2, RB]])
                    L = hand(LG[:, t0, last + 1:last + 2], [[50, n], [-2, RB]])
                    U = hand(UU[:, t0, last + 2:last + 3], [[50, n], [-2, RB]])
                    m = rmin[:, 0:n * RB].rearrange("p (t r) -> p t r", r=RB)
                    yield t0 + n, lambda m=m, cu=cu, cl=cl: tt(m, cu, cl, ALU.min)
                    yield t0 + n, lambda U=U, cu=cu, cl=cl: tt(U, cu, cl, ALU.is_le)
                    yield t0 + n, lambda G=G, m=m, cd=cd: tt(G, m, cd, ALU.is_ge)
                    yield t0 + n, lambda U=U, G=G: tt(U, U, G, ALU.is_gt)
                    yield t0 + n, lambda L=L, U=U, G=G: tt(L, U, G, ALU.is_equal)

            todo = list(choices())
            at = [0, None]

            def choose(complete):
                if at[0] < len(todo) and todo[at[0]][0] <= complete:
                    if at[1] is not None:
                        settle(at[1])
                    at[1] = did(todo[at[0]][1]())
                    at[0] += 1

            for t in range(T):
                inner = did(tt(dmin[:, :], R[:, t, 0:RB], R[:, t, 1:RB + 1], ALU.min))
                if t:
                    inner = did(dve.stream_shuffle(R[:, t + 1, 0:1], R[:, t, RB:RB + 1], above))
                choose(t - 1)
                settle(inner)
                scan = did(dve.tensor_tensor_scan(R[:, t + 1, 1:RB + 1], dmin[:, :], dwave[:, t, :],
                                                  first_up[:, 0:1] if t == 0 else R[:, t + 1, 0:1],
                                                  ALU.min, ALU.add))
                choose(t - 1)
                settle(scan)
                if t == 40:
                    wait_filled(dve, "wsum")
                    drain(ts(wmean[:, :], bank("wsum")[:, 0:2], 1.0 / (HID * D), 1e-5, ALU.mult, ALU.max), "wsum")
                    wait_drained(dve, "wsum")
                    dve.reciprocal(winv[:, :], wmean[:, :]).then_inc(winv_ready, 1)
            while at[0] < len(todo):
                choose(T)
            below_lane = [p + 1 if p % KB < KB - 1 else p - KB + 1 for p in range(32)]
            settle()
            did(dve.memset(LG[:, T - 1, 0:1], 0.0))
            did(dve.memset(UU[:, T - 1, 0:1], 0.0))
            did(dve.memset(PR[:, T, :], 0.0))
            did(dve.memset(PR[:, T - 1, 1:2], 0.0))
            did(dve.stream_shuffle(LG[:, 0:T - 1, 0], LG[:, 1:T, 2 * RB], below_lane))
            did(dve.stream_shuffle(UU[:, 0:T - 1, 0], UU[:, 1:T, 2 * RB], below_lane))
            settle()
            for t in range(T - 1, -1, -1):
                if t < T - 1:
                    inner = did(tt(prod[:, :].rearrange("p (q e) -> p q e", e=2),
                                   hand(PR[:, t + 1, 1:2], [[2, RB], [2, 2]]),
                                   LG[:, t + 1, 0:48].rearrange("p (q e) -> p q e", e=2), ALU.mult))
                    inner = did(dve.stream_shuffle(PR[:, t, 1:2], PR[:, t + 1, 49:50], below_lane))
                    settle(inner)
                scan = dve.tensor_tensor_scan(PR[:, t, 2:50], UU[:, t, 0:48], seed[:, :] if t == T - 1 else prod[:, :],
                                              PR[:, t, 1:2], ALU.mult, ALU.add)
                if t:
                    did(scan)
                    settle()
                else:
                    scan.then_inc(path_done, 1)
            dve.memset(pathT[:, :, :, RB:32], 0.0).then_inc(path_zero, 1)
            for m in range(3):
                nm = ("pathT", m)
                wait_filled(dve, nm)
                dst = hand(pathT[:, 0, 0, RB - 1 - 8 * m:RB - 8 * m], [[-1, 8], [32, B * KB]])
                drain(dve.tensor_copy(dst, bankb(nm)[0:T, :].rearrange("p (r l) -> p r l", r=8)), nm)
            dve.wait_ge(tg_ready, 1)
            for b in range(B):
                nm = ("expand", b)
                wait_filled(dve, nm)
                stt(x[:, b, :], bank(nm)[0:S, 0:D], tg[0:S, 0:1], x[:, b, :], ALU.mult, ALU.add).then_inc(x_ready, 1)
                if b:
                    statistics(1, b - 1)
            statistics(1, B - 1)

            layernorm(1, x, ln1)
            dve.wait_ge(ln_ready, 2 * B)
            did(dve.tensor_reduce(am[:, :], ln1[:, :, :], AX.X, ALU.max, apply_absolute_value=True))
            settle()
            did(ts(am[:, :], am[:, :], 1e-5, None, ALU.max))
            settle()
            did(dve.reciprocal(ari[:, :], am[:, :]))
            settle()
            did(ts(asc[:, :], ari[:, :], 127.0, None, ALU.mult))
            ts(sx[:, :], am[:, :], 1.0 / 127.0, None, ALU.mult).then_inc(sx_ready, 1)
            settle()
            for b in range(B):
                ts(ln1[:, b, :], ln1[:, b, :], asc[:, b:b + 1], MAGIC, ALU.mult, ALU.add).then_inc(rounded, 1)
            settle()
            dve.wait_ge(loaded["small"], 96)
            did(ts(cws[:, :, :], cw[:, :, :], wmean[:, 0:1], None, ALU.mult))
            did(dve.memset(hb[:, :, :, 0:1], 0.0))
            did(dve.memset(hb[:, :, :, S + 1:S + 2], 0.0))
            for half in range(2):
                nm = ("sxbc", half)
                wait_filled(dve, nm)
                drain(dve.tensor_copy(sxbc[:, 448 * half:448 * half + 448], bank(nm)[:, 0:448]), nm)
            settle()
            wait_drained(dve, ("sxbc", 1))
            wait_drained(dve, ("sxbc", 0))
            for c in range(HT + 3):
                if c < HT:
                    for half in range(2):
                        nm = ("ffn_up", c, half)
                        wait_filled(dve, nm)
                        if c >= 3:
                            dve.wait_ge(left_done, c - 2)
                            dve.wait_ge(conv_done, c - 2)
                        drain(tt(hb[:, c % 3, 4 * half:4 * half + 4, 1:S + 1],
                                 bank(nm)[:, 0:448].rearrange("p (b s) -> p b s", b=4),
                                 sxbc[:, 448 * half:448 * half + 448].rearrange("p (b s) -> p b s", b=4),
                                 ALU.mult), nm)
                if 2 <= c < HT + 2:
                    e = c - 2
                    acc = ct0[:, e % 3, :].rearrange("p (b s) -> p b s", b=B)
                    dve.wait_ge(left_done, e + 1)
                    stt(acc, hb[:, e % 3, :, 2:S + 2], cws[:, e, 2:3], acc, ALU.mult, ALU.add).then_inc(conv_done, 1)
                if c >= 4 and c % 2 == 0:
                    e = c - 4
                    dve.wait_ge(silu_done, e + 2)
                    pair = hs[:, e:e + 2, :].rearrange("p c t -> p t c")
                    if e == 0:
                        ins = dve.tensor_reduce(hmax[:, :], pair, AX.X, ALU.max, apply_absolute_value=True)
                    else:
                        did(dve.tensor_reduce(hmax2[:, :], pair, AX.X, ALU.max, apply_absolute_value=True))
                        settle()
                        dve.wait_ge(hmax_part, e // 2)
                        ins = tt(hmax[:, :], hmax[:, :], hmax2[:, :], ALU.max)
                    ins.then_inc(hmax_part, 1)
            for half in range(2):
                nm = ("hmaxT", half)
                wait_filled(dve, nm)
                drain(dve.tensor_reduce(am[:, 4 * half:4 * half + 4],
                                        bank(nm)[0:S, :].rearrange("p (b c) -> p b c", b=4), AX.X, ALU.max), nm)
            wait_drained(dve, ("hmaxT", 0))
            wait_drained(dve, ("hmaxT", 1))
            did(ts(am[:, :], am[:, :], 1e-5, None, ALU.max))
            settle()
            did(dve.reciprocal(ari[:, :], am[:, :]))
            settle()
            ts(asc[:, :], ari[:, :], 127.0, None, ALU.mult).then_inc(s2_ready, 1)
            did(ts(sx[:, :], am[:, :], 1.0 / 127.0, wmean[0:S, 1:2], ALU.mult, ALU.mult))
            settle()
            did(ts(sx[:, :], sx[:, :], tg[0:S, 2:3], None, ALU.mult))
            for half in range(2):
                nm = ("s2bc", half)
                wait_filled(dve, nm)
                drain(dve.tensor_copy(s2bc[:, 448 * half:448 * half + 448], bank(nm)[:, 0:448]), nm)
            wait_drained(dve, ("s2bc", 0))
            wait_drained(dve, ("s2bc", 1))
            for c in range(HT):
                if c < HT - PT:
                    did(tt(hs[:, c, :], hs[:, c, :], s2bc[:, :], ALU.mult))
                if c > HT - PT:
                    dve.wait_ge(scaled, c - (HT - PT))
                if c:
                    ts(q2[:, c - 1, :], hs[:, c - 1, :], MAGIC, MAGIC, ALU.add, ALU.subtract).then_inc(q2_ready, 1)
                settle()
            dve.wait_ge(scaled, PT)
            ts(q2[:, HT - 1, :], hs[:, HT - 1, :], MAGIC, MAGIC, ALU.add, ALU.subtract).then_inc(q2_ready, 1)
            for b in range(B):
                nm = ("ffn_down", b)
                wait_filled(dve, nm)
                stt(x[:, b, :], bank(nm)[0:S, 0:D], sx[:, b:b + 1], x[:, b, :], ALU.mult, ALU.add).then_inc(x_ready, 1)
                if b:
                    statistics(2, b - 1)
            statistics(2, B - 1)

            layernorm(2, x, ln2)
            for half in range(2):
                for t in range(2):
                    wait_drained(dve, ("qT", t, half))
                    cols = slice(448 * half, 448 * half + 448)
                    did(tt(qx32[:, t, cols], qx32[:, t, cols], qp[:, t, 0, cols], ALU.subtract))
                    settle()
                    did(dve.tensor_copy(qp[:, t, 1, cols], qx32[:, t, cols]))
                    settle()
                    tt(qp[:, t, 2, cols], qx32[:, t, cols], qp[:, t, 1, cols], ALU.subtract).then_inc(q_split, 1)

            def aggregate(half):
                settle()
                for b in range(HB * half, HB * half + HB):
                    last = dve.bn_aggr(mv[:, b, :], bn6[:, b, :])
                    if b % HB < HB - 1:
                        did(last)
                last.then_inc(var_ready, 1)

            def scale(half):
                dve.wait_ge(sd_ready, 4 + half)
                did(dve.reciprocal(rstd[:, HB * half:HB * half + HB], sd[:, HB * half:HB * half + HB]))
                settle()

            def normalise(b):
                ts(ln3[:, b % HB, :], x[:, b, :], mv[:, b, 0:1], rstd[:, b:b + 1],
                   ALU.subtract, ALU.mult).then_inc(ln_ready, 1)

            a0 = cells(acts[0], NIT)

            def mean_part(i):
                dve.wait_ge(gel_ready, i + 1)
                half = i // NIT
                dve.tensor_reduce(a0[:, HB * half:HB * half + HB, i % NIT],
                                  gel[:, i % 2, :].rearrange("p (b s) -> p b s", b=HB),
                                  AX.X, ALU.add).then_inc(gel_used, 1)

            for f in range(-LAG, 4 * B + 4):
                b, t = f // 4 - 1, f % 4
                u = f + LAG
                for i in range(4):
                    if u < 4 * B:
                        nm = ("smax", u, i)
                        wait_filled(dve, nm)
                        n = 4 * (u % 4) + i
                        drain(dve.tensor_reduce(negm[:, n:n + 1], bank(nm)[0:S, 0:SC], AX.X, ALU.max, negate=True), nm)
                    if i == 1 and b >= 0 and t == 1:
                        nm = ("pvT", b)
                        wait_filled(dve, nm)
                        pvt = bank(nm)[0:S, :].rearrange("p (h e) -> p h e", e=32)
                        did(dve.reciprocal(rs[:, :], pvt[:, :, HD]))
                        settle()
                        drain(tt(o[:, :, :], pvt[:, :, 0:HD], rs[:, :].unsqueeze(2).broadcast_to([S, NH, HD]),
                                 ALU.mult), nm)
                    if i == 1 and b >= 0 and t == 3:
                        nm = ("wo", b)
                        wait_filled(dve, nm)
                        dve.wait_ge(bias_added, b + 1)
                        stt(x[:, b, :], bank(nm)[0:S, 0:D], tg[0:S, 1:2], x[:, b, :],
                            ALU.mult, ALU.add).then_inc(x_ready, 1)
                    if i == 2 and 0 <= f + 1 < 4 * B:
                        nm = ("negT", f + 1)
                        wait_filled(dve, nm)
                        n = 4 * ((f + 1) % 4)
                        drain(dve.tensor_copy(qs[SR:SR + 3, (f + 1) // 4 % 3, n:n + 4, :].rearrange("p n s -> p (n s)"),
                                              bank(nm)[SR:SR + 3, 0:4 * S]), nm)
                if t == 0 and 1 <= b <= B - 1:
                    statistics(3, b - 1)
                    if b == HB:
                        aggregate(0)
                if f == 4 * HB + 6:
                    scale(0)
                if f in (4 * HB + 6, 4 * HB + 7):
                    for i in range(2):
                        normalise(2 * (f - 4 * HB - 6) + i)
                if FREE + 1 <= f < FREE + 5:
                    for i in range(2):
                        m = 2 * (f - FREE - 1) + i
                        nm = ("patT", m)
                        wait_filled(dve, nm)
                        drain(dve.tensor_copy(patT[:, :, 256 * m:256 * m + 256],
                                               bank(nm)[:, :].rearrange("p (h n) -> p h n", h=DH)), nm)
                if f >= 4 * B:
                    for i in range(2):
                        mean_part(2 * (f - 4 * B) + i)
                if u < 4 * B and u % 4 == 3:
                    for i in range(3):
                        wait_drained(dve, ("smax", u, i + 1))
                    part = negp[:, u // 4 % 2, :, :]
                    did(dve.tensor_copy(part[:, :, 0], negm[:, :]))
                    settle()
                    did(tt(negm[:, :], negm[:, :], part[:, :, 0], ALU.subtract))
                    settle()
                    did(dve.tensor_copy(part[:, :, 1], negm[:, :]))
                    settle()
                    tt(part[:, :, 2], negm[:, :], part[:, :, 1], ALU.subtract).then_inc(neg_ready, 1)
                    dve.wait_ge(neg_ready, u // 4 + 1)
            statistics(3, B - 1)
            aggregate(1)
            mean_part(8)
            mean_part(9)
            scale(1)
            for h in range(DH):
                wait_filled(dve, ("lnT3", h, 0))
            for b in range(HB, B):
                normalise(b)
            did(dve.memset(repr32[:, :, :], 0.0))
            did(dve.tensor_reduce(batch_of[:, :], ident[:, :].rearrange("p (g e) -> p e g", g=4)[:, 0:B, :],
                                  AX.X, ALU.add))
            for i in range(10, 2 * NIT):
                mean_part(i)
            dve.wait_ge(gel_used, 2 * NIT)
            ts(acts[0][:, :], acts[0][:, :], 1.0 / S, 0.0, ALU.mult, ALU.add).then_inc(acts_ready, 1)

            def largest(k, lanes, keep):
                nm = ("actT", k)
                wait_filled(dve, nm)
                drain(dve.tensor_copy(aT[0:lanes, :], bank(nm)[0:lanes, 0:128]), nm)
                wait_drained(dve, nm)
                bits = aT[0:lanes, :].bitcast(I32)
                v = {"key": key, "sgn": sgn, "low": eq, "khi": khi, "klo": klo, "kval": kval, "cand": cand,
                     "nextb": nextb, "nsel": nsel, "bound": bound, "most": most, "eq": eq, "gt": gt, "need": need,
                     "incl": incl, "sel": sel}
                v = {n: t[0:lanes, :] for n, t in v.items()}
                for n in ("cand", "nextb"):
                    v[n] = v[n][:, 0:NCAND[k]]
                v["low"] = v["low"].bitcast(I32)
                did(ts(v["sgn"], bits, 31, 0x7FFFFFFF, ALU.arith_shift_right, ALU.bitwise_and))
                settle()
                did(tt(v["key"], v["sgn"], bits, ALU.bitwise_xor))
                settle()
                did(dve.tensor_single_scalar(v["sgn"], v["key"], 16, ALU.arith_shift_right))
                did(dve.tensor_single_scalar(v["low"], v["key"], 0xFFFF, ALU.bitwise_and))
                settle()
                did(dve.tensor_copy(v["khi"], v["sgn"]))
                did(dve.tensor_copy(v["klo"], v["low"]))
                did(dve.memset(v["bound"], -32768.0))
                numbers = 128 * lanes // B
                did(dve.memset(most[0:lanes, 0:VC[k]], numbers - keep + 0.5))
                if VC[k] < NCAND[k]:
                    did(dve.memset(most[0:lanes, VC[k]:NCAND[k]], numbers - 2 * keep + 0.5))
                settle()
                ts(v["cand"], steps[min(k, 1)][0:lanes, 0, :], -32768.0, None, ALU.add).then_inc(cand_ready, 1)
                dve.wait_ge(cand_ready, ROUNDS_BEFORE[k] + 1)
                val = v["khi"]
                for r in range(2 * ROUNDS[k]):
                    q = r % ROUNDS[k]
                    last = q == ROUNDS[k] - 1
                    if r == ROUNDS[k]:
                        did(ts(v["kval"], v["khi"], v["bound"], 65536.0, ALU.subtract, ALU.mult))
                        settle()
                        val = v["kval"]
                        did(tt(val, val, v["klo"], ALU.add))
                        did(dve.memset(v["bound"], 0.0))
                        settle()
                        dve.tensor_copy(v["cand"], steps[min(k, 1)][0:lanes, 0, :]).then_inc(cand_ready, 1)
                        dve.wait_ge(cand_ready, ROUNDS_BEFORE[k] + r + 1)
                    only = last and k > 0
                    mine = 1 if only else VC[k]
                    with nc.allow_low_precision(reason="counts up to 128 are exact"):
                        for m in range(mine):
                            ins = ts(below[0:lanes, m, :], val, cand[0:lanes, m:m + 1], None, ALU.is_lt, ALU.add,
                                     accum_out=cnt[0:lanes, m:m + 1])
                            if m < mine - 1:
                                did(ins)
                    ins.then_inc(cnt_ready, 1)
                    if not last:
                        settle()
                        did(ts(v["nextb"], steps[min(k, 1)][0:lanes, q + 1, :], v["bound"], None, ALU.add))
                    nm = ("count", k, r)
                    wait_filled(dve, nm)
                    tests = 1 if only else NCAND[k]
                    drain(stt(reached[0:lanes, 0:tests], bank(nm)[0:lanes, 0:tests], 1.0, most[0:lanes, 0:tests],
                              ALU.mult, ALU.is_le, accum_out=v["nsel"]), nm)
                    settle()
                    wait_drained(dve, nm)
                    step = float(STEPS[k][q])
                    if not last:
                        stt(v["cand"], v["nsel"].broadcast_to([lanes, NCAND[k]]), step, v["nextb"],
                            ALU.mult, ALU.add).then_inc(cand_ready, 1)
                    did(stt(v["bound"], v["nsel"], step, v["bound"], ALU.mult, ALU.add))
                    if last:
                        settle()
                    else:
                        dve.wait_ge(cand_ready, ROUNDS_BEFORE[k] + r + 2)
                settle()
                with nc.allow_low_precision(reason="counts up to 128 are exact"):
                    did(ts(v["gt"], val, v["bound"], None, ALU.is_gt, ALU.add, accum_out=tie[0:lanes, 0:1]))
                    ts(v["eq"], val, v["bound"], None, ALU.is_equal, ALU.add,
                       accum_out=tie[0:lanes, 1:2]).then_inc(tie_ready, 1)
                dve.wait_ge(tie_ready, k + 1)
                did(dve.tensor_tensor_scan(v["incl"], ones[0:lanes, :], v["eq"], 0.0, ALU.mult, ALU.add))
                nm = ("ties", k)
                wait_filled(dve, nm)
                drain(ts(v["need"], bank(nm)[0:lanes, 0:1], -1.0, keep + 0.5, ALU.mult, ALU.add), nm)
                settle()
                wait_drained(dve, nm)
                did(stt(v["incl"], v["incl"], v["need"], v["eq"], ALU.is_lt, ALU.mult))
                settle()
                if k == 1:
                    tt(v["sel"], v["incl"], v["gt"], ALU.add).then_inc(sel_ready, 1)
                else:
                    did(tt(v["sel"], v["incl"], v["gt"], ALU.add))
                    settle()
                    tt(picked[0:lanes, :], v["sel"], aT[0:lanes, :], ALU.mult).then_inc(sel_ready, 1)

            largest(0, B * NIT, NI // 8)
            nm = ("selT", 0)
            wait_filled(dve, nm)
            drain(dve.tensor_copy(repr32[:, :, 0:B], bank(nm)[:, 0:B * NIT].rearrange("p (b n) -> p n b", b=B)), nm)
            for h in range(2):
                nm = ("processT", h)
                wait_filled(dve, nm)
                ins = dve.tensor_reduce(cells(praw, NPT)[:, :, 4 * h:4 * h + 4].rearrange("p b n -> p n b"),
                                        bank(nm)[:, :].rearrange("p (n g e) -> p n e g", n=4, g=4)[:, :, 0:B, :],
                                        AX.X, ALU.add)
                drain(ins, nm)
            dve.wait_ge(acts_ready, 2)
            dve.tensor_reduce(pmx[:, :], cells(acts[1], NPT), AX.X, ALU.max).then_inc(pmx_ready, 1)
            wait_filled(dve, "pmaxT")
            drain(dve.tensor_reduce(pm8[:, :], bank("pmaxT")[0:B, 0:128], AX.X, ALU.max), "pmaxT")
            wait_drained(dve, "pmaxT")
            ts(pmd[:, :], ident[0:B, 0:B], pm8[:, 0:1], None, ALU.mult).then_inc(pmd_ready, 1)
            wait_filled(dve, "pmaxb")
            drain(tt(cells(esel, NPT), cells(acts[1], NPT),
                     bank("pmaxb")[:, 0:B].unsqueeze(2).broadcast_to([128, B, NPT]), ALU.subtract), "pmaxb")
            largest(1, B * NPT, NP // 8)
            nm = ("selT", 1)
            wait_filled(dve, nm)
            dve.wait_ge(pexp_ready, 1)
            drain(tt(esel[:, :], esel[:, :], bank(nm)[:, 0:B * NPT], ALU.mult), nm)
            wait_filled(dve, "aggr")
            did(dve.reciprocal(agr[:, :], bank("aggr")[:, B:2 * B]))
            settle()
            drain(tt(agg[:, :], bank("aggr")[:, 0:B], agr[:, :], ALU.mult), "aggr")
            largest(2, B * NOT, NO // 8)
            nm = ("selT", 2)
            wait_filled(dve, nm)
            drain(dve.tensor_copy(repr32[:, :, 0:B], bank(nm)[:, 0:B * NOT].rearrange("p (b n) -> p n b", b=B)), nm)
            wait_filled(dve, "final")
            drain(dve.tensor_copy(fin[:, :], bank("final")[:, 0:D]), "final")
            for b in range(B):
                nm = ("spread", b)
                wait_filled(dve, nm)
                stt(x[:, b, :], bank(nm)[0:S, 0:D], tg[0:S, 3:4], x[:, b, :], ALU.mult, ALU.add).then_inc(x_ready, 1)

        @block.scalar
        def _(act):
            did, settle = counter(act, scl)
            fn = act.activation

            def root(n):
                act.wait_ge(var_ready, n + 1)
                fn(sd[:, :], mv[:, :, 1], ACT.Sqrt, bias=eps[0:S, 0:1]).then_inc(sd_ready, 1)

            def load_table(func):
                settle()
                did(fn(warm[:, :], eps[:, :], func))

            act.wait_ge(consts_ready, 1)
            load_table(ACT.Sqrt)
            root(0)
            for b in range(B):
                act.wait_ge(ln_ready, b + 1)
                settle()
                ins = fn(actscr[0:S, 0:D], ln0[:, b, :], ACT.Square, accum_out=bb[:, b:b + 1])
                if b == B - 1:
                    ins.then_inc(bb_ready, 1)
                else:
                    did(ins)
            for half in range(2):
                for h in range(DH):
                    nm = ("lnT0", h, half)
                    wait_filled(act, nm)
                    drain(fn(ln0T[:, h, 448 * half:448 * half + 448], bank(nm)[:, 0:448], ACT.Copy, scale=-2.0), nm)
            for kt in range(CT):
                act.wait_ge(loaded[f"ctx{kt}"], 16 * NCTX[kt])
                for b in range(B):
                    i = B * kt + b
                    settle()
                    if i == 0:
                        act.wait_ge(bb_ready, 1)
                    ins = fn(actscr[:, 0:D], ctxP[:, kt, b, :], ACT.Square, accum_out=aa[:, i:i + 1])
                    if i == CT * B - 1:
                        ins.then_inc(aa_ready, 1)
                    else:
                        did(ins)
            wait_filled(act, "aaT")
            drain(fn(aaT[:, :], bank("aaT")[0:CT * B, 0:128], ACT.Copy), "aaT")
            for m in range(KB // 2):
                nm = ("skew", m)
                wait_filled(act, nm)
                drain(fn(skewed[:, :, 2 * m:2 * m + 2, :].rearrange("p b k r -> p k b r"),
                         bank(nm)[0:T, 0:2 * B * RB].rearrange("p (k b r) -> p k b r", k=2, b=B), ACT.Sqrt), nm)
            for i, dst in enumerate((wqT, wkT, wvT, woT)):
                nm = ("attnWT", i)
                wait_filled(act, nm)
                drain(fn(dst[:, :, :].rearrange("p h d -> p (h d)"), bank(nm)[:, :], ACT.Copy), nm)
            act.wait_ge(loaded["ffnW"], 32)
            did(fn(tern[0][:, :], w1n[:, :], ACT.Abs, accum_out=wabs[:, 0:1]))
            fn(tern[1][:, :], w2n[:, :], ACT.Abs, accum_out=wabs[:, 1:2]).then_inc(wabs_ready, 1)
            act.wait_ge(loaded["small"], 96)
            fn(tg[:, :], gates[:, :], ACT.Tanh).then_inc(tg_ready, 1)
            wait_filled(act, "bo")
            act.wait_ge(tg_ready, 1)
            drain(fn(gbo[:, :], bank("bo")[0:S, 0:D], ACT.Identity, scale=tg[0:S, 1:2]), "bo")
            act.wait_ge(ones_v_ready, 1)
            for b in range(B):
                for c in range(KCH):
                    nm = ("V", b, c)
                    wait_filled(act, nm)
                    drain(fn(v1[:, c, b, 0:NH * (HD + 1)].rearrange("p (h e) -> p h e", e=HD + 1)[:, :, 0:HD],
                             bank(nm)[0:KC, 0:D].rearrange("p (h e) -> p h e", e=HD), ACT.Copy), nm)
            for w in range(2):
                for h in range(2):
                    nm = ("ternT", w, h)
                    wait_filled(act, nm)
                    if w == 0:
                        drain(fn(w1T[:, h, :], bankb(nm), ACT.Copy), nm)
                    else:
                        drain(fn(w2T[:, 4 * h:4 * h + 4, :].rearrange("p c d -> p (c d)"), bankb(nm), ACT.Copy), nm)
            act.wait_ge(loaded["biasT"], 32)
            for u in range(2 * B):
                nm = ("kT", u // B, u % B)
                t = u // B
                wait_filled(act, nm)
                if u >= 2:
                    act.wait_ge(k_split, u - 1)
                    act.wait_ge(parts_stored[u % 2], 16 * (u // 2))
                did(fn(kx[:, u % 2, :], bank(nm)[:, 0:SC], ACT.Identity, bias=bkT[:, t:t + 1]))
                drain(fn(kp[:, u % 2, 0, :], bank(nm)[:, 0:SC], ACT.Identity, bias=bkT[:, t:t + 1]), nm)
            did(fn(bqs[:, :], bqT[:, :], ACT.Copy, scale=HD ** -0.5))
            for b in range(B):
                nm = ("path", b)
                wait_filled(act, nm)
                drain(fn(path[:, b, :, :].rearrange("p c s -> p (c s)"), bank(nm)[:, 0:4 * S], ACT.Copy), nm)
            load_table(ACT.Sqrt)
            root(1)
            for b in range(B):
                act.wait_ge(rounded, b + 1)
                fn(qx[:, b, :], ln1[:, b, :], ACT.Identity, bias=no_magic[0:S, 0:1]).then_inc(qx_ready, 1)
            for h in range(DH):
                nm = ("qxT", h)
                wait_filled(act, nm)
                drain(fn(qxT[:, h, :], bankb(nm)[:, 0:TOK], ACT.Copy), nm)
            for c in range(HT + 2):
                if c < HT:
                    wait_drained(act, ("ffn_up", c, 1))
                    wait_drained(act, ("ffn_up", c, 0))
                    if c >= 3:
                        act.wait_ge(silu_done, c - 2)
                    fn(ct0[:, c % 3, :].rearrange("p (b s) -> p b s", b=B), hb[:, c % 3, :, 1:S + 1], ACT.Identity,
                       bias=cb[:, c:c + 1], scale=cws[:, c, 1:2]).then_inc(ct0_ready, 1)
                if c >= 2:
                    act.wait_ge(conv_done, c - 1)
                    fn(hs[:, c - 2, :], ct0[:, (c - 2) % 3, :], ACT.Silu).then_inc(silu_done, 1)
            load_table(ACT.Sqrt)
            root(2)
            for half in range(2):
                for h in range(DH):
                    nm = ("lnT2", h, half)
                    wait_filled(act, nm)
                    drain(fn(ln2T[:, h, 448 * half:448 * half + 448], bank(nm)[:, 0:448], ACT.Copy), nm)
            for half in range(2):
                for t in range(2):
                    nm = ("qT", t, half)
                    wait_filled(act, nm)
                    cols = slice(448 * half, 448 * half + 448)
                    did(fn(qx32[:, t, cols], bank(nm)[:, 0:448], ACT.Identity, bias=bqs[:, t:t + 1], scale=HD ** -0.5))
                    drain(fn(qp[:, t, 0, cols], bank(nm)[:, 0:448], ACT.Identity, bias=bqs[:, t:t + 1],
                             scale=HD ** -0.5), nm)

            def gelu(i):
                nm = ("pattern", i)
                wait_filled(act, nm)
                if i >= 2:
                    act.wait_ge(gel_used, i - 1)
                fn(gel[:, i % 2, :], bank(nm)[:, 0:448], ACT.Gelu).then_inc(gel_ready, 1)

            def tokens(h, half):
                nm = ("lnT3", h, half)
                wait_filled(act, nm)
                drain(fn(ln3T[half][:, h, :], bank(nm)[:, 0:448], ACT.Copy), nm)

            def half_root(half):
                act.wait_ge(var_ready, 4 + half)
                fn(sd[:, HB * half:HB * half + HB], mv[:, HB * half:HB * half + HB, 1], ACT.Sqrt,
                   bias=eps[0:S, 0:1]).then_inc(sd_ready, 1)

            for f in range(-LAG - 1, 4 * B + 4):
                b, t = f // 4 - 1, f % 4
                u = f + LAG + 1
                if f == -3:
                    load_table(ACT.Exp)
                if f == 4 * HB + 5:
                    half_root(0)
                if f in (FREE - 2, FREE - 1):
                    tokens(f - FREE + 2, 0)
                for c in range(KCH):
                    if c == 1 and b >= 0 and t == 2:
                        nm = ("oT", b)
                        wait_filled(act, nm)
                        drain(fn(oT[:, :, :].rearrange("p h s -> p (h s)"), bank(nm)[:, 0:DH * S], ACT.Copy), nm)
                    if c == 2 and u < 4 * B:
                        nm = ("qstack", u)
                        wait_filled(act, nm)
                        n = 4 * (u % 4)
                        drain(fn(qs[0:SR, u // 4 % 3, n:n + 4, :].rearrange("p n s -> p (n s)"),
                                 bank(nm)[0:SR, 0:4 * S], ACT.Copy), nm)
                    if 0 <= f < 4 * B:
                        if c == 0 and f >= 2:
                            wait_values(act, f - 2)
                        nm = ("scoreT", f, c)
                        wait_filled(act, nm)
                        drain(fn(E[:, (KCH * f + c) % 6, :], bank(nm)[0:KC, 0:4 * S], ACT.Exp), nm)
                if b >= 0 and t == 0:
                    nm = ("pv", b)
                    wait_filled(act, nm)
                    drain(fn(pvs[:, :], bank(nm)[:, 0:4 * S], ACT.Copy), nm)
                if f >= 4 * B:
                    gelu(2 * (f - 4 * B))
                    gelu(2 * (f - 4 * B) + 1)
            half_root(1)
            for i in range(8, 2 * NIT):
                if i == 14:
                    tokens(0, 1)
                    tokens(1, 1)
                gelu(i)
            for m in range(NOT // 4):
                nm = ("oiwT", m)
                wait_filled(act, nm)
                drain(fn(oiwT[:, 512 * m:512 * m + 512], bank(nm)[:, :], ACT.Copy), nm)

            def signs(k, r):
                if r % ROUNDS[k] == ROUNDS[k] - 1:
                    return
                n = B * (NIT, NPT, NOT)[k]
                act.wait_ge(cand_ready, ROUNDS_BEFORE[k] + r + 1)
                val = khi if r < ROUNDS[k] else kval
                with nc.allow_low_precision(reason="sums of signs up to 128 are exact"):
                    for m in range(VC[k], NCAND[k]):
                        ins = fn(below[0:n, m, :], val[0:n, :], ACT.Sign, bias=cand[0:n, m:m + 1], scale=-1.0,
                                 accum_out=cnt[0:n, m:m + 1])
                        if m < NCAND[k] - 1:
                            did(ins)
                ins.then_inc(signs_ready, 1)

            for i in range(NPT):
                for m in range(NIT // 4):
                    nm = ("piwT", i, m)
                    wait_filled(act, nm)
                    drain(fn(piwT[:, 4 * m:4 * m + 4, 128 * i:128 * i + 128],
                             bank(nm)[:, :].rearrange("p (c n) -> p c n", c=4), ACT.Copy), nm)
            load_table(ACT.Gelu)
            for h in range(2):
                nm = ("process", h)
                wait_filled(act, nm)
                drain(fn(pact[:, 512 * h:512 * h + 512], bank(nm)[:, :], ACT.Copy), nm)
            for h in range(2):
                wait_drained(act, ("processT", h))
            fn(acts[1][:, :], praw[:, :], ACT.Gelu).then_inc(acts_ready, 1)
            load_table(ACT.Exp)
            wait_drained(act, "pmaxb")
            fn(esel[:, :], esel[:, :], ACT.Exp).then_inc(pexp_ready, 1)
            for r in range(2 * ROUNDS[1]):
                signs(1, r)
            load_table(ACT.Gelu)
            wait_filled(act, "output")
            fn(cells(acts[2], NOT), bank("output")[:, 0:B * NOT].rearrange("p (n b) -> p b n", b=B),
               ACT.Gelu).then_inc(acts_ready, 1)
            load_table(ACT.Sign)
            for r in range(2 * ROUNDS[2]):
                signs(2, r)

        @block.tensor
        def _(pe):
            mm, tr = pe.matmul, pe.transpose

            def ln_transposes(n, name, src, dt_ident):
                for half in range(2):
                    for h in range(DH):
                        nm = (name, h, half)
                        claim(pe, nm)
                        for i in range(4):
                            b = 4 * half + i
                            pe.wait_ge(ln_ready, n * B + b + 1)
                            ins = tr(bank(nm)[:, S * i:S * i + S], src[:, b, 128 * h:128 * h + 128],
                                     ident[0:S, 0:S])
                        fill(ins, nm)

            pe.wait_ge(consts_ready, 1)
            ln_transposes(0, "lnT0", ln0, ident)
            for kt in range(CT):
                pe.wait_ge(loaded[f"ctx{kt}"], 16 * NCTX[kt])
            for b in range(B):
                for h in range(DH):
                    nm = ("ctxT", b, h)
                    claim(pe, nm)
                    for kt in range(CT):
                        ins = tr(bank(nm)[:, 128 * kt:128 * kt + 128], ctxP[:, kt, b, 128 * h:128 * h + 128],
                                 ident[:, :])
                    fill(ins, nm)
            for h in range(DH):
                for half in range(2):
                    wait_drained(pe, ("lnT0", h, half))

            def products(b):
                nm = ("dist", b)
                claim(pe, nm)
                for h in range(DH):
                    wait_drained(pe, ("ctxT", b, h))
                    mm(bank(nm)[0:S, 0:KB * RB], ln0T[:, h, S * b:S * b + S], ctxT[:, h, b, :],
                       start=(h == 0), stop=False)

            for b in range(B - 1):
                products(b)
            claim(pe, "aaT")
            pe.wait_ge(aa_ready, 1)
            fill(tr(bank("aaT")[0:CT * B, 0:128], aa[:, :], ident[:, :]), "aaT")
            wait_drained(pe, "aaT")
            products(B - 1)
            for b in range(B):
                nm = ("dist", b)
                for kt in range(CT):
                    i = B * kt + b
                    ins = mm(bank(nm)[0:S, 96 * kt:96 * kt + 96], ident[0:CT * B, i:i + 1].broadcast_to([CT * B, S]),
                             aaT[:, :].rearrange("p (g r) -> p g r", g=4)[:, :, 0:RB], start=False,
                             stop=(kt == CT - 1))
                fill(ins, nm)
            for b in range(B):
                wait_drained(pe, ("dist", b))
            for m in range(KB // 2):
                nm = ("skew", m)
                claim(pe, nm)
                for e in range(2):
                    k = 2 * m + e
                    ins = mm(bank(nm)[0:T, B * RB * e:B * RB * (e + 1)], skewI[0:S, KB - 1 - k:KB - 1 - k + T],
                             dist[:, :, k, :], start=True, stop=True)
                fill(ins, nm)
            for m in range(KB // 2):
                wait_drained(pe, ("skew", m))
            for m in range(RB // 4):
                nm = ("dwave", m)
                claim(pe, nm)
                for i in range(4):
                    ins = tr(bank(nm)[:, T * i:T * i + T],
                             skewed[:, :, :, 4 * m + i].rearrange("p b k -> p (b k)"), ident[0:T, 0:T])
                fill(ins, nm)
            pe.wait_ge(loaded["attnW"], 64)
            for i in range(4):
                nm = ("attnWT", i)
                claim(pe, nm)
                for h in range(DH):
                    for c in range(2):
                        ins = tr(bank(nm)[:, D * h + 128 * c:D * h + 128 * c + 128],
                                 wnat[:, i, c, 128 * h:128 * h + 128], ident[:, :])
                fill(ins, nm)
            claim(pe, "wsum")
            pe.wait_ge(wabs_ready, 1)
            fill(mm(bank("wsum")[:, 0:2], ones[:, :], wabs[:, :], start=True, stop=True), "wsum")
            pe.wait_ge(loaded["small"], 96)
            claim(pe, "bo")
            fill(mm(bank("bo")[0:S, 0:D], ones[0:1, 0:S], bor[0:1, :], start=True, stop=True), "bo")
            wait_drained(pe, ("attnWT", 2))
            for b in range(B):
                for c in range(KCH):
                    nm = ("V", b, c)
                    claim(pe, nm)
                    for h in range(DH):
                        mm(bank(nm)[0:KC, 0:D], ctxT[:, h, b, KC * c:KC * c + KC], wvT[:, h, :],
                           start=(h == 0), stop=False)
                    fill(mm(bank(nm)[0:KC, 0:D], ones[0:1, 0:KC], bvr[0:1, :], start=False, stop=True), nm)
            for w in range(2):
                pe.wait_ge(tern_ready, w + 1)
                for h in range(2):
                    nm = ("ternT", w, h)
                    claim(pe, nm)
                    for i in range(8):
                        if w == 0:
                            src = tern[0][:, D * i + 128 * h:D * i + 128 * h + 128]
                        else:
                            src = tern[1][:, HID * (i % 2) + 128 * (4 * h + i // 2):][:, 0:128]
                        ins = tr(bankb(nm)[:, 128 * i:128 * i + 128], src, identb[:, :])
                    fill(ins, nm)
            for t in range(2):
                for b in range(B):
                    nm = ("kT", t, b)
                    claim(pe, nm)
                    for h in range(DH):
                        ins = mm(bank(nm)[:, 0:SC], wkT[:, h, 128 * t:128 * t + 128], ctxT[:, h, b, 0:SC],
                                 start=(h == 0), stop=(h == DH - 1))
                    fill(ins, nm)
            pe.wait_ge(path_done, 1)
            for m in range(3):
                nm = ("pathT", m)
                claim(pe, nm)
                for i in range(8):
                    ins = tr(bankb(nm)[0:T, 128 * i:128 * i + 128], PR[:, 0:T, 2 * (8 * m + i) + 3], identb[:, :])
                fill(ins, nm)
            for m in range(3):
                wait_drained(pe, ("pathT", m))
            pe.wait_ge(path_zero, 1)
            for b in range(B):
                nm = ("path", b)
                claim(pe, nm)
                for kt in range(CT):
                    for g in range(4):
                        k = 4 * kt + g
                        ins = mm(bank(nm)[32 * g:32 * g + 32, S * kt:S * kt + S], pathT[:, b, k, :],
                                 skewB[0:T, KB - 1 + k:KB - 1 + k + S], start=True, stop=True)
                fill(ins, nm)
            pe.wait_ge(loaded["again"], 16 * sum(NCTX))
            for b in range(B):
                nm = ("expand", b)
                claim(pe, nm)
                wait_drained(pe, ("path", b))
                for kt in range(CT):
                    ins = mm(bank(nm)[0:S, 0:D], path[:, b, kt, :], ctx_again[:, kt, b, :], start=(kt == 0),
                             stop=(kt == CT - 1))
                fill(ins, nm)
            pe.wait_ge(qx_ready, B)
            for h in range(DH):
                nm = ("qxT", h)
                claim(pe, nm)
                for b in range(B):
                    ins = tr(bankb(nm)[:, S * b:S * b + S], qx[:, b, 128 * h:128 * h + 128], identb[0:S, 0:S])
                fill(ins, nm)
            pe.wait_ge(sx_ready, 1)

            def token_rows(name, cols):
                for half in range(2):
                    nm = (name, half)
                    claim(pe, nm)
                    for i in range(4):
                        b = 4 * half + i
                        ins = mm(bank(nm)[:, S * i:S * i + S], cols[:, b:b + 1].broadcast_to([S, 128]),
                                 ident[0:S, 0:S], start=True, stop=True)
                    fill(ins, nm)

            token_rows("sxbc", sx)
            for h in range(DH):
                wait_drained(pe, ("qxT", h))
            for c in range(HT):
                for half in range(2):
                    nm = ("ffn_up", c, half)
                    claim(pe, nm)
                    for h in range(DH):
                        ins = mm(bank(nm)[:, 0:448], w1T[:, h, 128 * c:128 * c + 128],
                                 qxT[:, h, 448 * half:448 * half + 448], start=(h == 0), stop=(h == DH - 1))
                    fill(ins, nm)
            pe.wait_ge(hmax_part, HT // 2)
            for half in range(2):
                nm = ("hmaxT", half)
                claim(pe, nm)
                for i in range(4):
                    b = 4 * half + i
                    ins = tr(bank(nm)[0:S, 128 * i:128 * i + 128], hmax[:, S * b:S * b + S], ident[:, :])
                fill(ins, nm)
            pe.wait_ge(s2_ready, 1)
            token_rows("s2bc", asc)
            for c in range(HT):
                pe.wait_ge(q2_ready, c + 1)
                for b in range(B):
                    nm = ("ffn_down", b)
                    if c == 0:
                        claim(pe, nm)
                    ins = mm(bank(nm)[0:S, 0:D], q2[:, c, S * b:S * b + S], w2T[:, c, :], start=(c == 0),
                             stop=(c == HT - 1))
                    if c == HT - 1:
                        fill(ins, nm)
            ln_transposes(2, "lnT2", ln2, ident)
            for half in range(2):
                for h in range(DH):
                    wait_drained(pe, ("lnT2", h, half))
                for t in range(2):
                    nm = ("qT", t, half)
                    claim(pe, nm)
                    for h in range(DH):
                        ins = mm(bank(nm)[:, 0:448], wqT[:, h, 128 * t:128 * t + 128],
                                 ln2T[:, h, 448 * half:448 * half + 448], start=(h == 0), stop=(h == DH - 1))
                    fill(ins, nm)

            def queries(u):
                nm = ("qstack", u)
                claim(pe, nm)
                tile = u % 4 // 2
                pe.wait_ge(q_split, 2 * (u // (2 * B)) + tile + 1)
                for i in range(4):
                    for part in range(3):
                        ins = mm(bank(nm)[0:SR, S * i:S * i + S], pick[:, part, 4 * (u % 2) + i, :],
                                 qp[:, tile, part, S * (u // 4):S * (u // 4) + S],
                                 start=(part == 0), stop=(part == 2))
                fill(ins, nm)

            def scores_for_maximum(u, i):
                if i == 0:
                    wait_drained(pe, ("qstack", u))
                    if u % 4 == 0:
                        pe.wait_ge(stack_loaded[u // 4 % 3], 16 * len(K_PARTS) * (u // 12 + 1))
                nm = ("smax", u, i)
                claim(pe, nm)
                n = 4 * (u % 4) + i
                fill(mm(bank(nm)[0:S, 0:SC], qs[0:SR, u // 4 % 3, n, :], ks[0:SR, u // 4 % 3, n, :],
                        start=True, stop=True), nm)

            def scores_less_maximum(f, c):
                if c == 0:
                    wait_drained(pe, ("negT", f))
                nm = ("scoreT", f, c)
                claim(pe, nm)
                for i in range(4):
                    n = 4 * (f % 4) + i
                    ins = mm(bank(nm)[0:KC, S * i:S * i + S],
                             ks[0:SR + 3, f // 4 % 3, n, KC * c:KC * c + KC], qs[0:SR + 3, f // 4 % 3, n, :],
                             start=True, stop=True)
                fill(ins, nm)

            def value_products(f, c):
                b, t = f // 4, f % 4
                if t == 0 and c == 0:
                    claim(pe, ("pv", b))
                wait_drained(pe, ("scoreT", f, c))
                for g in range(4):
                    n = 4 * t + g
                    ins = mm(bank(("pv", b))[32 * g:32 * g + 32, S * t:S * t + S],
                             v1[:, c, b, (HD + 1) * n:(HD + 1) * n + 32],
                             E[:, (KCH * f + c) % 6, S * g:S * g + S],
                             start=(c == 0), stop=(c == KCH - 1))
                if c < KCH - 1:
                    return
                if t == 3:
                    fill(ins, ("pv", b))
                else:
                    ins.then_inc(pv_part, 1)

            def maxima(f):
                nm = ("negT", f)
                claim(pe, nm)
                pe.wait_ge(neg_ready, f // 4 + 1)
                for i in range(4):
                    ins = mm(bank(nm)[SR:SR + 3, S * i:S * i + S], negp[:, f // 4 % 2, 4 * (f % 4) + i, :],
                             identb[0:S, 0:S], start=True, stop=True)
                fill(ins, nm)

            def token_transposes(h, half):
                nm = ("lnT3", h, half)
                claim(pe, nm)
                for i in range(HB):
                    pe.wait_ge(ln_ready, 3 * B + HB * half + i + 1)
                    ins = tr(bank(nm)[:, S * i:S * i + S], ln3[:, i, 128 * h:128 * h + 128], ident[0:S, 0:S])
                fill(ins, nm)

            def pattern_transposes(m):
                nm = ("patT", m)
                claim(pe, nm)
                for h in range(DH):
                    for i in range(2):
                        ins = tr(bank(nm)[:, 256 * h + 128 * i:256 * h + 128 * i + 128],
                                 patn[:, 2 * m + i, 128 * h:128 * h + 128], ident[:, :])
                fill(ins, nm)

            def pattern_product(i):
                nm = ("pattern", i)
                claim(pe, nm)
                wait_drained(pe, ("patT", i % NIT // 2))
                for h in range(DH):
                    wait_drained(pe, ("lnT3", h, i // NIT))
                    ins = mm(bank(nm)[:, 0:448], patT[:, h, 128 * (i % NIT):128 * (i % NIT) + 128],
                             ln3T[i // NIT][:, h, :], start=(h == 0), stop=(h == DH - 1))
                fill(ins, nm)

            pe.wait_ge(k_ones, 1)
            queries(0)
            for f in range(-LAG, 4 * B + 4):
                b, t = f // 4 - 1, f % 4
                ahead, now, behind = f + LAG < 4 * B, 0 <= f < 4 * B, 1 <= f <= 4 * B
                if ahead:
                    scores_for_maximum(f + LAG, 0)
                if now:
                    scores_less_maximum(f, 0)
                if ahead:
                    scores_for_maximum(f + LAG, 1)
                if b >= 0 and t == 1:
                    nm = ("pvT", b)
                    claim(pe, nm)
                    wait_drained(pe, ("pv", b))
                    for i in range(4):
                        ins = tr(bank(nm)[0:S, 128 * i:128 * i + 128], pvs[:, S * i:S * i + S], ident[:, :])
                    fill(ins, nm)
                if b >= 0 and t == 2:
                    nm = ("oT", b)
                    claim(pe, nm)
                    of = o[:, :, :].rearrange("p h e -> p (h e)")
                    for h in range(DH):
                        ins = tr(bank(nm)[:, S * h:S * h + S], of[:, 128 * h:128 * h + 128], ident[0:S, 0:S])
                    fill(ins, nm)
                if b >= 0 and t == 3:
                    nm = ("wo", b)
                    claim(pe, nm)
                    for h in range(DH):
                        ins = mm(bank(nm)[0:S, 0:D], oT[:, h, :], woT[:, h, :], start=(h == 0), stop=(h == DH - 1))
                    fill(ins, nm)
                if behind:
                    value_products(f - 1, 0)
                if now:
                    scores_less_maximum(f, 1)
                if ahead:
                    scores_for_maximum(f + LAG, 2)
                if f + LAG + 1 < 4 * B:
                    queries(f + LAG + 1)
                if 0 <= f + 1 < 4 * B:
                    maxima(f + 1)
                if behind:
                    value_products(f - 1, 1)
                if ahead:
                    scores_for_maximum(f + LAG, 3)
                if now:
                    scores_less_maximum(f, 2)
                if behind:
                    value_products(f - 1, 2)
                if f in (FREE - 3, FREE - 2):
                    token_transposes(f - FREE + 3, 0)
                if f == FREE + 1:
                    pe.wait_ge(loaded["pat"], 16)
                if FREE + 1 <= f < FREE + 5:
                    pattern_transposes(2 * (f - FREE - 1))
                    pattern_transposes(2 * (f - FREE - 1) + 1)
                if f >= 4 * B:
                    pattern_product(2 * (f - 4 * B))
                    pattern_product(2 * (f - 4 * B) + 1)
            for i in range(8, 2 * NIT):
                if i == 14:
                    for h in range(DH):
                        token_transposes(h, 1)
                pattern_product(i)
            pe.wait_ge(loaded["oiw"], 16)
            for m in range(NOT // 4):
                nm = ("oiwT", m)
                claim(pe, nm)
                for i in range(4):
                    ins = tr(bank(nm)[:, 128 * i:128 * i + 128], oiwn[:, 4 * m + i, :], ident[:, :])
                fill(ins, nm)

            def lanes_of(k):
                return B * (NIT, NPT, NOT)[k]

            def act_transpose(k):
                nm = ("actT", k)
                claim(pe, nm)
                pe.wait_ge(acts_ready, k + 1)
                fill(tr(bank(nm)[0:lanes_of(k), 0:128], acts[k][:, :], ident[:, :]), nm)

            def count(k, r):
                nm = ("count", k, r)
                n = lanes_of(k)
                claim(pe, nm)
                pe.wait_ge(cnt_ready, ROUNDS_BEFORE[k] + r + 1)
                m = NCAND[k]
                if k:
                    if r % ROUNDS[k] == ROUNDS[k] - 1:
                        m = 1
                    else:
                        pe.wait_ge(signs_ready, 2 * (ROUNDS[k] - 1) * (k - 1) + r - r // ROUNDS[k] + 1)
                fill(mm(bank(nm)[0:n, 0:m], same[k % 2][:, :], cnt[0:n, 0:m], start=True, stop=True), nm)

            def ties(k):
                nm = ("ties", k)
                n = lanes_of(k)
                claim(pe, nm)
                pe.wait_ge(tie_ready, k + 1)
                mm(bank(nm)[0:n, 0:1], same[k % 2][:, :], tie[0:n, 0:1], start=True, stop=False)
                fill(mm(bank(nm)[0:n, 0:1], under[k % 2][:, :], tie[0:n, 1:2], start=False, stop=True), nm)

            def sel_transpose(k):
                nm = ("selT", k)
                n = lanes_of(k)
                claim(pe, nm)
                pe.wait_ge(sel_ready, k + 1)
                src = sel if k == 1 else picked
                fill(tr(bank(nm)[:, 0:n], src[0:n, :], ident[0:n, 0:n]), nm)

            act_transpose(0)
            for i in range(NPT):
                pe.wait_ge(loaded[f"piw{i % 2}"], 16 * (i // 2 + 1))
                for m in range(NIT // 4):
                    nm = ("piwT", i, m)
                    claim(pe, nm)
                    for e in range(4):
                        c = 4 * m + e
                        ins = tr(bank(nm)[:, 128 * e:128 * e + 128], piw[:, i % 2, 128 * c:128 * c + 128],
                                 ident[:, :])
                    fill(ins, nm)
                for r in (2 * i, 2 * i + 1):
                    count(0, r)
            ties(0)
            sel_transpose(0)
            wait_drained(pe, ("selT", 0))
            for i in range(NPT):
                for m in range(NIT // 4):
                    wait_drained(pe, ("piwT", i, m))
            for h in range(2):
                nm = ("process", h)
                claim(pe, nm)
                for c in range(NIT):
                    g = c % 4
                    ins = mm(bank(nm)[32 * g:32 * g + 32, :], repr32[:, c, :], piwT[:, c, 512 * h:512 * h + 512],
                             start=(c < 4), stop=(c >= NIT - 4))
                fill(ins, nm)
            for h in range(2):
                nm = ("processT", h)
                claim(pe, nm)
                wait_drained(pe, ("process", h))
                for i in range(4):
                    ins = tr(bank(nm)[:, 128 * i:128 * i + 128], pact[:, 512 * h + 128 * i:512 * h + 128 * i + 128],
                             ident[:, :])
                fill(ins, nm)
            claim(pe, "pmaxT")
            pe.wait_ge(pmx_ready, 1)
            fill(tr(bank("pmaxT")[0:B, 0:128], pmx[:, :], ident[:, :]), "pmaxT")
            claim(pe, "pmaxb")
            pe.wait_ge(pmd_ready, 1)
            fill(mm(bank("pmaxb")[:, 0:B], ones[0:B, :], pmd[:, :], start=True, stop=True), "pmaxb")
            act_transpose(1)
            for r in range(2 * ROUNDS[1]):
                count(1, r)
            ties(1)
            sel_transpose(1)
            claim(pe, "aggr")
            wait_drained(pe, ("selT", 1))
            pe.wait_ge(loaded["pval"], 16)
            for i in range(NPT):
                mm(bank("aggr")[:, 0:B], pval[:, i, :], cells(esel, NPT)[:, :, i], start=(i == 0),
                   stop=(i == NPT - 1))
            for i in range(NPT):
                ins = mm(bank("aggr")[:, B:2 * B], ones[:, :], cells(esel, NPT)[:, :, i], start=(i == 0),
                         stop=(i == NPT - 1))
            fill(ins, "aggr")
            claim(pe, "output")
            wait_drained(pe, "aggr")
            for m in range(NOT // 4):
                wait_drained(pe, ("oiwT", m))
            for i in range(NOT):
                ins = mm(bank("output")[:, B * i:B * i + B], oiwT[:, 128 * i:128 * i + 128], agg[:, :], start=True,
                         stop=True)
            fill(ins, "output")
            act_transpose(2)
            for r in range(2 * ROUNDS[2]):
                count(2, r)
            ties(2)
            sel_transpose(2)
            wait_drained(pe, ("selT", 2))
            claim(pe, "final")
            pe.wait_ge(loaded["opat"], 16)
            for i in range(NOT):
                g = i % 4
                ins = mm(bank("final")[32 * g:32 * g + 32, 0:D], repr32[:, i, :], opat[:, i, :], start=(i < 4),
                         stop=(i >= NOT - 4))
            fill(ins, "final")
            wait_drained(pe, "final")
            for b in range(B):
                nm = ("spread", b)
                claim(pe, nm)
                fill(mm(bank(nm)[0:S, 0:D], batch_of[:, b:b + 1].broadcast_to([128, S]), fin[:, :], start=True,
                        stop=True), nm)


INPUTS = ["x", "ctx_1024", "g_xattn", "g_ffn", "L0_ffn_w1", "L0_ffn_conv_w", "L0_ffn_conv_b", "L0_ffn_w2",
          "L1_xattn_Wq", "L1_xattn_bq", "L1_xattn_Wk", "L1_xattn_bk", "L1_xattn_Wv", "L1_xattn_bv",
          "L1_xattn_Wo", "L1_xattn_bo", "L1_ffn_input_patterns", "L1_ffn_process_input_weights",
          "L1_ffn_process_values", "L1_ffn_output_input_weights", "L1_ffn_output_patterns"]


def kernel(**inputs):
    import concourse.bacc as bacc
    from concourse.bass_utils import run_bass_kernel_spmd

    nc = bacc.Bacc("TRN2", target_bir_lowering=False, num_devices=1)
    arrays, args = {}, []
    for name in INPUTS:
        a = np.ascontiguousarray(inputs[name])
        arrays[f"in_{name}"] = a
        args.append(nc.dram_tensor(f"in_{name}", a.shape, mybir.dt.from_np(a.dtype), kind="ExternalInput").ap())
    args.append(nc.dram_tensor("out", (B, S, D), F32, kind="ExternalOutput").ap())
    args.append(nc.dram_tensor("key_parts", (B, 3, D, SC), BF16, kind="Internal").ap())
    build_program(nc, *args)
    return run_bass_kernel_spmd(nc, [arrays], core_ids=[0]).results[0]["out"]
```
